# Optimizing a Trainium2 kernel written in Bass

```python
import numpy as np
import jax
import jax.numpy as jnp

def _softmax(x, axis=-1):
    return jax.nn.softmax(x, axis=axis)

def _gelu(x):
    return jax.nn.gelu(x, approximate=True)

def _silu(x):
    return jax.nn.silu(x)

def _sigmoid(x):
    return jax.nn.sigmoid(x)

def _layernorm(x, axis=-1, eps=1e-05):
    m = jnp.mean(x, axis=axis, keepdims=True)
    v = jnp.var(x, axis=axis, keepdims=True)
    return (x - m) / jnp.sqrt(v + eps)

def _scatter_add(tgt, idx, src, axis=0):
    return tgt.at[idx].add(src)

def _segment_sum(src, seg, n):
    return jax.ops.segment_sum(src, seg, n)
kernel_name = 'mk_audio_tower_d1_tok_audfeat256_r4_90bc21'

def setup_inputs(seed: int=0):
    np.random.seed(seed)
    _w = jnp.asarray

    def _rec_inputs():
        import jax
        import jax.numpy as jnp
        _rk = jax.random.key(seed)
        x = -0.000292821 + 1.00034 * jax.random.normal(jax.random.fold_in(_rk, 1), (16, 256, 64), jnp.float32)
        return x
    x = _rec_inputs()

    def _L0_tok_setup():
        import jax, jax.numpy as jnp
        import numpy as np
        NHEAD = 8
        KSIZE = 32
        EPS = 1e-05
        DIV_BASE = 10.0

        def _pos_encoding(S, D):
            pos = np.arange(S)[:, None].astype(np.float64)
            div = np.exp(np.arange(0, D, 2) * (-np.log(10000.0) / D))
            pe = np.zeros((S, D), np.float32)
            pe[:, 0::2] = np.sin(pos * div)
            pe[:, 1::2] = np.cos(pos * div)
            return jnp.asarray(pe)

        def _layer_norm(x, g, b):
            m = x.mean(-1, keepdims=True)
            v = ((x - m) ** 2).mean(-1, keepdims=True)
            return (x - m) / jnp.sqrt(v + EPS) * g + b

        def _mha(x, in_w, in_b, out_w, out_b):
            B, S, D = x.shape
            dh = D // NHEAD
            qkv = x @ in_w.T + in_b
            q, k, v = jnp.split(qkv, 3, axis=-1)
            sp = lambda t: t.reshape(B, S, NHEAD, dh).transpose(0, 2, 1, 3)
            q, k, v = (sp(q), sp(k), sp(v))
            att = jax.nn.softmax(jnp.einsum('bhqd,bhkd->bhqk', q, k) / jnp.sqrt(jnp.float32(dh)), axis=-1)
            o = jnp.einsum('bhqk,bhkd->bhqd', att, v).transpose(0, 2, 1, 3).reshape(B, S, D)
            return o @ out_w.T + out_b

        def _forward(x, l_in_w, l_in_b, l_out_w, l_out_b, ln1_g, ln1_b, ff_w1, ff_b1, ff_w2, ff_b2, ln2_g, ln2_b, m_in_w, m_in_b, m_out_w, m_out_b):
            B, L, D = x.shape
            amp = jnp.abs(jnp.fft.rfft(x, axis=1))
            feat = jax.lax.stop_gradient(jnp.concatenate([x[:, -1:, :], amp], axis=1))
            src = feat + _pos_encoding(feat.shape[1], D)[None]
            a = _mha(src, l_in_w, l_in_b, l_out_w, l_out_b)
            src = _layer_norm(src + a, ln1_g, ln1_b)
            ff = jax.nn.relu(src @ ff_w1.T + ff_b1) @ ff_w2.T + ff_b2
            src = _layer_norm(src + ff, ln2_g, ln2_b)
            out = _mha(src, m_in_w, m_in_b, m_out_w, m_out_b)
            tau = jnp.clip(jax.nn.softplus(out[:, -1:, :]) / DIV_BASE, 0.01, 1.0)
            Lout = L - KSIZE + 1
            idx = jnp.arange(Lout)[:, None] + jnp.arange(KSIZE)[None, :]
            xw = x[:, idx, :]
            seq = jnp.arange(KSIZE - 1, -1, -1, dtype=x.dtype)
            powers = tau[:, 0, :, None] ** seq
            w = powers / powers.sum(-1, keepdims=True)
            return jnp.einsum('bdk,blkd->bld', w, xw)
        key = jax.random.key(seed)
        ks = jax.random.split(key, 12)
        B, L, D = (128, 128, 64)
        Dff = 4 * D
        s = 0.02
        inp = {'x': jax.random.normal(ks[0], (B, L, D), jnp.float32), 'l_in_w': jax.random.normal(ks[1], (3 * D, D), jnp.float32) * s, 'l_in_b': jnp.zeros((3 * D,), jnp.float32), 'l_out_w': jax.random.normal(ks[2], (D, D), jnp.float32) * s, 'l_out_b': jnp.zeros((D,), jnp.float32), 'ln1_g': jnp.ones((D,), jnp.float32), 'ln1_b': jnp.zeros((D,), jnp.float32), 'ff_w1': jax.random.normal(ks[3], (Dff, D), jnp.float32) * s, 'ff_b1': jnp.zeros((Dff,), jnp.float32), 'ff_w2': jax.random.normal(ks[4], (D, Dff), jnp.float32) * s, 'ff_b2': jnp.zeros((D,), jnp.float32), 'ln2_g': jnp.ones((D,), jnp.float32), 'ln2_b': jnp.zeros((D,), jnp.float32), 'm_in_w': jax.random.normal(ks[5], (3 * D, D), jnp.float32) * s, 'm_in_b': jnp.zeros((3 * D,), jnp.float32), 'm_out_w': jax.random.normal(ks[6], (D, D), jnp.float32) * s, 'm_out_b': jnp.zeros((D,), jnp.float32)}
        return inp
    _L0_tok_all = _L0_tok_setup()
    _L0_tok_in = {k: v for k, v in _L0_tok_all.items() if k in ('l_in_w', 'l_in_b', 'l_out_w', 'l_out_b', 'ln1_g', 'ln1_b', 'ff_w1', 'ff_b1', 'ff_w2', 'ff_b2', 'ln2_g', 'ln2_b', 'm_in_w', 'm_in_b', 'm_out_w', 'm_out_b')}
    del _L0_tok_all

    def _L0_attn_setup():
        import jax, jax.numpy as jnp
        import numpy as np
        HEADS = 4
        DIM_HEAD = 32
        key = jax.random.key(seed)
        k1, k2, k3 = jax.random.split(key, 3)
        B, L, D = (16, 2048, 64)
        hidden = HEADS * DIM_HEAD
        x = jax.random.normal(k1, (B, L, D), dtype=jnp.float32)
        W_qkv = jax.random.normal(k2, (D, 3 * hidden), dtype=jnp.float32) * D ** (-0.5)
        W_out = jax.random.normal(k3, (hidden, D), dtype=jnp.float32) * hidden ** (-0.5)
        b_out = jnp.zeros((D,), dtype=jnp.float32)
        return {'x': x, 'W_qkv': W_qkv, 'W_out': W_out, 'b_out': b_out}
    _L0_attn_all = _L0_attn_setup()
    _L0_attn_in = {k: v for k, v in _L0_attn_all.items() if k in ('W_qkv', 'W_out', 'b_out')}
    del _L0_attn_all

    def _L0_ffn_setup():
        import jax, jax.numpy as jnp
        import numpy as np
        B, S, D, E, H, K = (4, 1024, 64, 8, 128, 2)
        key = jax.random.key(seed)
        ks = jax.random.split(key, 6)
        x = jax.random.normal(ks[0], (B, S, D), jnp.float32)
        Wg = jax.random.normal(ks[1], (D, E), jnp.float32) * 0.02
        bg = jnp.zeros((E,), jnp.float32)
        W1 = jax.random.normal(ks[2], (E, D, H), jnp.float32) * 0.02
        b1 = jnp.zeros((E, H), jnp.float32)
        W2 = jax.random.normal(ks[3], (E, H, D), jnp.float32) * 0.02
        b2 = jnp.zeros((E, D), jnp.float32)
        return {'x': x, 'Wg': Wg, 'bg': bg, 'W1': W1, 'b1': b1, 'W2': W2, 'b2': b2}
    _L0_ffn_all = _L0_ffn_setup()
    _L0_ffn_in = {k: v for k, v in _L0_ffn_all.items() if k in ('Wg', 'bg', 'W1', 'b1', 'W2', 'b2')}
    del _L0_ffn_all
    return {'x': x, 'L0_tok_l_in_w': _L0_tok_in['l_in_w'], 'L0_tok_l_in_b': _L0_tok_in['l_in_b'], 'L0_tok_l_out_w': _L0_tok_in['l_out_w'], 'L0_tok_l_out_b': _L0_tok_in['l_out_b'], 'L0_tok_ln1_g': _L0_tok_in['ln1_g'], 'L0_tok_ln1_b': _L0_tok_in['ln1_b'], 'L0_tok_ff_w1': _L0_tok_in['ff_w1'], 'L0_tok_ff_b1': _L0_tok_in['ff_b1'], 'L0_tok_ff_w2': _L0_tok_in['ff_w2'], 'L0_tok_ff_b2': _L0_tok_in['ff_b2'], 'L0_tok_ln2_g': _L0_tok_in['ln2_g'], 'L0_tok_ln2_b': _L0_tok_in['ln2_b'], 'L0_tok_m_in_w': _L0_tok_in['m_in_w'], 'L0_tok_m_in_b': _L0_tok_in['m_in_b'], 'L0_tok_m_out_w': _L0_tok_in['m_out_w'], 'L0_tok_m_out_b': _L0_tok_in['m_out_b'], 'L0_attn_W_qkv': _L0_attn_in['W_qkv'], 'L0_attn_W_out': _L0_attn_in['W_out'], 'L0_attn_b_out': _L0_attn_in['b_out'], 'L0_ffn_Wg': _L0_ffn_in['Wg'], 'L0_ffn_bg': _L0_ffn_in['bg'], 'L0_ffn_W1': _L0_ffn_in['W1'], 'L0_ffn_b1': _L0_ffn_in['b1'], 'L0_ffn_W2': _L0_ffn_in['W2'], 'L0_ffn_b2': _L0_ffn_in['b2']}

def reference(x, L0_tok_l_in_w, L0_tok_l_in_b, L0_tok_l_out_w, L0_tok_l_out_b, L0_tok_ln1_g, L0_tok_ln1_b, L0_tok_ff_w1, L0_tok_ff_b1, L0_tok_ff_w2, L0_tok_ff_b2, L0_tok_ln2_g, L0_tok_ln2_b, L0_tok_m_in_w, L0_tok_m_in_b, L0_tok_m_out_w, L0_tok_m_out_b, L0_attn_W_qkv, L0_attn_W_out, L0_attn_b_out, L0_ffn_Wg, L0_ffn_bg, L0_ffn_W1, L0_ffn_b1, L0_ffn_W2, L0_ffn_b2):
    import jax
    import jax.numpy as jnp

    def _L0_tok_ref(x, l_in_w, l_in_b, l_out_w, l_out_b, ln1_g, ln1_b, ff_w1, ff_b1, ff_w2, ff_b2, ln2_g, ln2_b, m_in_w, m_in_b, m_out_w, m_out_b):
        import jax, jax.numpy as jnp
        import numpy as np
        NHEAD = 8
        KSIZE = 32
        EPS = 1e-05
        DIV_BASE = 10.0

        def _pos_encoding(S, D):
            pos = np.arange(S)[:, None].astype(np.float64)
            div = np.exp(np.arange(0, D, 2) * (-np.log(10000.0) / D))
            pe = np.zeros((S, D), np.float32)
            pe[:, 0::2] = np.sin(pos * div)
            pe[:, 1::2] = np.cos(pos * div)
            return jnp.asarray(pe)

        def _layer_norm(x, g, b):
            m = x.mean(-1, keepdims=True)
            v = ((x - m) ** 2).mean(-1, keepdims=True)
            return (x - m) / jnp.sqrt(v + EPS) * g + b

        def _mha(x, in_w, in_b, out_w, out_b):
            B, S, D = x.shape
            dh = D // NHEAD
            qkv = x @ in_w.T + in_b
            q, k, v = jnp.split(qkv, 3, axis=-1)
            sp = lambda t: t.reshape(B, S, NHEAD, dh).transpose(0, 2, 1, 3)
            q, k, v = (sp(q), sp(k), sp(v))
            att = jax.nn.softmax(jnp.einsum('bhqd,bhkd->bhqk', q, k) / jnp.sqrt(jnp.float32(dh)), axis=-1)
            o = jnp.einsum('bhqk,bhkd->bhqd', att, v).transpose(0, 2, 1, 3).reshape(B, S, D)
            return o @ out_w.T + out_b

        def _forward(x, l_in_w, l_in_b, l_out_w, l_out_b, ln1_g, ln1_b, ff_w1, ff_b1, ff_w2, ff_b2, ln2_g, ln2_b, m_in_w, m_in_b, m_out_w, m_out_b):
            B, L, D = x.shape
            amp = jnp.abs(jnp.fft.rfft(x, axis=1))
            feat = jax.lax.stop_gradient(jnp.concatenate([x[:, -1:, :], amp], axis=1))
            src = feat + _pos_encoding(feat.shape[1], D)[None]
            a = _mha(src, l_in_w, l_in_b, l_out_w, l_out_b)
            src = _layer_norm(src + a, ln1_g, ln1_b)
            ff = jax.nn.relu(src @ ff_w1.T + ff_b1) @ ff_w2.T + ff_b2
            src = _layer_norm(src + ff, ln2_g, ln2_b)
            out = _mha(src, m_in_w, m_in_b, m_out_w, m_out_b)
            tau = jnp.clip(jax.nn.softplus(out[:, -1:, :]) / DIV_BASE, 0.01, 1.0)
            Lout = L - KSIZE + 1
            idx = jnp.arange(Lout)[:, None] + jnp.arange(KSIZE)[None, :]
            xw = x[:, idx, :]
            seq = jnp.arange(KSIZE - 1, -1, -1, dtype=x.dtype)
            powers = tau[:, 0, :, None] ** seq
            w = powers / powers.sum(-1, keepdims=True)
            return jnp.einsum('bdk,blkd->bld', w, xw)
        return _forward(x, l_in_w, l_in_b, l_out_w, l_out_b, ln1_g, ln1_b, ff_w1, ff_b1, ff_w2, ff_b2, ln2_g, ln2_b, m_in_w, m_in_b, m_out_w, m_out_b)

    def _L0_attn_ref(x, W_qkv, W_out, b_out):
        import jax, jax.numpy as jnp
        import numpy as np
        HEADS = 4
        DIM_HEAD = 32
        B, L, D = x.shape
        scale = DIM_HEAD ** (-0.5)
        qkv = jnp.einsum('bld,df->blf', x, W_qkv)
        qkv = qkv.reshape(B, L, 3, HEADS, DIM_HEAD)
        q = jnp.transpose(qkv[:, :, 0], (0, 2, 1, 3)) * scale
        k = jax.nn.softmax(jnp.transpose(qkv[:, :, 1], (0, 2, 1, 3)), axis=2)
        v = jnp.transpose(qkv[:, :, 2], (0, 2, 1, 3))
        context = jnp.einsum('bhld,bhle->bhde', k, v)
        out = jnp.einsum('bhde,bhld->bhle', context, q)
        out = jnp.transpose(out, (0, 2, 1, 3)).reshape(B, L, HEADS * DIM_HEAD)
        return jnp.einsum('blf,fd->bld', out, W_out) + b_out

    def _L0_ffn_ref(x, Wg, bg, W1, b1, W2, b2):
        import jax, jax.numpy as jnp
        import numpy as np
        B, S, D, E, H, K = (4, 1024, 64, 8, 128, 2)
        Bv, Sv, Dv = x.shape
        gate_scores = x @ Wg + bg
        _, idx = jax.lax.top_k(gate_scores, K)
        mask = jax.nn.one_hot(idx, E, dtype=x.dtype).sum(axis=-2)
        xf = x.reshape(-1, Dv)
        mf = mask.reshape(-1, E)
        h = jax.nn.gelu(jnp.einsum('td,edh->teh', xf, W1) + b1[None], approximate=False)
        y = jnp.einsum('teh,ehd->ted', h, W2) + b2[None]
        out = jnp.einsum('ted,te->td', y, mf)
        return out.reshape(Bv, Sv, Dv)
    h = _L0_tok_ref(x, L0_tok_l_in_w, L0_tok_l_in_b, L0_tok_l_out_w, L0_tok_l_out_b, L0_tok_ln1_g, L0_tok_ln1_b, L0_tok_ff_w1, L0_tok_ff_b1, L0_tok_ff_w2, L0_tok_ff_b2, L0_tok_ln2_g, L0_tok_ln2_b, L0_tok_m_in_w, L0_tok_m_in_b, L0_tok_m_out_w, L0_tok_m_out_b)
    h = h + _L0_attn_ref(_layernorm(h, axis=-1), L0_attn_W_qkv, L0_attn_W_out, L0_attn_b_out)
    h = h + _L0_ffn_ref(_layernorm(h, axis=-1), L0_ffn_Wg, L0_ffn_bg, L0_ffn_W1, L0_ffn_b1, L0_ffn_W2, L0_ffn_b2)
    return h

_drawn_inputs = setup_inputs


def setup_inputs(seed=0):
    import zlib

    import numpy as np

    out = dict(_drawn_inputs(seed))
    spreads = {'L0_tok_l_in_b': (0.0, 2.0),
     'L0_tok_l_out_b': (0.0, 2.0),
     'L0_tok_ln1_g': (1.0, 0.6),
     'L0_tok_ln1_b': (0.0, 0.8),
     'L0_tok_ff_b1': (0.0, 0.8),
     'L0_tok_ff_b2': (0.0, 0.8),
     'L0_tok_ln2_g': (1.0, 0.6),
     'L0_tok_ln2_b': (0.0, 0.8),
     'L0_tok_m_in_b': (0.0, 0.8),
     'L0_tok_m_out_b': (0.0, 0.533),
     'L0_attn_b_out': (0.0, 0.1),
     'L0_ffn_bg': (0.0, 0.1),
     'L0_ffn_b1': (0.0, 0.498),
     'L0_ffn_b2': (0.0, 0.1)}
    factors = {'L0_tok_l_in_w': 8.0,
     'L0_tok_l_out_w': 8.0,
     'L0_tok_ff_w1': 8.0,
     'L0_tok_ff_w2': 8.0,
     'L0_tok_m_in_w': 8.0,
     'L0_tok_m_out_w': 8.0}
    for name, (base, spread) in spreads.items():
        noise = np.random.default_rng([zlib.crc32(name.encode()), seed]).standard_normal(out[name].shape)
        drawn = base * np.exp(spread * noise) if base else spread * noise
        out[name] = jnp.asarray(drawn.astype(out[name].dtype))
    for name, factor in factors.items():
        out[name] = (out[name] * factor).astype(out[name].dtype)
    return out
```

```python
from contextlib import ExitStack

import numpy as np
import concourse.bass as bass
from concourse import mybir

ACT = mybir.ActivationFunctionType
ALU = mybir.AluOpType
F32 = mybir.dt.float32
BF16 = mybir.dt.bfloat16
AX_X = mybir.AxisListType.X

B, L, D = 16, 256, 64
P = 128
PAIRS = B // 2
HALF = PAIRS // 2
QUADS = PAIRS // 2
NFREQ = L // 2
TOK = NFREQ + 2
HEADS, DH = 8, 8
LEFT = TOK - P
WIN = 32
LOUT = L - WIN + 1
CH = 113
STEP = LOUT - CH
FF = 4 * D
AH, AD = 4, 32
E_N, HID = 8, 128
EPS = 1e-5
BIG = 2.0 ** 60
TERMS = 6
ARENA = 28300
Q_TERM = (0, 0, 1, 0, 1, 2)
K_TERM = (0, 1, 0, 2, 1, 0)
SHIFT_ROW = TERMS * DH
N_ROW, M_ROW, ONE_ROW = D, D + E_N, D + 2 * E_N

PACKS = {
    "dft": [("dft", 2 * L), ("ident", P)],
    "qkv": [("posenc", TOK), ("wq", P), ("wk", P), ("wv", P), ("wv_stack", D), ("bq", 1), ("bk", 1),
            ("bv_row", P), ("head16", 16), ("batch16", 16), ("vl_mask", 2 * D), ("vl_const", 2 * P),
            ("sel_left", 2 * D), ("sel_pair", P)],
    "enc": [("wo", P), ("center", P), ("mean", P), ("bo", 1), ("g1", 1), ("b1", 1), ("g2", 1), ("b2", 1),
            ("eps", 1), ("ff1", 4 * P), ("ffb1", 2), ("ff2", 4 * P), ("ffb2", 1),
            ("wq2", P), ("bq2", 1), ("wk2", P), ("head32", 32), ("wv2", P), ("bv2", 1), ("wo2", P), ("bo2", 1)],
    "att": [("wk_att", 2 * P), ("wv_att", 2 * P), ("ctx_mask", P), ("wqT", D), ("wout", D), ("mix_mask", P),
            ("bout_row", P), ("rank", 2 * P), ("neghalf", 32), ("gate", E_N), ("b2rows", D)],
    "ffn": [("up", E_N * HID), ("down", E_N * D)],
}
WIDTH = {k: sum(w for _, w in v) for k, v in PACKS.items()}


def audio_tower(nc, x, packs, out):
    scr_qk = nc.dram_tensor("scr_qk", (2, 2 * 3, P, HALF * TOK), BF16, kind="Internal").ap()
    scr_m = nc.dram_tensor("scr_m", (2, 3, HALF * 16, TOK), BF16, kind="Internal").ap()

    with ExitStack() as ctx:
        def sb(name, shape, dt=F32):
            return ctx.enter_context(nc.sbuf_tensor(name, shape, dt))

        def sem(name):
            return ctx.enter_context(nc.semaphore(name))

        psum = ctx.enter_context(nc.psum_tensor("psum", [P, 8, 512], F32))
        bank = [psum[:, i, :] for i in range(8)]

        pk = {k: sb(f"pk_{k}", [P, w]) for k, w in WIDTH.items()}
        col = {}
        for k, cols in PACKS.items():
            at = 0
            for name, w in cols:
                col[name] = pk[k][:, at:at + w]
                at += w
        dft = col["dft"].rearrange("p (c n) -> p c n", c=2)
        ident = col["ident"]
        vl_mask = col["vl_mask"].rearrange("p (s d) -> p s d", s=2)
        sel_left = col["sel_left"].rearrange("p (t m) -> p t m", t=2)
        sel_pair = col["sel_pair"].rearrange("p (j m) -> p j m", j=HALF)
        ff1 = col["ff1"].rearrange("p (q n) -> p q n", q=4)
        ff2 = col["ff2"].rearrange("p (q n) -> p q n", q=4)
        wk_att = col["wk_att"].rearrange("p (s n) -> p s n", s=2)
        up = col["up"].rearrange("p (e n) -> p e n", e=E_N)
        down = col["down"].rearrange("p (e n) -> p e n", e=E_N)

        arena = sb("arena", [P, ARENA])
        used = {"encoder": 0, "middle": 0, "layers": 0}

        def shared(time, shape, dt=F32):
            n = int(np.prod(shape[1:])) * (1 if dt == F32 else 2) // (1 if dt == F32 else 4)
            a = used[time]
            used[time] += n
            assert used[time] <= ARENA
            v = arena[0:shape[0], a:a + n]
            v = v if dt == F32 else v.bitcast(dt)
            dims = " ".join(f"d{i}" for i in range(1, len(shape)))
            return v.rearrange(f"p ({dims}) -> p {dims}", **{f"d{i}": shape[i] for i in range(1, len(shape))})

        sq = sb("sq", [P, PAIRS, L])
        xT = sb("xT", [P, PAIRS, L])
        amp2 = sb("amp2", [P, PAIRS, NFREQ + 1])
        amp = amp2
        src = sb("src", [P, PAIRS, TOK])
        QT = shared("encoder", [P, PAIRS, TOK])
        KT = shared("encoder", [P, PAIRS, TOK])
        V = shared("encoder", [P, PAIRS, P])
        vleft_in = sb("vleft_in", [P, PAIRS, 16, LEFT])
        vl_tmp = sb("vl_tmp", [P, 2, D])
        VL = sb("VL", [P, 2, 2, P])
        resid = shared("encoder", [P, 2, HALF * TOK])
        qk3 = [shared("encoder", [P, 6, HALF * TOK], BF16) for h in range(2)]
        QS32 = [shared("encoder", [P, 8 * HALF * TOK]) for h in range(2)]
        QS = [q[:, :].bitcast(BF16).rearrange("p (u s g n) -> p u s g n", u=2, s=2, g=4) for q in QS32]
        KS = [shared("encoder", [P, 2, 4, HALF * TOK], BF16) for h in range(2)]
        qleft = shared("encoder", [P, PAIRS, 16, LEFT])
        kleft = shared("encoder", [P, PAIRS, 16, LEFT])
        mneg = sb("mneg", [P, 2, HALF * 16])
        mlneg = sb("mlneg", [P, 2])
        mT = sb("mT", [HALF * 16, 2, TOK])
        mres = sb("mres", [HALF * 16, 2, 2, TOK])
        m3 = sb("m3", [HALF * 16, 2, 3, TOK], BF16)
        EL = sb("EL", [P, 2, TOK])
        ET = shared("encoder", [P, 4, 4, TOK])
        xl = ET.rearrange("p a b n -> p (a b n)")[:, 0:2 * B * D].rearrange("p (c n) -> p c n", c=2)
        Vx = shared("encoder", [P, 4, HEADS, P])
        rden = sb("rden", [P, 2, TOK])
        OT = sb("OT", [P, PAIRS, TOK])
        z = [shared("middle", [P, PAIRS, TOK]) for k in range(2)]
        lnsq = shared("middle", [P, PAIRS, TOK])
        sdev = shared("middle", [P, PAIRS, TOK])
        rstd = shared("middle", [P, PAIRS, TOK])
        lnn = shared("middle", [P, PAIRS, TOK])
        enc = [sb(f"enc{k}", [P, PAIRS, TOK]) for k in range(2)]
        relu = shared("middle", [P, 2, 4, 2 * TOK])
        y = shared("middle", [P, PAIRS, L + 1])
        hraw = sq[:, :, 0:LOUT]
        hT = sb("hT", [P, PAIRS, LOUT])

        s2t = shared("middle", [P, PAIRS, P])
        s2l = sb("s2l", [LEFT, PAIRS, P])
        tv = {n: sb(f"tau_{n}", [P, PAIRS]) for n in ("q", "o", "ob", "t0", "abs", "exp", "ln", "sp", "clip", "tau", "p2",
                                                      "p4", "p8", "p16", "p32", "neg32", "s1", "s2", "s3", "s4", "s5",
                                                      "inv")}
        q2m = sb("q2m", [P, PAIRS, 32])
        u2 = sb("u2", [P, PAIRS, 32])
        c2 = sb("c2", [P, PAIRS, 32])
        o2t = sb("o2t", [P, PAIRS, 32])
        mx2 = sb("mx2", [P, 3, 2])
        psm = sb("psm", [P, 2])
        prob = sb("prob", [P, 2, TOK])
        PT = sb("PT", [P, 2, P])
        PTl = sb("PTl", [LEFT, 2, P])
        asq = shared("layers", [CH, QUADS, 512])
        xn = shared("layers", [CH, QUADS, 2, 2, 2, D])
        xnT = shared("layers", [P, PAIRS, LOUT])
        st = {n: sb(f"st_{n}", [CH, 32]) for n in ("ss0", "var0", "rs0", "sum1", "mean1", "ss1", "var1", "rs1")}
        km = sb("km", [P, 8, 2])
        ksum = sb("ksum", [P, 8, 2])
        rks = sb("rks", [P, 8, 2])
        E = shared("layers", [P, 8, 2, LOUT])
        ETt = shared("layers", [CH, 8, 2, 2, P])
        hid = arena[:, 0:2 * E_N * 2 * LOUT].rearrange("p (a e n) -> p a e n", a=2, e=E_N)
        GT = shared("layers", [P, PAIRS, P])
        cx = shared("layers", [P, PAIRS, 2, P])
        Zs = shared("layers", [P, PAIRS, P])
        Mb = shared("layers", [P, PAIRS, 2, D])
        h2 = shared("layers", [CH, QUADS, 2, 2, 2, D])
        xg = shared("layers", [P, B, LOUT])
        tp = {n: shared("layers", [CH, 32, E_N]) for n in ("g", "eq1", "rk1", "sel1", "g2", "eq2", "rk2", "sel2")}
        tm = {n: sb(f"topm_{n}", [CH, 32]) for n in ("m1", "p1", "m2", "p2")}
        nm = sb("nm", [CH, 32, 16], BF16)
        identb = sb("identb", [P, P], BF16)
        osb = shared("layers", [CH, 2, 2, 2, D])

        step_sems = {e: sem(f"{e}_step") for e in ("dve", "pool")}
        names = ("ld_dft ld_x0 ld_x1 ld_qkv ld_enc ld_att ld_ffn qs_zero ks_one fft_done xt_done sq_done xT_ready "
                 "amp2_ready amp_ready src_ready q_done k_done v_done vl_done qT_ready kT_ready v_ready vl_ready "
                 "vleft_in_ready split_ready qk_stored strips0 strips1 left_ready s_done max_ready sl_done "
                 "mlneg_ready mt_done mT_ready m3_ready m_stored shift0 shift1 kl_done el_ready st_done exp_done "
                 "vx_ready pv_done ot_ready wo_done z_ready0 z_ready1 ctr_done0 ctr_done1 lsq_ready0 lsq_ready1 "
                 "var_done0 var_done1 sdev_ready0 sdev_ready1 enc_ready0 enc_ready1 ff1_done relu_ready ff2_done "
                 "tau_q tau_q_ready tau_u tau_u_ready tau_s tau_m tau_e tau_p_ready s2t_done s2t_ready pT_done "
                 "pT_ready tau_c tau_c_ready tau_v tau_o_ready tau_out tau_abs tau_exp tau_ln inv_ready hraw_ready "
                 "h_ready xg_preset identb_ready a1_done asq_ready var_ready rs_ready xn_ready a2_done xnT_ready "
                 "kp_done km_ready ke_ready et_done ett_ready gt_done gt_ready ctx_done ctx_ready zz_done zz_ready "
                 "mx_done mix_ready h2_done h2_ready xc_ready x2_ready a11_done xg_even xg_odd gate_done nm_ready "
                 "mk_done mk_ready up_done gelu_done down_done o_ready out_stored0 out_stored1").split()
        S = {n: sem(n) for n in names}

        block = ctx.enter_context(nc.Block())
        scale_h = 1.0 / float(np.sqrt(np.float32(DH)))

        @block.sync
        def _(sp):
            xs = x.rearrange("b (c l) d -> l c b d", c=2)
            xd = xl[:, :, :].rearrange("p c (b d) -> p c b d", b=B)
            for h in range(2):
                for c in range(2):
                    sp.dma_start(xd[:, c, 8 * h:8 * h + 8, :], xs[:, c, 8 * h:8 * h + 8, :]).then_inc(S[f"ld_x{h}"], 16)
            for h in range(2):
                sp.wait_ge(S["split_ready"], h + 1)
                sp.dma_start(scr_qk[h].rearrange("t p n -> p t n"), qk3[h][:, :, :]).then_inc(S["qk_stored"], 16)
                sp.wait_ge(S["qs_zero"], h + 1)
                sp.wait_ge(S["ks_one"], h + 1)
                sp.wait_ge(S["qk_stored"], 16 * (h + 1))
                for t in range(TERMS):
                    qsrc = scr_qk[h, Q_TERM[t]].rearrange("(s g u i) n -> u i (s g) n", s=2, g=4, u=2)
                    ksrc = scr_qk[h, 3 + K_TERM[t]].rearrange("(s g u i) n -> u i (s g) n", s=2, g=4, u=2)
                    for u in range(2):
                        r = 64 * u + DH * t
                        sp.dma_start(QS[h][r:r + DH, u, :, :, :].rearrange("p s g n -> p (s g) n"), qsrc[u]).then_inc(S[f"strips{h}"], 16)
                        sp.dma_start(KS[h][r:r + DH, :, :, :].rearrange("p s g n -> p (s g) n"), ksrc[u]).then_inc(S[f"strips{h}"], 16)
            for h in range(2):
                sp.wait_ge(S["m3_ready"], h + 1)
                sp.dma_start(scr_m[h].rearrange("k r n -> r k n"), m3[:, h, :, :]).then_inc(S["m_stored"], 16)
                sp.wait_ge(S["m_stored"], 16 * (h + 1))
                for k in range(3):
                    msrc = scr_m[h, k].rearrange("(j s g u) n -> u s g j n", j=HALF, s=2, g=4)
                    for u in range(2):
                        r = 64 * u + SHIFT_ROW + k
                        for s in range(2):
                            dst = QS[h][r:r + 1, u, s, :, :].rearrange("p g (j n) -> p g j n", j=HALF)
                            sp.dma_start(dst, msrc[u, s].unsqueeze(0)).then_inc(S[f"shift{h}"], 16)
            for t in range(PAIRS):
                sp.wait_ge(S["o_ready"], t + 1)
                for c in range(2):
                    n = STEP + c
                    sp.dma_start(out[2 * t:2 * t + 2, STEP * c:STEP * c + n, :].rearrange("s l d -> l s d"),
                                 osb[0:n, t % 2, :, c, :]).then_inc(S[f"out_stored{t % 2}"], 16)
            for k in range(2):
                sp.wait_ge(S[f"out_stored{k}"], 16 * PAIRS)

        @block.gpsimd
        def _(pool):
            for h in range(2):
                nc.gpsimd.memset(QS32[h][:, :], 0.0).then_inc(S["qs_zero"], 1)
                nc.gpsimd.memset(KS[h][:, :, :, :], 1.0).then_inc(S["ks_one"], 1)
            nc.gpsimd.memset(Vx[:, :, :, :], 0.0).then_inc(step_sems["pool"], 1)
            pool.wait_ge(step_sems["pool"], 1)
            for slot in range(4):
                for hd in range(HEADS):
                    c0 = 64 * (1 - slot % 2) + DH * hd
                    last = nc.gpsimd.memset(Vx[:, slot, hd, c0:c0 + DH], 1.0)
            last.then_inc(step_sems["pool"], 1)
            pool.wait_ge(step_sems["pool"], 2)
            for b in range(B):
                j, s = b // 2, b % 2
                pool.wait_ge(S["v_ready"], j // 2 + 1)
                if b >= 4:
                    pool.wait_ge(S["pv_done"], b - 3)
                for hd in range(HEADS):
                    c0 = 64 * s + DH * hd
                    last = nc.gpsimd.tensor_copy(Vx[:, b % 4, hd, c0:c0 + DH],
                                                 V[:, j, 64 * s + DH * hd:64 * s + DH * hd + DH])
                last.then_inc(S["vx_ready"], 1)
            pool.wait_ge(S["ld_att"], 16)
            for k in range(2):
                pool.wait_ge(S["var_ready"], k + 1)
                if k:
                    pool.wait_ge(S["xg_preset"], 1)
                nc.gpsimd.tensor_tensor(st[f"rs{k}"][:, :], st[f"var{k}"][:, :], col["neghalf"][0:CH, :],
                                        ALU.pow).then_inc(S["rs_ready"], 1)
                if k == 0:
                    pool.wait_ge(S["rs_ready"], 1)
                    nc.gpsimd.memset(xg[64:96, :, :], 1.0).then_inc(step_sems["pool"], 1)
                    pool.wait_ge(step_sems["pool"], 3)
                    nc.gpsimd.memset(xg[96:128, :, :], 0.0).then_inc(S["xg_preset"], 1)

        @block.scalar
        def _(act):
            for k in PACKS:
                act.dma_start(pk[k][:, :], packs[k]).then_inc(S[f"ld_{k}"], 16)
            for c in range(QUADS):
                act.wait_ge(S["fft_done"], c + 1)
                nc.scalar.activation(sq[:, 2 * c:2 * c + 2, :], bank[c][:, :].rearrange("p (j n) -> p j n", j=2),
                                     ACT.Square).then_inc(S["sq_done"], 1)
            for c in range(QUADS):
                act.wait_ge(S["amp2_ready"], c + 1)
                nc.scalar.activation(amp[:, 2 * c:2 * c + 2, :], amp2[:, 2 * c:2 * c + 2, :],
                                     ACT.Sqrt).then_inc(S["amp_ready"], 1)
            act.wait_ge(S["ld_qkv"], 16)
            for c in range(QUADS):
                for (w, T, b) in (("q", QT, "bq"), ("k", KT, "bk")):
                    act.wait_ge(S[f"{w}_done"], c + 1)
                    ps = bank[(0 if w == "q" else 2) + c % 2][:, 0:2 * TOK].rearrange("p (j n) -> p j n", j=2)
                    nc.scalar.activation(T[:, 2 * c:2 * c + 2, :], ps, ACT.Identity,
                                         bias=col[b]).then_inc(S[f"{w}T_ready"], 1)
            unit = 0
            for h in range(2):
                act.wait_ge(S["kl_done"], h + 1)
                nc.scalar.activation(EL[:, h, :], bank[6][:, 0:TOK], ACT.Exp, scale=scale_h).then_inc(S["el_ready"], 1)
                for _b in range(2 * HALF):
                    for _u in range(2):
                        act.wait_ge(S["st_done"], unit + 1)
                        if unit >= 4:
                            act.wait_ge(S["pv_done"], unit // 2 - 1)
                        k0 = 2 + 2 * (unit % 2)
                        nc.scalar.activation(ET[:, unit % 4, :, :].rearrange("p (k u) n -> p k (u n)", k=2),
                                             psum[:, k0:k0 + 2, 0:2 * TOK], ACT.Exp,
                                             scale=scale_h).then_inc(S["exp_done"], 1)
                        unit += 1

            def layer_norm_act(k, ctr, var):
                for c in range(QUADS):
                    act.wait_ge(S[f"ctr_done{k}"], c + 1)
                    nc.scalar.activation(lnsq[:, 2 * c:2 * c + 2, :],
                                         bank[ctr + c][:, 0:2 * TOK].rearrange("p (j n) -> p j n", j=2),
                                         ACT.Square).then_inc(S[f"lsq_ready{k}"], 1)
                for c in range(QUADS):
                    act.wait_ge(S[f"var_done{k}"], c + 1)
                    nc.scalar.activation(sdev[:, 2 * c:2 * c + 2, :],
                                         bank[var + c][:, 0:2 * TOK].rearrange("p (j n) -> p j n", j=2),
                                         ACT.Sqrt, bias=col["eps"]).then_inc(S[f"sdev_ready{k}"], 1)

            act.wait_ge(S["ld_enc"], 16)
            layer_norm_act(0, 4, 0)
            for c in range(QUADS):
                for q in range(4):
                    act.wait_ge(S["ff1_done"], 4 * c + q + 1)
                    if c >= 2:
                        act.wait_ge(S["ff2_done"], c - 1)
                    nc.scalar.activation(relu[:, c % 2, q, :], bank[q][:, 0:2 * TOK], ACT.Relu,
                                         bias=col["ffb1"][:, q % 2:q % 2 + 1]).then_inc(S["relu_ready"], 1)
            layer_norm_act(1, 0, 4)
            for n in range(2):
                act.wait_ge(S["s2t_done"], n + 1)
                nc.scalar.copy(s2t[:, 4 * n:4 * n + 4, :], bank[n].rearrange("p (j n) -> p j n", j=4))
                nc.scalar.copy(s2l[:, 4 * n:4 * n + 4, :],
                               bank[2 + n][0:LEFT, :].rearrange("p (j n) -> p j n", j=4)).then_inc(S["s2t_ready"], 1)
            act.wait_ge(S["tau_m"], 1)
            for jj in range(2):
                ins = nc.scalar.activation(prob[:, jj, :], bank[6][:, TOK * jj:TOK * jj + TOK], ACT.Exp,
                                           bias=mx2[:, 1, jj:jj + 1], scale=scale_h, accum_out=psm[:, jj:jj + 1])
            ins.then_inc(S["tau_e"], 1)
            act.wait_ge(S["tau_abs"], 1)
            nc.scalar.activation(tv["exp"][:, :], tv["abs"][:, :], ACT.Exp, scale=-1.0).then_inc(S["tau_exp"], 1)
            act.wait_ge(S["tau_exp"], 1)
            nc.scalar.activation(tv["ln"][:, :], tv["exp"][:, :], ACT.Ln, bias=1.0).then_inc(S["tau_ln"], 1)
            act.wait_ge(S["inv_ready"], 1)
            for j in range(PAIRS):
                act.wait_ge(S["hraw_ready"], j + 1)
                nc.scalar.activation(hT[:, j, :], hraw[:, j, :], ACT.Identity,
                                     scale=tv["inv"][:, j:j + 1]).then_inc(S["h_ready"], 1)
            for c in range(QUADS):
                act.wait_ge(S["a1_done"], c + 1)
                nc.scalar.activation(asq[:, c, :], bank[c][0:CH, :], ACT.Square).then_inc(S["asq_ready"], 1)
            for c in range(QUADS):
                act.wait_ge(S["a2_done"], c + 1)
                nc.scalar.copy(xnT[:, 2 * c:2 * c + 2, :],
                               bank[4 + c][:, 0:2 * LOUT].rearrange("p (j n) -> p j n", j=2)).then_inc(S["xnT_ready"], 1)
            for n in range(8):
                act.wait_ge(S["km_ready"], n + 1)
                for jj in range(2):
                    ins = nc.scalar.activation(E[:, n, jj, :], bank[n % 4][:, LOUT * jj:LOUT * jj + LOUT], ACT.Exp,
                                               bias=km[:, n, jj:jj + 1], accum_out=ksum[:, n, jj:jj + 1])
                ins.then_inc(S["ke_ready"], 1)
            for n in range(2):
                act.wait_ge(S["gt_done"], n + 1)
                nc.scalar.copy(GT[:, 4 * n:4 * n + 4, :], bank[n].rearrange("p (j n) -> p j n", j=4)).then_inc(S["gt_ready"], 1)
            for n in range(2):
                act.wait_ge(S["zz_done"], n + 1)
                nc.scalar.copy(Zs[:, 4 * n:4 * n + 4, :], bank[2 + n].rearrange("p (j n) -> p j n", j=4)).then_inc(S["zz_ready"], 1)
            for c in range(QUADS):
                act.wait_ge(S["xc_ready"], c + 1)
                nc.scalar.activation(asq[:, c, :], xn[:, c, :, :, :, :].rearrange("p a b s d -> p (a b s d)"),
                                     ACT.Square).then_inc(S["asq_ready"], 1)
            act.wait_ge(S["xg_preset"], 1)
            for c in range(QUADS):
                act.wait_ge(S["a11_done"], c + 1)
                nc.scalar.copy(xg[0:64, 4 * c:4 * c + 4:2, :],
                               bank[c][0:64, 0:2 * LOUT].rearrange("p (j n) -> p j n", j=2)).then_inc(S["xg_even"], 1)
            unit = 0
            for t in range(PAIRS):
                for e in range(0, E_N, 2):
                    act.wait_ge(S["up_done"], unit + 1)
                    if t >= 2:
                        act.wait_ge(S["down_done"], t - 1)
                    k0 = 2 * (unit % 2)
                    nc.scalar.activation(hid[:, t % 2, e:e + 2, :], psum[:, k0:k0 + 2, 0:2 * LOUT],
                                         ACT.Gelu).then_inc(S["gelu_done"], 1)
                    unit += 1

        @block.vector
        def _(dve):
            chain = [0]

            def link(ins):
                chain[0] += 1
                ins.then_inc(step_sems["dve"], 1)
                dve.wait_ge(step_sems["dve"], chain[0])

            for c in range(QUADS):
                dve.wait_ge(S["xt_done"], c + 1)
                nc.vector.tensor_copy(xT[:, 2 * c:2 * c + 2, :],
                                      bank[4 + c][:, :].rearrange("p (j n) -> p j n", j=2)).then_inc(S["xT_ready"], 1)
            for c in range(QUADS):
                dve.wait_ge(S["sq_done"], c + 1)
                two = slice(2 * c, 2 * c + 2)
                nc.vector.tensor_tensor(amp2[:, two, 1:NFREQ], sq[:, two, 1:NFREQ], sq[:, two, NFREQ + 1:L], ALU.add)
                nc.vector.tensor_copy(amp2[:, two, 0:NFREQ + 1:NFREQ],
                                      sq[:, two, 0:NFREQ + 1:NFREQ]).then_inc(S["amp2_ready"], 1)
            dve.wait_ge(S["ld_qkv"], 16)
            dve.wait_ge(S["xT_ready"], QUADS)
            for c in range(QUADS):
                dve.wait_ge(S["amp_ready"], c + 1)
                two = slice(2 * c, 2 * c + 2)
                pe = col["posenc"].unsqueeze(1)
                nc.vector.tensor_tensor(src[:, two, 0:NFREQ + 1], amp[:, two, :],
                                        pe[:, :, 0:NFREQ + 1].to_broadcast([P, 2, NFREQ + 1]), ALU.add)
                nc.vector.tensor_tensor(src[:, two, TOK - 1:TOK], xT[:, two, L - 1:L],
                                        pe[:, :, TOK - 1:TOK].to_broadcast([P, 2, 1]), ALU.add).then_inc(S["src_ready"], 1)
            head16 = col["head16"].unsqueeze(2).to_broadcast([P, 16, LEFT])
            batch16 = col["batch16"].unsqueeze(2).to_broadcast([P, 16, LEFT])
            nc.vector.tensor_copy(VL[:, :, :, :].rearrange("p h s n -> p h (s n)"),
                                  col["vl_const"].unsqueeze(1).to_broadcast([P, 2, 2 * P]))
            dve.wait_ge(S["src_ready"], QUADS)
            for j in range(PAIRS):
                ins = nc.vector.tensor_tensor(vleft_in[:, j, :, :], src[:, j, P:TOK].unsqueeze(1).to_broadcast([P, 16, LEFT]),
                                              batch16, ALU.mult)
            ins.then_inc(S["vleft_in_ready"], 1)
            bv2 = col["bv_row"].unsqueeze(1).to_broadcast([P, 2, P])
            for h in range(2):
                for c in range(2 * h, 2 * h + 2):
                    dve.wait_ge(S["v_done"], c + 1)
                    nc.vector.tensor_tensor(V[:, 2 * c:2 * c + 2, :],
                                            bank[4 + c % 2][:, 0:2 * P].rearrange("p (j n) -> p j n", j=2),
                                            bv2, ALU.add).then_inc(S["v_ready"], 1)
                dve.wait_ge(S["vl_done"], h + 1)
                link(nc.vector.tensor_tensor(vl_tmp[:, h, :], bank[6 + h][:, 0:D], col["bv_row"][:, 0:D], ALU.add))
                for s in range(2):
                    ins = nc.vector.tensor_tensor(VL[:, h, s, 64 * s:64 * s + 64], vl_tmp[:, h, :], vl_mask[:, s, :], ALU.mult)
                ins.then_inc(S["vl_ready"], 1)
                four = slice(HALF * h, HALF * h + HALF)
                dve.wait_ge(S["qT_ready"], 2 * h + 2)
                dve.wait_ge(S["kT_ready"], 2 * h + 2)
                for n, T in enumerate((QT, KT)):
                    full = T[:, four, :].rearrange("p j n -> p (j n)")
                    link(nc.vector.tensor_copy(qk3[h][:, 3 * n, :], full))
                    link(nc.vector.tensor_tensor(resid[:, n, :], full, qk3[h][:, 3 * n, :], ALU.subtract))
                    link(nc.vector.tensor_copy(qk3[h][:, 3 * n + 1, :], resid[:, n, :]))
                    ins = nc.vector.tensor_tensor(qk3[h][:, 3 * n + 2, :], resid[:, n, :], qk3[h][:, 3 * n + 1, :],
                                                  ALU.subtract)
                    if n == 0:
                        link(ins)
                ins.then_inc(S["split_ready"], 1)
                for j in range(HALF * h, HALF * h + HALF):
                    nc.vector.tensor_tensor(qleft[:, j, :, :], QT[:, j, P:TOK].unsqueeze(1).to_broadcast([P, 16, LEFT]),
                                            head16, ALU.mult)
                    ins = nc.vector.tensor_tensor(kleft[:, j, :, :], KT[:, j, P:TOK].unsqueeze(1).to_broadcast([P, 16, LEFT]),
                                                  head16, ALU.mult)
                ins.then_inc(S["left_ready"], 1)
            unit = 0
            for h in range(2):
                for b in range(2 * HALF):
                    for n, hd0 in ((3, 0), (3, 3), (2, 6)):
                        dve.wait_ge(S["s_done"], unit + 1)
                        nc.vector.tensor_reduce(mneg[:, h, 8 * b + hd0:8 * b + hd0 + n],
                                                bank[unit % 2][:, 0:n * TOK].rearrange("p (a n) -> p a n", a=n),
                                                AX_X, ALU.max, negate=True).then_inc(S["max_ready"], 1)
                        unit += 1
                dve.wait_ge(S["sl_done"], h + 1)
                nc.vector.tensor_reduce(mlneg[:, h:h + 1], bank[6][:, 0:TOK], AX_X, ALU.max,
                                        negate=True).then_inc(S["mlneg_ready"], 1)
                dve.wait_ge(S["mt_done"], h + 1)
                nc.vector.tensor_copy(mT[:, h, :], bank[7][0:64, 0:TOK]).then_inc(S["mT_ready"], 1)
                dve.wait_ge(S["mT_ready"], h + 1)
                link(nc.vector.tensor_copy(m3[:, h, 0, :], mT[:, h, :]))
                link(nc.vector.tensor_tensor(mres[:, h, 0, :], mT[:, h, :], m3[:, h, 0, :], ALU.subtract))
                link(nc.vector.tensor_copy(m3[:, h, 1, :], mres[:, h, 0, :]))
                nc.vector.tensor_tensor(m3[:, h, 2, :], mres[:, h, 0, :], m3[:, h, 1, :],
                                        ALU.subtract).then_inc(S["m3_ready"], 1)
            for b in range(B):
                j, s = b // 2, b % 2
                mine, other = slice(64 * s, 64 * s + 64), slice(64 * (1 - s), 64 * (1 - s) + 64)
                dve.wait_ge(S["pv_done"], b + 1)
                link(nc.vector.reciprocal(rden[mine, b % 2, :], bank[6 + b % 2][other, 0:TOK]))
                nc.vector.tensor_tensor(OT[mine, j, :], bank[6 + b % 2][mine, 0:TOK], rden[mine, b % 2, :],
                                        ALU.mult).then_inc(S["ot_ready"], 1)

            def two_of(ap, c):
                return ap[:, 2 * c:2 * c + 2, :].rearrange("p j n -> p (j n)")

            def layer_norm_dve(k, ctr, gname, bname):
                for c in range(QUADS):
                    dve.wait_ge(S[f"sdev_ready{k}"], c + 1)
                    link(nc.vector.reciprocal(two_of(rstd, c), two_of(sdev, c)))
                    link(nc.vector.tensor_tensor(two_of(lnn, c), bank[ctr + c][:, 0:2 * TOK], two_of(rstd, c), ALU.mult))
                    nc.vector.tensor_scalar(two_of(enc[k], c), two_of(lnn, c), col[gname], col[bname],
                                            ALU.mult, ALU.add).then_inc(S[f"enc_ready{k}"], 1)

            dve.wait_ge(S["ld_enc"], 16)
            for c in range(QUADS):
                dve.wait_ge(S["wo_done"], c + 1)
                nc.vector.scalar_tensor_tensor(two_of(z[0], c), bank[c][:, 0:2 * TOK], col["bo"], two_of(src, c),
                                               ALU.add, ALU.add).then_inc(S["z_ready0"], 1)
            layer_norm_dve(0, 4, "g1", "b1")
            dve.wait_ge(S["enc_ready0"], QUADS)
            for c in range(QUADS):
                dve.wait_ge(S["ff2_done"], c + 1)
                nc.vector.scalar_tensor_tensor(two_of(z[1], c), bank[4 + c][:, 0:2 * TOK], col["ffb2"],
                                               two_of(enc[0], c), ALU.add, ALU.add).then_inc(S["z_ready1"], 1)
            layer_norm_dve(1, 0, "g2", "b2")

            dve.wait_ge(S["tau_q"], 1)
            link(nc.vector.tensor_scalar(tv["q"][:, :], bank[4][:, 0:PAIRS], col["bq2"], None, ALU.add))
            head32 = col["head32"].unsqueeze(1).to_broadcast([P, PAIRS, 32])
            nc.vector.tensor_tensor(q2m[:, :, :], tv["q"][:, :].unsqueeze(2).to_broadcast([P, PAIRS, 32]), head32,
                                    ALU.mult).then_inc(S["tau_q_ready"], 1)
            dve.wait_ge(S["tau_u"], 1)
            nc.vector.tensor_copy(u2[:, :, :], bank[5][:, 0:256].rearrange("p (j r) -> p j r", r=32)).then_inc(S["tau_u_ready"], 1)
            dve.wait_ge(S["tau_s"], 1)
            link(nc.vector.tensor_reduce(mx2[:, 0, :], bank[6][:, 0:2 * TOK].rearrange("p (j n) -> p j n", j=2), AX_X,
                                         ALU.max, negate=True))
            nc.vector.tensor_scalar(mx2[:, 1, :], mx2[:, 0, :], scale_h, None, ALU.mult).then_inc(S["tau_m"], 1)
            dve.wait_ge(S["tau_e"], 1)
            link(nc.vector.reciprocal(mx2[:, 2, :], psm[:, :]))
            for jj in range(2):
                ins = nc.vector.tensor_scalar(prob[:, jj, :], prob[:, jj, :], mx2[:, 2, jj:jj + 1], None, ALU.mult)
            ins.then_inc(S["tau_p_ready"], 1)
            dve.wait_ge(S["pT_done"], 1)
            nc.vector.tensor_copy(PT[:, :, :], bank[7][:, 0:2 * P].rearrange("p (j n) -> p j n", j=2))
            nc.vector.tensor_copy(PTl[:, :, :],
                                  bank[4][0:LEFT, 0:2 * P].rearrange("p (j n) -> p j n", j=2)).then_inc(S["pT_ready"], 1)
            dve.wait_ge(S["tau_c"], 1)
            nc.vector.tensor_copy(c2[:, :, :], bank[5][:, 0:256].rearrange("p (j r) -> p j r", r=32)).then_inc(S["tau_c_ready"], 1)
            dve.wait_ge(S["tau_v"], 1)
            link(nc.vector.tensor_tensor(o2t[:, :, :], bank[6][:, 0:256].rearrange("p (j r) -> p j r", r=32), head32, ALU.mult))
            link(nc.vector.tensor_reduce(tv["o"][:, :], o2t[:, :, :], AX_X, ALU.add))
            nc.vector.tensor_scalar(tv["ob"][:, :], tv["o"][:, :], col["bv2"], None, ALU.add).then_inc(S["tau_o_ready"], 1)
            dve.wait_ge(S["tau_out"], 1)
            link(nc.vector.tensor_scalar(tv["t0"][:, :], bank[7][:, 0:PAIRS], col["bo2"], None, ALU.add))
            nc.vector.scalar_tensor_tensor(tv["abs"][:, :], tv["t0"][:, :], -1.0, tv["t0"][:, :], ALU.mult, ALU.max).then_inc(S["tau_abs"], 1)
            dve.wait_ge(S["tau_ln"], 1)
            link(nc.vector.scalar_tensor_tensor(tv["sp"][:, :], tv["t0"][:, :], 0.0, tv["ln"][:, :], ALU.max, ALU.add))
            link(nc.vector.tensor_scalar(tv["clip"][:, :], tv["sp"][:, :], 0.1, 0.01, ALU.mult, ALU.max))
            link(nc.vector.tensor_scalar(tv["tau"][:, :], tv["clip"][:, :], 1.0, None, ALU.min))
            was = "tau"
            for n in ("p2", "p4", "p8", "p16", "p32"):
                link(nc.vector.tensor_tensor(tv[n][:, :], tv[was][:, :], tv[was][:, :], ALU.mult))
                was = n
            link(nc.vector.tensor_scalar(tv["s1"][:, :], tv["tau"][:, :], 1.0, None, ALU.add))
            was = "s1"
            for n, p in (("s2", "p2"), ("s3", "p4"), ("s4", "p8"), ("s5", "p16")):
                link(nc.vector.scalar_tensor_tensor(tv[n][:, :], tv[p][:, :], 1.0, tv[was][:, :], ALU.add, ALU.mult))
                was = n
            nc.vector.reciprocal(tv["inv"][:, :], tv["s5"][:, :]).then_inc(S["inv_ready"], 1)
            link(nc.vector.tensor_scalar(tv["neg32"][:, :], tv["p32"][:, :], -1.0, None, ALU.mult))
            link(nc.vector.memset(y[:, :, 0:1], 0.0))
            for j in range(PAIRS):
                link(nc.vector.tensor_tensor_scan(y[:, j, 1:L + 1], tv["tau"][:, j:j + 1].to_broadcast([P, L]), xT[:, j, :],
                                                  0.0, ALU.mult, ALU.add))
                nc.vector.scalar_tensor_tensor(hraw[:, j, :], y[:, j, 0:LOUT], tv["neg32"][:, j:j + 1],
                                               y[:, j, WIN:WIN + LOUT], ALU.mult, ALU.add).then_inc(S["hraw_ready"], 1)

            def grouped(ap):
                return ap.rearrange("p (g d) -> p g d", d=D)

            def variance(k):
                for c in range(QUADS):
                    dve.wait_ge(S["asq_ready"], QUADS * k + c + 1)
                    ins = nc.vector.tensor_reduce(st[f"ss{k}"][:, 8 * c:8 * c + 8], grouped(asq[:, c, :]), AX_X, ALU.add)
                link(ins)
                nc.vector.tensor_scalar(st[f"var{k}"][:, :], st[f"ss{k}"][:, :], 1.0 / D, EPS, ALU.mult,
                                        ALU.add).then_inc(S["var_ready"], 1)

            def xn_of(c):
                return xn[:, c, :, :, :, :].rearrange("p a b s d -> p (a b s) d")

            def per_group(name, c):
                return st[name][:, 8 * c:8 * c + 8].unsqueeze(2).to_broadcast([CH, 8, D])

            variance(0)
            dve.wait_ge(S["rs_ready"], 1)
            for c in range(QUADS):
                nc.vector.tensor_tensor(xn_of(c), grouped(bank[c][0:CH, :]), per_group("rs0", c),
                                        ALU.mult).then_inc(S["xn_ready"], 1)
            nc.vector.tensor_copy(identb[:, :], ident).then_inc(S["identb_ready"], 1)

            def key_max(n):
                dve.wait_ge(S["kp_done"], n + 1)
                nc.vector.tensor_reduce(km[:, n, :], bank[n % 4][:, 0:2 * LOUT].rearrange("p (j n) -> p j n", j=2), AX_X,
                                        ALU.max, negate=True).then_inc(S["km_ready"], 1)

            def key_transposed(n):
                dve.wait_ge(S["et_done"], n + 1)
                nc.vector.tensor_copy(ETt[:, n, :, :, :].rearrange("p a b n -> p (a b n)"),
                                      bank[4 + n % 4][0:CH, :]).then_inc(S["ett_ready"], 1)

            for n in range(8):
                key_max(n)
                if n >= 3:
                    key_transposed(n - 3)
            for n in range(5, 8):
                key_transposed(n)
            dve.wait_ge(S["ld_att"], 16)
            link(nc.vector.reciprocal(rks[:, :, :], ksum[:, :, :]))
            for c in range(QUADS):
                dve.wait_ge(S["ctx_done"], c + 1)
                for jj in range(2):
                    for s in range(2):
                        a = 256 * jj + P * s
                        ins = nc.vector.scalar_tensor_tensor(cx[:, 2 * c + jj, s, :], bank[4 + c][:, a:a + P],
                                                             rks[:, 2 * c + s, jj:jj + 1], col["ctx_mask"],
                                                             ALU.mult, ALU.mult)
                ins.then_inc(S["ctx_ready"], 1)
            dve.wait_ge(S["mx_done"], 1)
            nc.vector.tensor_tensor(Mb[:, :, :, :],
                                    bank[0].rearrange("p (j o) -> p j o", o=D).unsqueeze(2).to_broadcast([P, PAIRS, 2, D]),
                                    col["mix_mask"].rearrange("p (s o) -> p s o", s=2).unsqueeze(1).to_broadcast([P, PAIRS, 2, D]),
                                    ALU.mult).then_inc(S["mix_ready"], 1)

            def h2_of(c):
                return h2[:, c, :, :, :, :].rearrange("p a b s d -> p (a b s) d")

            for c in range(QUADS):
                dve.wait_ge(S["h2_done"], c + 1)
                nc.vector.tensor_tensor(h2[:, c, :, :, :, :].rearrange("p a b s d -> p (a b) (s d)"),
                                        bank[4 + c][0:CH, :].rearrange("p (a n) -> p a n", n=P),
                                        col["bout_row"][0:CH, :].unsqueeze(1).to_broadcast([CH, 4, P]),
                                        ALU.add).then_inc(S["h2_ready"], 1)
            for c in range(QUADS):
                dve.wait_ge(S["h2_ready"], c + 1)
                ins = nc.vector.tensor_reduce(st["sum1"][:, 8 * c:8 * c + 8], h2_of(c), AX_X, ALU.add)
            link(ins)
            link(nc.vector.tensor_scalar(st["mean1"][:, :], st["sum1"][:, :], 1.0 / D, None, ALU.mult))
            for c in range(QUADS):
                nc.vector.tensor_tensor(xn_of(c), h2_of(c), per_group("mean1", c), ALU.subtract).then_inc(S["xc_ready"], 1)
            variance(1)
            dve.wait_ge(S["rs_ready"], 2)
            for c in range(QUADS):
                nc.vector.tensor_tensor(xn_of(c), xn_of(c), per_group("rs1", c), ALU.mult).then_inc(S["x2_ready"], 1)
            for c in range(QUADS):
                dve.wait_ge(S["a11_done"], c + 1)
                nc.vector.tensor_copy(xg[0:64, 4 * c + 1:4 * c + 4:2, :],
                                      bank[c][64:128, 0:2 * LOUT].rearrange("p (j n) -> p j n", j=2)).then_inc(S["xg_odd"], 1)

            rank = col["rank"][0:CH, :].rearrange("p (u e) -> p u e", e=E_N)

            def per_unit(ap):
                return ap[:, :].unsqueeze(2).to_broadcast([CH, 32, E_N])

            dve.wait_ge(S["gate_done"], 1)
            link(nc.vector.tensor_copy(tp["g"][:, :, :], bank[4][0:CH, 0:256].rearrange("p (u e) -> p u e", e=E_N)))
            for k, g in ((1, "g"), (2, "g2")):
                m, p, eq, rk, sel = tm[f"m{k}"], tm[f"p{k}"], tp[f"eq{k}"], tp[f"rk{k}"], tp[f"sel{k}"]
                link(nc.vector.tensor_reduce(m[:, :], tp[g][:, :, :], AX_X, ALU.max))
                link(nc.vector.tensor_tensor(eq[:, :, :], tp[g][:, :, :], per_unit(m), ALU.is_equal))
                link(nc.vector.tensor_tensor(rk[:, :, :], eq[:, :, :], rank, ALU.mult))
                link(nc.vector.tensor_reduce(p[:, :], rk[:, :, :], AX_X, ALU.max))
                link(nc.vector.tensor_tensor(sel[:, :, :], rk[:, :, :], per_unit(p), ALU.is_equal))
                if k == 1:
                    link(nc.vector.scalar_tensor_tensor(tp["g2"][:, :, :], sel[:, :, :], -3.0e38, tp["g"][:, :, :],
                                                        ALU.mult, ALU.add))
            link(nc.vector.tensor_tensor(nm[:, :, E_N:], tp["sel1"][:, :, :], tp["sel2"][:, :, :], ALU.add))
            nc.vector.tensor_scalar(nm[:, :, 0:E_N], nm[:, :, E_N:], -1.0, 1.0, ALU.mult, ALU.add).then_inc(S["nm_ready"], 1)
            for t in range(PAIRS):
                dve.wait_ge(S["mk_done"], t + 1)
                nc.vector.tensor_copy(xg[64:80, 2 * t:2 * t + 2, :],
                                      bank[4 + t % 2][64:80, 0:2 * LOUT].rearrange("p (j n) -> p j n", j=2)).then_inc(S["mk_ready"], 1)
            for t in range(PAIRS):
                dve.wait_ge(S["down_done"], t + 1)
                if t >= 2:
                    dve.wait_ge(S[f"out_stored{t % 2}"], 32 * (t // 2))
                nc.vector.tensor_tensor(osb[:, t % 2, :, :, :],
                                        bank[6 + t % 2][0:CH, 0:4 * D].rearrange("p (s c d) -> p s c d", s=2, c=2),
                                        h2[:, t // 2, t % 2, :, :, :].rearrange("p c s d -> p s c d"),
                                        ALU.add).then_inc(S["o_ready"], 1)

        @block.tensor
        def _(pe):
            mm, tr = nc.tensor.matmul, nc.tensor.transpose
            pe.wait_ge(S["ld_dft"], 16)
            for c in range(QUADS):
                if c % 2 == 0:
                    pe.wait_ge(S[f"ld_x{c // 2}"], 32)
                for jj in range(2):
                    j = 2 * c + jj
                    for t in range(2):
                        last = mm(bank[c][:, L * jj:L * jj + L], xl[:, t, P * j:P * j + P], dft[:, t, :],
                                  start=t == 0, stop=t == 1)
                last.then_inc(S["fft_done"], 1)
                for jj in range(2):
                    j = 2 * c + jj
                    for t in range(2):
                        last = tr(bank[4 + c][:, L * jj + P * t:L * jj + P * t + P], xl[:, t, P * j:P * j + P], ident)
                last.then_inc(S["xt_done"], 1)
            pe.wait_ge(S["ld_qkv"], 16)
            pe.wait_ge(S["sq_done"], QUADS)
            pe.wait_ge(S["xT_ready"], QUADS)
            for c in range(QUADS):
                pe.wait_ge(S["src_ready"], c + 1)
                pair2 = src[:, 2 * c:2 * c + 2, :]
                if c >= 2:
                    pe.wait_ge(S["qT_ready"], c - 1)
                mm(bank[c % 2][:, 0:2 * TOK], col["wq"], pair2, start=True, stop=True).then_inc(S["q_done"], 1)
                if c >= 2:
                    pe.wait_ge(S["kT_ready"], c - 1)
                mm(bank[2 + c % 2][:, 0:2 * TOK], col["wk"], pair2, start=True, stop=True).then_inc(S["k_done"], 1)
                if c >= 2:
                    pe.wait_ge(S["v_ready"], c - 1)
                for jj in range(2):
                    last = mm(bank[4 + c % 2][:, P * jj:P * jj + P], src[:, 2 * c + jj, 0:P], col["wv"],
                              start=True, stop=True)
                last.then_inc(S["v_done"], 1)
            pe.wait_ge(S["vleft_in_ready"], 1)
            for h in range(2):
                for q in range(HALF):
                    last = mm(bank[6 + h][32 * q:32 * q + 32, 0:D],
                              vleft_in[:, HALF * h + q, :, :].rearrange("p a t -> p (a t)"), col["wv_stack"],
                              start=True, stop=True)
                last.then_inc(S["vl_done"], 1)
            pe.wait_ge(S["qT_ready"], QUADS)
            pe.wait_ge(S["vl_ready"], 2)
            unit = 0
            for h in range(2):
                pe.wait_ge(S[f"strips{h}"], 16 * 4 * TERMS)
                for b in range(2 * HALF):
                    j, s = b // 2, b % 2
                    for n, hd0 in ((3, 0), (3, 3), (2, 6)):
                        if unit >= 2:
                            pe.wait_ge(S["max_ready"], unit - 1)
                        for a in range(n):
                            g, u = (hd0 + a) // 2, (hd0 + a) % 2
                            last = mm(bank[unit % 2][:, TOK * a:TOK * a + TOK], QS[h][:, u, s, g, TOK * j:TOK * j + P],
                                      KS[h][:, s, g, TOK * j:TOK * j + TOK], start=True, stop=True)
                        last.then_inc(S["s_done"], 1)
                        unit += 1
                pe.wait_ge(S["left_ready"], h + 1)
                for q in range(HALF):
                    last = mm(bank[6][32 * q:32 * q + 32, 0:TOK],
                              qleft[:, HALF * h + q, :, :].rearrange("p a t -> p (a t)"), KT[:, HALF * h + q, :],
                              start=True, stop=True)
                last.then_inc(S["sl_done"], 1)
                pe.wait_ge(S["max_ready"], unit)
                if h:
                    pe.wait_ge(S["mT_ready"], h)
                tr(bank[7][0:64, 0:P], mneg[:, h, :], ident)
                pe.wait_ge(S["mlneg_ready"], h + 1)
                for t in range(LEFT):
                    last = mm(bank[7][0:64, P + t:P + t + 1], sel_left[:, t, :], mlneg[:, h:h + 1], start=True, stop=True)
                last.then_inc(S["mt_done"], 1)
            pe.wait_ge(S["mT_ready"], 2)
            unit = 0

            def weighted_values(b):
                j, s, h = b // 2, b % 2, b // (2 * HALF)
                pe.wait_ge(S["exp_done"], 2 * b + 2)
                pe.wait_ge(S["vx_ready"], b + 1)
                pe.wait_ge(S["el_ready"], h + 1)
                if b >= 2:
                    pe.wait_ge(S["ot_ready"], b - 1)
                for hd in range(HEADS):
                    mm(bank[6 + b % 2][:, 0:TOK], Vx[:, b % 4, hd, :], ET[:, (2 * b + hd // 4) % 4, hd % 4, :],
                       start=hd == 0, stop=False)
                q = j % HALF
                mm(bank[6 + b % 2][:, 0:TOK], VL[32 * q:32 * q + 32, h, s, :], EL[32 * q:32 * q + 32, h, :],
                   start=False, stop=True).then_inc(S["pv_done"], 1)

            for h in range(2):
                if h:
                    weighted_values(2 * HALF - 1)
                    pe.wait_ge(S["ot_ready"], 2 * HALF - 1)
                for q in range(HALF):
                    mm(bank[6][32 * q:32 * q + 32, 0:TOK], kleft[:, HALF * h + q, :, :].rearrange("p a t -> p (a t)"),
                       QT[:, HALF * h + q, :], start=True, stop=False)
                    last = mm(bank[6][32 * q:32 * q + 32, 0:TOK], sel_pair[0:64, q, :], mT[:, h, :], start=False, stop=True)
                last.then_inc(S["kl_done"], 1)
                pe.wait_ge(S[f"shift{h}"], 16 * 12)
                for b in range(2 * HALF):
                    j, s = b // 2, b % 2
                    for pr in range(2):
                        if unit >= 2:
                            pe.wait_ge(S["exp_done"], unit - 1)
                        for a in range(4):
                            g, u = 2 * pr + a // 2, a % 2
                            last = mm(bank[2 + 2 * (unit % 2) + a // 2][:, TOK * u:TOK * u + TOK],
                                      KS[h][:, s, g, TOK * j:TOK * j + P],
                                      QS[h][:, u, s, g, TOK * j:TOK * j + TOK], start=True, stop=True)
                        last.then_inc(S["st_done"], 1)
                        unit += 1
                    if b >= 1:
                        weighted_values(2 * HALF * h + b - 1)
            weighted_values(B - 1)
            pe.wait_ge(S["exp_done"], 2 * B)
            pe.wait_ge(S["ld_enc"], 16)
            pe.wait_ge(S["ot_ready"], B)
            for c in range(QUADS):
                mm(bank[c][:, 0:2 * TOK], col["wo"], OT[:, 2 * c:2 * c + 2, :], start=True, stop=True).then_inc(S["wo_done"], 1)

            def layer_norm_pe(k, ctr, var):
                for c in range(QUADS):
                    pe.wait_ge(S[f"z_ready{k}"], c + 1)
                    mm(bank[ctr + c][:, 0:2 * TOK], col["center"], z[k][:, 2 * c:2 * c + 2, :],
                       start=True, stop=True).then_inc(S[f"ctr_done{k}"], 1)
                for c in range(QUADS):
                    pe.wait_ge(S[f"lsq_ready{k}"], c + 1)
                    mm(bank[var + c][:, 0:2 * TOK], col["mean"], lnsq[:, 2 * c:2 * c + 2, :],
                       start=True, stop=True).then_inc(S[f"var_done{k}"], 1)

            layer_norm_pe(0, 4, 0)
            pe.wait_ge(S["sdev_ready0"], QUADS)
            for c in range(QUADS):
                pe.wait_ge(S["enc_ready0"], c + 1)
                for q in range(4):
                    if c >= 1:
                        pe.wait_ge(S["relu_ready"], 4 * (c - 1) + q + 1)
                    mm(bank[q][:, 0:2 * TOK], ff1[:, q, :], enc[0][:, 2 * c:2 * c + 2, :],
                       start=True, stop=True).then_inc(S["ff1_done"], 1)
                for q in range(4):
                    pe.wait_ge(S["relu_ready"], 4 * c + q + 1)
                    last = mm(bank[4 + c][:, 0:2 * TOK], ff2[:, q, :], relu[:, c % 2, q, :], start=q == 0, stop=q == 3)
                last.then_inc(S["ff2_done"], 1)
            layer_norm_pe(1, 0, 4)

            pe.wait_ge(S["enc_ready1"], QUADS)
            for n in range(2):
                for jj in range(4):
                    tr(bank[n][:, P * jj:P * jj + P], enc[1][:, 4 * n + jj, 0:P], ident)
                    last = tr(bank[2 + n][0:LEFT, P * jj:P * jj + P], enc[1][:, 4 * n + jj, P:TOK], ident)
                last.then_inc(S["s2t_done"], 1)
            mm(bank[4][:, 0:PAIRS], col["wq2"], enc[1][:, :, P], start=True, stop=True).then_inc(S["tau_q"], 1)
            pe.wait_ge(S["tau_q_ready"], 1)
            mm(bank[5][:, 0:256], col["wk2"], q2m[:, :, :].rearrange("p j r -> p (j r)"),
               start=True, stop=True).then_inc(S["tau_u"], 1)
            pe.wait_ge(S["tau_u_ready"], 1)
            for j in range(PAIRS):
                a = TOK * (j // 4)
                last = mm(bank[6][32 * (j % 4):32 * (j % 4) + 32, a:a + TOK], u2[:, j, :], enc[1][:, j, :],
                          start=True, stop=True)
            last.then_inc(S["tau_s"], 1)
            pe.wait_ge(S["tau_p_ready"], 1)
            for jj in range(2):
                tr(bank[7][:, P * jj:P * jj + P], prob[:, jj, 0:P], ident)
                last = tr(bank[4][0:LEFT, P * jj:P * jj + P], prob[:, jj, P:TOK], ident)
            last.then_inc(S["pT_done"], 1)
            pe.wait_ge(S["pT_ready"], 1)
            pe.wait_ge(S["s2t_ready"], 2)
            for j in range(PAIRS):
                r = 32 * (j % 4)
                o = bank[5][:, 32 * j:32 * j + 32]
                mm(o, s2t[:, j, :], PT[:, j // 4, r:r + 32], start=True, stop=False)
                last = mm(o, s2l[:, j, :], PTl[:, j // 4, r:r + 32], start=False, stop=True)
            last.then_inc(S["tau_c"], 1)
            pe.wait_ge(S["tau_c_ready"], 1)
            mm(bank[6][:, 0:256], col["wv2"], c2[:, :, :].rearrange("p j r -> p (j r)"),
               start=True, stop=True).then_inc(S["tau_v"], 1)
            pe.wait_ge(S["tau_o_ready"], 1)
            mm(bank[7][:, 0:PAIRS], col["wo2"], tv["ob"][:, :], start=True, stop=True).then_inc(S["tau_out"], 1)

            for c in range(QUADS):
                pe.wait_ge(S["h_ready"], 2 * c + 2)
                for jj in range(2):
                    for t in range(2):
                        a = 256 * jj + P * t
                        last = mm(bank[c][0:CH, a:a + P], hT[:, 2 * c + jj, STEP * t:STEP * t + CH], col["center"],
                                  start=True, stop=True)
                last.then_inc(S["a1_done"], 1)

            def to_feature_major(bank0, ready, done):
                for c in range(QUADS):
                    pe.wait_ge(ready, c + 1)
                    for jj in range(2):
                        for t in range(2):
                            a = LOUT * jj + STEP * t
                            last = tr(bank[bank0 + c][:, a:a + CH], xn[:, c, jj, t, :, :].rearrange("p s d -> p (s d)"),
                                      ident[0:CH, 0:CH])
                    last.then_inc(done, 1)

            to_feature_major(4, S["xn_ready"], S["a2_done"])
            pe.wait_ge(S["ld_att"], 16)

            def exp_transposed(n):
                pe.wait_ge(S["ke_ready"], n + 1)
                if n >= 4:
                    pe.wait_ge(S["ett_ready"], n - 3)
                for jj in range(2):
                    for t in range(2):
                        a = 256 * jj + P * t
                        last = tr(bank[4 + n % 4][0:CH, a:a + P], E[:, n, jj, STEP * t:STEP * t + CH], ident)
                last.then_inc(S["et_done"], 1)

            for n in range(8):
                c, s = n // 2, n % 2
                pe.wait_ge(S["xnT_ready"], QUADS if n >= 1 else 1)
                if n >= 4:
                    pe.wait_ge(S["ke_ready"], n - 3)
                mm(bank[n % 4][:, 0:2 * LOUT], wk_att[:, s, :], xnT[:, 2 * c:2 * c + 2, :], start=True,
                   stop=True).then_inc(S["kp_done"], 1)
                if n >= 3:
                    exp_transposed(n - 3)
            for n in range(5, 8):
                exp_transposed(n)
            pe.wait_ge(S["ett_ready"], 8)
            for j in range(PAIRS):
                c, jj = j // 2, j % 2
                for s in range(2):
                    o = bank[j // 4][64 * s:64 * s + 64, P * (j % 4):P * (j % 4) + P]
                    mm(o, xn[0:STEP, c, jj, 0, s, :], ETt[0:STEP, 2 * c + s, jj, 0, :], start=True, stop=False)
                    last = mm(o, xn[:, c, jj, 1, s, :], ETt[:, 2 * c + s, jj, 1, :], start=False, stop=True)
                if j % 4 == 3:
                    last.then_inc(S["gt_done"], 1)
            for j in range(PAIRS):
                pe.wait_ge(S["gt_ready"], j // 4 + 1)
                last = mm(bank[4 + j // 2][:, 256 * (j % 2):256 * (j % 2) + 256], GT[:, j, :], col["wv_att"],
                          start=True, stop=True)
                if j % 2:
                    last.then_inc(S["ctx_done"], 1)
            for j in range(PAIRS):
                pe.wait_ge(S["ctx_ready"], j // 2 + 1)
                for s in range(2):
                    a = P * (j % 4) + D * s
                    last = mm(bank[2 + j // 4][:, a:a + D], cx[:, j, s, :], col["wqT"], start=True, stop=True)
                if j % 4 == 3:
                    last.then_inc(S["zz_done"], 1)
            for j in range(PAIRS):
                pe.wait_ge(S["zz_ready"], j // 4 + 1)
                last = mm(bank[0][:, D * j:D * j + D], Zs[:, j, :], col["wout"], start=True, stop=True)
            last.then_inc(S["mx_done"], 1)
            pe.wait_ge(S["mix_ready"], 1)
            for c in range(QUADS):
                for jj in range(2):
                    for t in range(2):
                        j, a = 2 * c + jj, 256 * jj + P * t
                        mm(bank[4 + c][0:CH, a:a + P], xnT[:, j, STEP * t:STEP * t + CH],
                           Mb[:, j, :, :].rearrange("p s o -> p (s o)"), start=True, stop=False)
                        last = mm(bank[4 + c][0:CH, a:a + P], hT[:, j, STEP * t:STEP * t + CH], ident,
                                  start=False, stop=True)
                last.then_inc(S["h2_done"], 1)
            to_feature_major(0, S["x2_ready"], S["a11_done"])
            pe.wait_ge(S["xg_even"], QUADS)
            pe.wait_ge(S["xg_odd"], QUADS)
            pe.wait_ge(S["xg_preset"], 1)
            for u in range(32):
                b, t = u // 2, u % 2
                last = mm(bank[4][0:CH, E_N * u:E_N * u + E_N], xg[:, b, STEP * t:STEP * t + CH], col["gate"],
                          start=True, stop=True)
            last.then_inc(S["gate_done"], 1)
            pe.wait_ge(S["nm_ready"], 1)
            for t in range(PAIRS):
                if t >= 2:
                    pe.wait_ge(S["mk_ready"], t - 1)
                for bb in range(2):
                    for ch in range(2):
                        a = LOUT * bb + STEP * ch
                        last = mm(bank[4 + t % 2][64:80, a:a + CH], nm[:, 4 * t + 2 * bb + ch, :], identb[0:CH, 0:CH],
                                  start=True, stop=True)
                last.then_inc(S["mk_done"], 1)
            pe.wait_ge(S["ld_ffn"], 16)
            unit = 0

            def down_tile(t):
                pe.wait_ge(S["gelu_done"], 4 * t + 4)
                if t >= 2:
                    pe.wait_ge(S["o_ready"], t - 1)
                for bb in range(2):
                    for ch in range(2):
                        o = bank[6 + t % 2][0:CH, D * (2 * bb + ch):D * (2 * bb + ch) + D]
                        for e in range(E_N):
                            a = LOUT * bb + STEP * ch
                            mm(o, hid[:, t % 2, e, a:a + CH], down[:, e, :], start=e == 0, stop=False)
                        last = mm(o, xg[:, 2 * t + bb, STEP * ch:STEP * ch + CH], col["b2rows"], start=False, stop=True)
                last.then_inc(S["down_done"], 1)

            for t in range(PAIRS):
                pe.wait_ge(S["mk_ready"], t + 1)
                for e in range(0, E_N, 2):
                    if unit >= 2:
                        pe.wait_ge(S["gelu_done"], unit - 1)
                    for k in range(2):
                        last = mm(bank[2 * (unit % 2) + k][:, 0:2 * LOUT], up[:, e + k, :], xg[:, 2 * t:2 * t + 2, :],
                                  start=True, stop=True)
                    last.then_inc(S["up_done"], 1)
                    unit += 1
                if t >= 1:
                    down_tile(t - 1)
            down_tile(PAIRS - 1)


def host_packs(w):
    f = np.float32

    def pair(m):
        o = np.zeros((P, 2 * m.shape[1]), f)
        o[:D, :m.shape[1]] = m
        o[D:, m.shape[1]:] = m
        return o

    def twice(v):
        return np.concatenate([v, v]).reshape(P, 1)

    def rows(v):
        return np.broadcast_to(v, (P, v.shape[0]))

    c = {}
    l = np.arange(L)[:, None].astype(np.float64)
    k = np.arange(NFREQ)[None, :]
    table = np.concatenate([np.cos(2 * np.pi * (l * k % L) / L), np.sin(2 * np.pi * (l * k % L) / L)], 1)
    table[:, NFREQ] = 1 - 2 * (l[:, 0] % 2)
    c["dft"] = table.astype(f).reshape(2, P, L).transpose(1, 0, 2).reshape(P, 2 * L)
    c["ident"] = np.eye(P, dtype=f)
    pos = np.arange(TOK)[:, None].astype(np.float64)
    div = np.exp(np.arange(0, D, 2) * (-np.log(10000.0) / D))
    pe = np.zeros((TOK, D), f)
    pe[:, 0::2] = np.sin(pos * div)
    pe[:, 1::2] = np.cos(pos * div)
    pe = np.concatenate([pe[1:], pe[:1]]).T
    c["posenc"] = np.concatenate([pe, pe])
    wi, bi = w["L0_tok_l_in_w"], w["L0_tok_l_in_b"]
    for n, name in enumerate("qkv"):
        c[f"w{name}"] = pair(wi[D * n:D * n + D].T)
    c["wv_stack"] = np.concatenate([wi[2 * D:].T] * 2)
    c["bq"], c["bk"] = twice(bi[:D]), twice(bi[D:2 * D])
    c["bv_row"] = rows(np.concatenate([bi[2 * D:]] * 2))
    p = np.arange(P)
    c["head16"] = (p[:, None] // DH == np.arange(16)[None]).astype(f)
    c["batch16"] = (p[:, None] // D == np.arange(16)[None] // HEADS).astype(f)
    ps, ph, pt, pj = p // 16 % 2, p // 2 % HEADS, p % 2, p // 32
    vm = np.zeros((P, 2, D), f)
    vc = np.zeros((P, 2, P), f)
    for s in range(2):
        own = (ps[:, None] == s) & (ph[:, None] == np.arange(D)[None] // DH)
        vm[:, s] = own
        vc[:, s, D * (1 - s):D * (1 - s) + D] = own
    c["vl_mask"], c["vl_const"] = vm.reshape(P, -1), vc.reshape(P, -1)
    m = np.arange(D)
    c["sel_left"] = np.stack([((p // 2)[:, None] == m[None]) & (pt[:, None] == t) for t in range(2)], 1).astype(f).reshape(P, -1)
    sp = np.zeros((P, HALF, 32), f)
    for j in range(HALF):
        sp[:D, j] = (m[:, None] // 16 == j) & (m[:, None] % 16 == np.arange(32)[None] // 2)
    c["sel_pair"] = sp.reshape(P, -1)

    c["wo"] = pair(w["L0_tok_l_out_w"].T)
    c["center"] = pair((np.eye(D) - 1.0 / D).astype(f))
    c["mean"] = pair(np.full((D, D), 1.0 / D, f))
    for n, name in (("bo", "l_out_b"), ("g1", "ln1_g"), ("b1", "ln1_b"), ("g2", "ln2_g"), ("b2", "ln2_b"), ("ffb2", "ff_b2"),
                    ("bo2", "m_out_b")):
        c[n] = twice(w["L0_tok_" + name])
    c["eps"] = np.full((P, 1), EPS, f)
    f1, f2 = np.zeros((P, 4, P), f), np.zeros((P, 4, P), f)
    for s in range(2):
        for k in range(2):
            f1[D * s:D * s + D, 2 * s + k] = w["L0_tok_ff_w1"][P * k:P * k + P].T
            f2[:, 2 * s + k, D * s:D * s + D] = w["L0_tok_ff_w2"][:, P * k:P * k + P].T
    c["ff1"], c["ff2"] = f1.reshape(P, -1), f2.reshape(P, -1)
    c["ffb1"] = w["L0_tok_ff_b1"].reshape(2, P).T
    wi, bi = w["L0_tok_m_in_w"], w["L0_tok_m_in_b"]
    c["wq2"], c["wk2"], c["wv2"] = pair(wi[:D].T), pair(wi[D:2 * D]), pair(wi[2 * D:].T)
    c["bq2"], c["bv2"] = twice(bi[:D]), twice(bi[2 * D:])
    c["head32"] = (p[:, None] // DH == np.arange(32)[None]).astype(f)
    c["wo2"] = pair(w["L0_tok_m_out_w"].T)

    wqkv, wout = w["L0_attn_W_qkv"], w["L0_attn_W_out"]
    c["wk_att"], c["wv_att"] = pair(wqkv[:, P:2 * P]), pair(wqkv[:, 2 * P:])
    c["ctx_mask"] = (p[:, None] // AD == p[None] // AD).astype(f)
    c["wqT"], c["wout"] = wqkv[:, :P].T, wout
    c["mix_mask"] = ((p[:, None] // D == p[None] // D) * AD ** -0.5).astype(f)
    c["bout_row"] = rows(np.concatenate([w["L0_attn_b_out"]] * 2))
    c["rank"] = rows((E_N - np.arange(2 * P) % E_N).astype(f))
    c["neghalf"] = np.full((P, 32), -0.5, f)
    c["gate"] = np.zeros((P, E_N), f)
    c["gate"][:D], c["gate"][ONE_ROW] = w["L0_ffn_Wg"], w["L0_ffn_bg"]
    c["b2rows"] = np.zeros((P, D), f)
    c["b2rows"][M_ROW:M_ROW + E_N] = w["L0_ffn_b2"]
    u = np.zeros((P, E_N, HID), f)
    u[:D] = w["L0_ffn_W1"].transpose(1, 0, 2)
    for e in range(E_N):
        u[N_ROW + e, e] = -BIG
    u[ONE_ROW] = w["L0_ffn_b1"]
    c["up"] = u.reshape(P, -1)
    c["down"] = w["L0_ffn_W2"].transpose(1, 0, 2).reshape(P, -1)
    return {k: np.ascontiguousarray(np.concatenate([c[n] for n, _ in v], 1), dtype=f) for k, v in PACKS.items()}


def kernel(**inputs):
    import concourse.bacc as bacc
    from concourse.bass_utils import run_bass_kernel_spmd

    w = {k: np.asarray(v) for k, v in inputs.items()}
    arrays = {"x_dram": np.ascontiguousarray(w["x"])}
    arrays.update({f"pack_{k}_dram": v for k, v in host_packs(w).items()})
    nc = bacc.Bacc("TRN2", target_bir_lowering=False, num_devices=1)
    aps = {k: nc.dram_tensor(k, v.shape, F32, kind="ExternalInput").ap() for k, v in arrays.items()}
    out = nc.dram_tensor("out_dram", (B, LOUT, D), F32, kind="ExternalOutput").ap()
    audio_tower(nc, aps["x_dram"], {k: aps[f"pack_{k}_dram"] for k in PACKS}, out)
    r = run_bass_kernel_spmd(nc, [arrays], core_ids=[0])
    return r.results[0]["out_dram"]
```

```python
from contextlib import ExitStack

import numpy as np
import concourse.bass as bass
from concourse import mybir

ACT = mybir.ActivationFunctionType
ALU = mybir.AluOpType
F32 = mybir.dt.float32
F16 = mybir.dt.float16
BF16 = mybir.dt.bfloat16
I32 = mybir.dt.int32
AX_X = mybir.AxisListType.X
RMAX = bass.bass_isa.ReduceOp.max

B, L, D = 16, 256, 64
P = 128
PAIRS = B // 2
HALF = PAIRS // 2
QUADS = PAIRS // 2
NFREQ = L // 2
TOK = NFREQ + 2
HEADS, DH = 8, 8
LEFT = TOK - P
WIN = 32
LOUT = L - WIN + 1
CH = 113
STEP = LOUT - CH
FF = 4 * D
AH, AD = 4, 32
E_N, HID = 8, 128
EPS = 1e-5
SX = 4096.0
MASK = 2.0 ** 15
CHOICE = 2.0 ** 14
PARTS = 3
EXPONENT = 0x7F800000
TERMS = 6
HPAIRS = 4
ARENA = 27480
Q_TERM = (0, 0, 1, 0, 1, 2)
K_TERM = (0, 1, 0, 2, 1, 0)
SHIFT_ROW = TERMS * DH
N_ROW, M_ROW = D, D + E_N

PACKS = {
    "dft": [("dft", 2 * L), ("ident", P)],
    "qkv": [("posenc", TOK), ("wq", P), ("wk", P), ("wv", P), ("wv_stack", D), ("bq", 1), ("bk", 1),
            ("bv_row", P), ("head16", 16), ("batch16", 16), ("vl_mask", 2 * D), ("vl_const", 2 * P),
            ("sel_left", 2 * D), ("sel_pair", P)],
    "enc": [("wo", P), ("center", P), ("mean", P), ("bo", 1), ("g1", 1), ("b1", 1), ("g2", 1), ("b2", 1),
            ("eps", 1), ("ff1", 4 * P), ("ffb1", 2), ("ff2", 4 * P), ("ffb2", 1),
            ("wq2", P), ("bq2", 1), ("wk2", P), ("head32", 32), ("wv2", P), ("bv2", 1), ("wo2", P), ("bo2", 1)],
    "att": [("wk_att", 2 * P), ("wv_att", 2 * P), ("ctx_mask", P), ("wqT", D), ("wout", D), ("mix_mask", P),
            ("bout_row", P), ("rank", 2 * P), ("gate", E_N), ("bg_row", E_N), ("b2rows", D), ("b2part", PARTS),
            ("eb1", E_N), ("mask_rows", E_N), ("eps_sx", 1)],
    "ffn": [("up", E_N * HID), ("down", E_N * D)],
}
WIDTH = {k: sum(w for _, w in v) for k, v in PACKS.items()}


def audio_tower(nc, x, packs, out):
    scr_qk = nc.dram_tensor("scr_qk", (2, 2 * 3, P, HALF * TOK), BF16, kind="Internal").ap()
    scr_m = nc.dram_tensor("scr_m", (2, 3, HALF * 16, TOK), BF16, kind="Internal").ap()

    with ExitStack() as ctx:
        def sb(name, shape, dt=F32):
            return ctx.enter_context(nc.sbuf_tensor(name, shape, dt))

        def sem(name):
            return ctx.enter_context(nc.semaphore(name))

        psum = ctx.enter_context(nc.psum_tensor("psum", [P, 8, 512], F32))
        bank = [psum[:, i, :] for i in range(8)]

        pk = {k: sb(f"pk_{k}", [P, w]) for k, w in WIDTH.items()}
        col = {}
        for k, cols in PACKS.items():
            at = 0
            for name, w in cols:
                col[name] = pk[k][:, at:at + w]
                at += w
        dft = col["dft"].rearrange("p (c n) -> p c n", c=2)
        ident = col["ident"]
        vl_mask = col["vl_mask"].rearrange("p (s d) -> p s d", s=2)
        sel_left = col["sel_left"].rearrange("p (t m) -> p t m", t=2)
        sel_pair = col["sel_pair"].rearrange("p (j m) -> p j m", j=HALF)
        ff1 = col["ff1"].rearrange("p (q n) -> p q n", q=4)
        ff2 = col["ff2"].rearrange("p (q n) -> p q n", q=4)
        wk_att = col["wk_att"].rearrange("p (s n) -> p s n", s=2)
        up = col["up"].rearrange("p (e n) -> p e n", e=E_N)
        down = col["down"].rearrange("p (e n) -> p e n", e=E_N)

        arena = sb("arena", [P, ARENA])
        used = {"encoder": 0, "middle": 0, "layers": 0}

        def shared(time, shape, dt=F32):
            n = int(np.prod(shape[1:])) * (1 if dt == F32 else 2) // (1 if dt == F32 else 4)
            a = used[time]
            used[time] += n
            assert used[time] <= ARENA
            v = arena[0:shape[0], a:a + n]
            v = v if dt == F32 else v.bitcast(dt)
            dims = " ".join(f"d{i}" for i in range(1, len(shape)))
            return v.rearrange(f"p ({dims}) -> p {dims}", **{f"d{i}": shape[i] for i in range(1, len(shape))})

        sq = sb("sq", [P, PAIRS, L])
        xT = sb("xT", [P, PAIRS, L])
        amp2 = sb("amp2", [P, PAIRS, NFREQ + 1])
        amp = amp2
        src = sb("src", [P, PAIRS, TOK])
        QT = shared("encoder", [P, PAIRS, TOK])
        KT = shared("encoder", [P, PAIRS, TOK])
        V = shared("encoder", [P, PAIRS, P])
        vleft_in = sb("vleft_in", [P, PAIRS, 16, LEFT])
        vl_tmp = sb("vl_tmp", [P, 2, D])
        VL = sb("VL", [P, 2, 2, P])
        resid = shared("encoder", [P, 2, HALF * TOK])
        qk3 = [shared("encoder", [P, 6, HALF * TOK], BF16) for h in range(2)]
        QS32 = [shared("encoder", [P, 8 * HALF * TOK]) for h in range(2)]
        QS = [q[:, :].bitcast(BF16).rearrange("p (u s g n) -> p u s g n", u=2, s=2, g=4) for q in QS32]
        KS = [shared("encoder", [P, 2, 4, HALF * TOK], BF16) for h in range(2)]
        qleft = shared("encoder", [P, PAIRS, 16, LEFT])
        kleft = shared("encoder", [P, PAIRS, 16, LEFT])
        mneg = sb("mneg", [P, 2, HALF * 16])
        mlneg = sb("mlneg", [P, 2])
        mT = sb("mT", [HALF * 16, 2, TOK])
        mres = sb("mres", [HALF * 16, 2, 2, TOK])
        m3 = sb("m3", [HALF * 16, 2, 3, TOK], BF16)
        EL = sb("EL", [P, 2, TOK])
        ET = shared("encoder", [P, 4, 4, TOK])
        xl = ET.rearrange("p a b n -> p (a b n)")[:, 0:2 * B * D].rearrange("p (c n) -> p c n", c=2)
        Vx = shared("encoder", [P, 4, HEADS, P])
        rden = sb("rden", [P, 2, TOK])
        OT = sb("OT", [P, PAIRS, TOK])
        z = [shared("middle", [P, PAIRS, TOK]) for k in range(2)]
        lnsq = shared("middle", [P, PAIRS, TOK])
        sdev = shared("middle", [P, PAIRS, TOK])
        rstd = shared("middle", [P, PAIRS, TOK])
        lnn = shared("middle", [P, PAIRS, TOK])
        enc = [sb(f"enc{k}", [P, PAIRS, TOK]) for k in range(2)]
        relu = shared("middle", [P, 2, 4, 2 * TOK])
        y = shared("middle", [P, PAIRS, L + 1])
        hraw = sq[:, :, 0:LOUT]
        hT = sb("hT", [P, PAIRS, LOUT])

        s2t = shared("middle", [P, PAIRS, P])
        s2l = sb("s2l", [LEFT, PAIRS, P])
        tv = {n: sb(f"tau_{n}", [P, PAIRS]) for n in ("q", "o", "ob", "t0", "abs", "exp", "ln", "sp", "clip", "tau", "p2",
                                                      "p4", "p8", "p16", "p32", "neg32", "s1", "s2", "s3", "s4", "s5",
                                                      "inv")}
        q2m = sb("q2m", [P, PAIRS, 32])
        u2 = sb("u2", [P, PAIRS, 32])
        c2 = sb("c2", [P, PAIRS, 32])
        o2t = sb("o2t", [P, PAIRS, 32])
        mx2 = sb("mx2", [P, 3, 2])
        psm = sb("psm", [P, 2])
        prob = sb("prob", [P, 2, TOK])
        PT = sb("PT", [P, 2, P])
        PTl = sb("PTl", [LEFT, 2, P])
        asq = shared("layers", [CH, QUADS, 512])
        xn = shared("layers", [CH, QUADS, 2, 2, 2, D])
        xnT = shared("layers", [P, PAIRS, LOUT])
        st = {n: sb(f"st_{n}", [CH, 32]) for n in ("ss0", "var0", "rs0", "sum1", "mean1", "ss1", "var1", "rs1")}
        km = sb("km", [P, 8, 2])
        ksum = sb("ksum", [P, 8, 2])
        rks = sb("rks", [P, 8, 2])
        E = shared("layers", [P, 8, 2, LOUT])
        ETt = shared("layers", [CH, 8, 2, 2, P])
        n_hid = 2 * E_N * 2 * LOUT
        hid = arena[:, 0:n_hid].rearrange("p (a e n) -> p a e n", a=2, e=E_N)
        hparts = arena[:, n_hid:2 * n_hid].bitcast(F16).rearrange("p (a k e n) -> p a k e n", a=2, k=2, e=E_N)
        GT = shared("layers", [P, PAIRS, P])
        cx = shared("layers", [P, PAIRS, 2, P])
        Zs = shared("layers", [P, PAIRS, P])
        Mb = shared("layers", [P, PAIRS, 2, D])
        h2 = shared("layers", [CH, QUADS, 2, 2, 2, D])
        xparts = asq[:, :, :].rearrange("p c n -> p (c n)").bitcast(F16).rearrange(
            "p (c a b s k d) -> p c a b s k d", c=QUADS, a=2, b=2, s=2, k=2)
        xa = shared("layers", [P, B, LOUT], F16)
        xb = shared("layers", [P, B, LOUT], F16)
        tp = {n: shared("layers", [CH, 32, E_N]) for n in ("g", "eq1", "rk1", "sel1", "g2", "eq2", "rk2", "sel2")}
        tm = {n: sb(f"topm_{n}", [CH, 32]) for n in ("m1", "p1", "m2", "p2")}
        nm = sb("nm", [CH, 32, 4 * E_N], F16)
        identh = sb("identh", [P, P], F16)
        wmax = sb("wmax", [P, 2, 5])
        scale = sb("scale", [P, 4, 4])
        up_ab = amp2[:, :, :].rearrange("p j n -> p (j n)")[:, 0:E_N * HID].bitcast(F16).rearrange(
            "p (k e n) -> p k e n", k=2, e=E_N)
        up_a, up_b = up_ab[:, 0], up_ab[:, 1]
        down2 = col["dft"].bitcast(F16).rearrange("p (e k d) -> p e k d", e=E_N, k=2)
        gate2 = sb("gate2", [P, 2, E_N], F16)
        bg2 = sb("bg2", [P, E_N])
        b2s = vleft_in[:, :, :, :].rearrange("p j a t -> p (j a t)")[:, 0:3 * D].rearrange("p (k d) -> p k d", k=3)
        b2p = sb("b2p", [P, PARTS, D], F16)
        b2r = sb("b2r", [P, D], F16)
        ob = shared("layers", [CH, 2, 2, 2, D])
        osb = shared("layers", [CH, 2, 2, 2, D])

        both = scale[:, 2, :]
        s_hid, s_up, s_gate, s_down = (scale[:, 1, n:n + 1] for n in range(4))
        inv_up, inv_down = scale[:, 3, 0:1], scale[:, 3, 1:2]
        step_sems = {e: sem(f"{e}_step") for e in ("dve", "pool")}
        names = ("ld_dft ld_x0 ld_x1 ld_qkv ld_enc ld_att ld_ffn qs_zero ks_one fft_done xt_done sq_done xT_ready "
                 "amp2_ready amp_ready src_ready q_done k_done v_done vl_done qT_ready kT_ready v_ready vl_ready "
                 "vleft_in_ready split_ready qk_stored strips0 strips1 left_ready s_done max_ready sl_done "
                 "mlneg_ready mt_done mT_ready m3_ready m_stored shift0 shift1 kl_done el_ready st_done exp_done "
                 "vx_ready pv_done ot_ready wo_done z_ready0 z_ready1 ctr_done0 ctr_done1 lsq_ready0 lsq_ready1 "
                 "var_done0 var_done1 sdev_ready0 sdev_ready1 enc_ready0 enc_ready1 ff1_done relu_ready ff2_done "
                 "tau_q tau_q_ready tau_u tau_u_ready tau_s tau_m tau_e tau_p_ready s2t_done s2t_ready pT_done "
                 "pT_ready tau_c tau_c_ready tau_v tau_o_ready tau_out tau_abs tau_exp tau_ln inv_ready hraw_ready "
                 "h_ready xb_preset identh_ready a1_done asq_ready var_ready rs_ready xn_ready a2_done xnT_ready "
                 "kp_done km_ready ke_ready et_done ett_ready gt_done gt_ready ctx_done ctx_ready zz_done zz_ready "
                 "mx_done mix_ready h2_done h2_ready xc_ready x2_ready xhi_ready xlo_ready a11_done xa_ready xb_ready gate_done nm_ready "
                 "wmax_ready wred_ready wsplit_ready hi_dve hi_act lo_ready sd_ready "
                 "mk_done mk_ready up_done gelu_done down_done o_ready out_stored0 out_stored1").split()
        S = {n: sem(n) for n in names}

        block = ctx.enter_context(nc.Block())
        scale_h = 1.0 / float(np.sqrt(np.float32(DH)))

        @block.sync
        def _(sp):
            xs = x.rearrange("b (c l) d -> l c b d", c=2)
            xd = xl[:, :, :].rearrange("p c (b d) -> p c b d", b=B)
            for h in range(2):
                for c in range(2):
                    sp.dma_start(xd[:, c, 8 * h:8 * h + 8, :], xs[:, c, 8 * h:8 * h + 8, :]).then_inc(S[f"ld_x{h}"], 16)
            for h in range(2):
                sp.wait_ge(S["split_ready"], h + 1)
                sp.dma_start(scr_qk[h].rearrange("t p n -> p t n"), qk3[h][:, :, :]).then_inc(S["qk_stored"], 16)
                sp.wait_ge(S["qs_zero"], h + 1)
                sp.wait_ge(S["ks_one"], h + 1)
                sp.wait_ge(S["qk_stored"], 16 * (h + 1))
                for t in range(TERMS):
                    qsrc = scr_qk[h, Q_TERM[t]].rearrange("(s g u i) n -> u i (s g) n", s=2, g=4, u=2)
                    ksrc = scr_qk[h, 3 + K_TERM[t]].rearrange("(s g u i) n -> u i (s g) n", s=2, g=4, u=2)
                    for u in range(2):
                        r = 64 * u + DH * t
                        sp.dma_start(QS[h][r:r + DH, u, :, :, :].rearrange("p s g n -> p (s g) n"), qsrc[u]).then_inc(S[f"strips{h}"], 16)
                        sp.dma_start(KS[h][r:r + DH, :, :, :].rearrange("p s g n -> p (s g) n"), ksrc[u]).then_inc(S[f"strips{h}"], 16)
            for h in range(2):
                sp.wait_ge(S["m3_ready"], h + 1)
                sp.dma_start(scr_m[h].rearrange("k r n -> r k n"), m3[:, h, :, :]).then_inc(S["m_stored"], 16)
                sp.wait_ge(S["m_stored"], 16 * (h + 1))
                for k in range(3):
                    msrc = scr_m[h, k].rearrange("(j s g u) n -> u s g j n", j=HALF, s=2, g=4)
                    for u in range(2):
                        r = 64 * u + SHIFT_ROW + k
                        for s in range(2):
                            dst = QS[h][r:r + 1, u, s, :, :].rearrange("p g (j n) -> p g j n", j=HALF)
                            sp.dma_start(dst, msrc[u, s].unsqueeze(0)).then_inc(S[f"shift{h}"], 16)
            for t in range(PAIRS):
                sp.wait_ge(S["o_ready"], t + 1)
                for c in range(2):
                    n = STEP + c
                    sp.dma_start(out[2 * t:2 * t + 2, STEP * c:STEP * c + n, :].rearrange("s l d -> l s d"),
                                 osb[0:n, t % 2, :, c, :]).then_inc(S[f"out_stored{t % 2}"], 16)
            for k in range(2):
                sp.wait_ge(S[f"out_stored{k}"], 16 * PAIRS)

        @block.gpsimd
        def _(pool):
            for h in range(2):
                nc.gpsimd.memset(QS32[h][:, :], 0.0).then_inc(S["qs_zero"], 1)
                nc.gpsimd.memset(KS[h][:, :, :, :], 1.0).then_inc(S["ks_one"], 1)
            nc.gpsimd.memset(Vx[:, :, :, :], 0.0).then_inc(step_sems["pool"], 1)
            pool.wait_ge(step_sems["pool"], 1)
            for slot in range(4):
                for hd in range(HEADS):
                    c0 = 64 * (1 - slot % 2) + DH * hd
                    last = nc.gpsimd.memset(Vx[:, slot, hd, c0:c0 + DH], 1.0)
            last.then_inc(step_sems["pool"], 1)
            pool.wait_ge(step_sems["pool"], 2)
            for b in range(B):
                j, s = b // 2, b % 2
                pool.wait_ge(S["v_ready"], j // 2 + 1)
                if b >= 4:
                    pool.wait_ge(S["pv_done"], b - 3)
                for hd in range(HEADS):
                    c0 = 64 * s + DH * hd
                    last = nc.gpsimd.tensor_copy(Vx[:, b % 4, hd, c0:c0 + DH],
                                                 V[:, j, 64 * s + DH * hd:64 * s + DH * hd + DH])
                last.then_inc(S["vx_ready"], 1)
                if b == 3:
                    pool.wait_ge(S["wmax_ready"], 1)
                    nc.gpsimd.partition_all_reduce(wmax[:, 1, :], wmax[:, 0, :], P, RMAX).then_inc(S["wred_ready"], 1)
            pool.wait_ge(S["rs_ready"], 1)
            nc.gpsimd.memset(xb[96:128, :, :], 0.0).then_inc(S["xb_preset"], 1)

        @block.scalar
        def _(act):
            for k in PACKS:
                act.dma_start(pk[k][:, :], packs[k]).then_inc(S[f"ld_{k}"], 16)
            for c in range(QUADS):
                act.wait_ge(S["fft_done"], c + 1)
                nc.scalar.activation(sq[:, 2 * c:2 * c + 2, :], bank[c][:, :].rearrange("p (j n) -> p j n", j=2),
                                     ACT.Square).then_inc(S["sq_done"], 1)
            for c in range(QUADS):
                act.wait_ge(S["amp2_ready"], c + 1)
                nc.scalar.activation(amp[:, 2 * c:2 * c + 2, :], amp2[:, 2 * c:2 * c + 2, :],
                                     ACT.Sqrt).then_inc(S["amp_ready"], 1)
            act.wait_ge(S["ld_qkv"], 16)
            for c in range(QUADS):
                for (w, T, b) in (("q", QT, "bq"), ("k", KT, "bk")):
                    act.wait_ge(S[f"{w}_done"], c + 1)
                    ps = bank[(0 if w == "q" else 2) + c % 2][:, 0:2 * TOK].rearrange("p (j n) -> p j n", j=2)
                    nc.scalar.activation(T[:, 2 * c:2 * c + 2, :], ps, ACT.Identity,
                                         bias=col[b]).then_inc(S[f"{w}T_ready"], 1)
            unit = 0
            for h in range(2):
                act.wait_ge(S["kl_done"], h + 1)
                nc.scalar.activation(EL[:, h, :], bank[6][:, 0:TOK], ACT.Exp, scale=scale_h).then_inc(S["el_ready"], 1)
                for _b in range(2 * HALF):
                    for _u in range(2):
                        act.wait_ge(S["st_done"], unit + 1)
                        if unit >= 4:
                            act.wait_ge(S["pv_done"], unit // 2 - 1)
                        k0 = 2 + 2 * (unit % 2)
                        nc.scalar.activation(ET[:, unit % 4, :, :].rearrange("p (k u) n -> p k (u n)", k=2),
                                             psum[:, k0:k0 + 2, 0:2 * TOK], ACT.Exp,
                                             scale=scale_h).then_inc(S["exp_done"], 1)
                        unit += 1

            def layer_norm_act(k, ctr, var):
                for c in range(QUADS):
                    act.wait_ge(S[f"ctr_done{k}"], c + 1)
                    nc.scalar.activation(lnsq[:, 2 * c:2 * c + 2, :],
                                         bank[ctr + c][:, 0:2 * TOK].rearrange("p (j n) -> p j n", j=2),
                                         ACT.Square).then_inc(S[f"lsq_ready{k}"], 1)
                for c in range(QUADS):
                    act.wait_ge(S[f"var_done{k}"], c + 1)
                    nc.scalar.activation(sdev[:, 2 * c:2 * c + 2, :],
                                         bank[var + c][:, 0:2 * TOK].rearrange("p (j n) -> p j n", j=2),
                                         ACT.Sqrt, bias=col["eps"]).then_inc(S[f"sdev_ready{k}"], 1)

            act.wait_ge(S["ld_enc"], 16)
            layer_norm_act(0, 4, 0)
            for c in range(QUADS):
                for q in range(4):
                    act.wait_ge(S["ff1_done"], 4 * c + q + 1)
                    if c >= 2:
                        act.wait_ge(S["ff2_done"], c - 1)
                    nc.scalar.activation(relu[:, c % 2, q, :], bank[q][:, 0:2 * TOK], ACT.Relu,
                                         bias=col["ffb1"][:, q % 2:q % 2 + 1]).then_inc(S["relu_ready"], 1)
            layer_norm_act(1, 0, 4)
            for n in range(2):
                act.wait_ge(S["s2t_done"], n + 1)
                nc.scalar.copy(s2t[:, 4 * n:4 * n + 4, :], bank[n].rearrange("p (j n) -> p j n", j=4))
                nc.scalar.copy(s2l[:, 4 * n:4 * n + 4, :],
                               bank[2 + n][0:LEFT, :].rearrange("p (j n) -> p j n", j=4)).then_inc(S["s2t_ready"], 1)
            act.wait_ge(S["tau_m"], 1)
            for jj in range(2):
                ins = nc.scalar.activation(prob[:, jj, :], bank[6][:, TOK * jj:TOK * jj + TOK], ACT.Exp,
                                           bias=mx2[:, 1, jj:jj + 1], scale=scale_h, accum_out=psm[:, jj:jj + 1])
            ins.then_inc(S["tau_e"], 1)
            act.wait_ge(S["tau_abs"], 1)
            nc.scalar.activation(tv["exp"][:, :], tv["abs"][:, :], ACT.Exp, scale=-1.0).then_inc(S["tau_exp"], 1)
            act.wait_ge(S["tau_exp"], 1)
            nc.scalar.activation(tv["ln"][:, :], tv["exp"][:, :], ACT.Ln, bias=1.0).then_inc(S["tau_ln"], 1)
            act.wait_ge(S["inv_ready"], 1)
            for j in range(PAIRS):
                act.wait_ge(S["hraw_ready"], j + 1)
                nc.scalar.activation(hT[:, j, :], hraw[:, j, :], ACT.Identity,
                                     scale=tv["inv"][:, j:j + 1]).then_inc(S["h_ready"], 1)
            for c in range(QUADS):
                act.wait_ge(S["a1_done"], c + 1)
                nc.scalar.activation(asq[:, c, :], bank[c][0:CH, :], ACT.Square).then_inc(S["asq_ready"], 1)

            def deviation(k, eps):
                act.wait_ge(S["var_ready"], k + 1)
                nc.scalar.activation(st[f"var{k}"][:, :], st[f"ss{k}"][:, :], ACT.Sqrt, bias=eps[0:CH, :],
                                     scale=1.0 / D if k == 0 else 1.0 / (D * SX * SX)).then_inc(S["sd_ready"], 1)

            act.wait_ge(S["ld_att"], 16)
            deviation(0, col["eps"])
            for c in range(QUADS):
                act.wait_ge(S["a2_done"], c + 1)
                nc.scalar.copy(xnT[:, 2 * c:2 * c + 2, :],
                               bank[4 + c][:, 0:2 * LOUT].rearrange("p (j n) -> p j n", j=2)).then_inc(S["xnT_ready"], 1)
            for n in range(8):
                act.wait_ge(S["km_ready"], n + 1)
                for jj in range(2):
                    ins = nc.scalar.activation(E[:, n, jj, :], bank[n % 4][:, LOUT * jj:LOUT * jj + LOUT], ACT.Exp,
                                               bias=km[:, n, jj:jj + 1], accum_out=ksum[:, n, jj:jj + 1])
                ins.then_inc(S["ke_ready"], 1)
            for n in range(2):
                act.wait_ge(S["gt_done"], n + 1)
                nc.scalar.copy(GT[:, 4 * n:4 * n + 4, :], bank[n].rearrange("p (j n) -> p j n", j=4)).then_inc(S["gt_ready"], 1)
            for n in range(2):
                act.wait_ge(S["zz_done"], n + 1)
                nc.scalar.copy(Zs[:, 4 * n:4 * n + 4, :], bank[2 + n].rearrange("p (j n) -> p j n", j=4)).then_inc(S["zz_ready"], 1)
            for c in range(QUADS):
                act.wait_ge(S["xc_ready"], c + 1)
                nc.scalar.activation(asq[:, c, :], xn[:, c, :, :, :, :].rearrange("p a b s d -> p (a b s d)"),
                                     ACT.Square).then_inc(S["asq_ready"], 1)
            deviation(1, col["eps_sx"])
            for c in range(QUADS):
                act.wait_ge(S["x2_ready"], c + 1)
                nc.scalar.copy(xparts[:, c, :, :, :, 0, :].rearrange("p a b s d -> p (a b s) d"),
                               xn[:, c, :, :, :, :].rearrange("p a b s d -> p (a b s) d")).then_inc(S["xhi_ready"], 1)
            for t in range(PAIRS):
                act.wait_ge(S["a11_done"], t + 1)
                nc.scalar.copy(xa[:, 2 * t:2 * t + 2, :],
                               bank[t][:, 0:2 * LOUT].rearrange("p (j n) -> p j n", j=2)).then_inc(S["xa_ready"], 1)
            act.wait_ge(S["wsplit_ready"], 1)
            for t in range(PAIRS):
                if t >= 2:
                    act.wait_ge(S["lo_ready"], HPAIRS * (t - 1))
                for e in range(E_N):
                    act.wait_ge(S["up_done"], E_N * t + e + 1)
                    nc.scalar.activation(hid[:, t % 2, e, :], bank[e % 4][:, 0:2 * LOUT], ACT.Gelu,
                                         bias=col["eb1"][:, e:e + 1], scale=inv_up).then_inc(S["gelu_done"], 1)
                act.wait_ge(S["gelu_done"], E_N * (t + 1))
                if t >= 2:
                    act.wait_ge(S["down_done"], t - 1)
                nc.scalar.activation(hparts[:, t % 2, 0, E_N - 2:, :], hid[:, t % 2, E_N - 2:, :], ACT.Copy,
                                     scale=s_hid).then_inc(S["hi_act"], 1)

        @block.vector
        def _(dve):
            chain = [0]

            def link(ins):
                chain[0] += 1
                ins.then_inc(step_sems["dve"], 1)
                dve.wait_ge(step_sems["dve"], chain[0])

            for c in range(QUADS):
                dve.wait_ge(S["xt_done"], c + 1)
                nc.vector.tensor_copy(xT[:, 2 * c:2 * c + 2, :],
                                      bank[4 + c][:, :].rearrange("p (j n) -> p j n", j=2)).then_inc(S["xT_ready"], 1)
            for c in range(QUADS):
                dve.wait_ge(S["sq_done"], c + 1)
                two = slice(2 * c, 2 * c + 2)
                nc.vector.tensor_tensor(amp2[:, two, 1:NFREQ], sq[:, two, 1:NFREQ], sq[:, two, NFREQ + 1:L], ALU.add)
                nc.vector.tensor_copy(amp2[:, two, 0:NFREQ + 1:NFREQ],
                                      sq[:, two, 0:NFREQ + 1:NFREQ]).then_inc(S["amp2_ready"], 1)
            dve.wait_ge(S["ld_qkv"], 16)
            dve.wait_ge(S["xT_ready"], QUADS)
            for c in range(QUADS):
                dve.wait_ge(S["amp_ready"], c + 1)
                two = slice(2 * c, 2 * c + 2)
                pe = col["posenc"].unsqueeze(1)
                nc.vector.tensor_tensor(src[:, two, 0:NFREQ + 1], amp[:, two, :],
                                        pe[:, :, 0:NFREQ + 1].to_broadcast([P, 2, NFREQ + 1]), ALU.add)
                nc.vector.tensor_tensor(src[:, two, TOK - 1:TOK], xT[:, two, L - 1:L],
                                        pe[:, :, TOK - 1:TOK].to_broadcast([P, 2, 1]), ALU.add).then_inc(S["src_ready"], 1)
            head16 = col["head16"].unsqueeze(2).to_broadcast([P, 16, LEFT])
            batch16 = col["batch16"].unsqueeze(2).to_broadcast([P, 16, LEFT])
            nc.vector.tensor_copy(VL[:, :, :, :].rearrange("p h s n -> p h (s n)"),
                                  col["vl_const"].unsqueeze(1).to_broadcast([P, 2, 2 * P]))
            dve.wait_ge(S["src_ready"], QUADS)
            for j in range(PAIRS):
                ins = nc.vector.tensor_tensor(vleft_in[:, j, :, :], src[:, j, P:TOK].unsqueeze(1).to_broadcast([P, 16, LEFT]),
                                              batch16, ALU.mult)
            ins.then_inc(S["vleft_in_ready"], 1)
            bv2 = col["bv_row"].unsqueeze(1).to_broadcast([P, 2, P])
            for h in range(2):
                for c in range(2 * h, 2 * h + 2):
                    dve.wait_ge(S["v_done"], c + 1)
                    nc.vector.tensor_tensor(V[:, 2 * c:2 * c + 2, :],
                                            bank[4 + c % 2][:, 0:2 * P].rearrange("p (j n) -> p j n", j=2),
                                            bv2, ALU.add).then_inc(S["v_ready"], 1)
                dve.wait_ge(S["vl_done"], h + 1)
                link(nc.vector.tensor_tensor(vl_tmp[:, h, :], bank[6 + h][:, 0:D], col["bv_row"][:, 0:D], ALU.add))
                for s in range(2):
                    ins = nc.vector.tensor_tensor(VL[:, h, s, 64 * s:64 * s + 64], vl_tmp[:, h, :], vl_mask[:, s, :], ALU.mult)
                ins.then_inc(S["vl_ready"], 1)
                four = slice(HALF * h, HALF * h + HALF)
                dve.wait_ge(S["qT_ready"], 2 * h + 2)
                dve.wait_ge(S["kT_ready"], 2 * h + 2)
                for n, T in enumerate((QT, KT)):
                    full = T[:, four, :].rearrange("p j n -> p (j n)")
                    link(nc.vector.tensor_copy(qk3[h][:, 3 * n, :], full))
                    link(nc.vector.tensor_tensor(resid[:, n, :], full, qk3[h][:, 3 * n, :], ALU.subtract))
                    link(nc.vector.tensor_copy(qk3[h][:, 3 * n + 1, :], resid[:, n, :]))
                    ins = nc.vector.tensor_tensor(qk3[h][:, 3 * n + 2, :], resid[:, n, :], qk3[h][:, 3 * n + 1, :],
                                                  ALU.subtract)
                    if n == 0:
                        link(ins)
                ins.then_inc(S["split_ready"], 1)
                for j in range(HALF * h, HALF * h + HALF):
                    nc.vector.tensor_tensor(qleft[:, j, :, :], QT[:, j, P:TOK].unsqueeze(1).to_broadcast([P, 16, LEFT]),
                                            head16, ALU.mult)
                    ins = nc.vector.tensor_tensor(kleft[:, j, :, :], KT[:, j, P:TOK].unsqueeze(1).to_broadcast([P, 16, LEFT]),
                                                  head16, ALU.mult)
                ins.then_inc(S["left_ready"], 1)
            dve.wait_ge(S["ld_att"], 16)
            dve.wait_ge(S["ld_ffn"], 16)
            for n, name in enumerate(("up", "eb1", "down", "gate", "b2rows")):
                ins = nc.vector.tensor_reduce(wmax[:, 0, n:n + 1], col[name], AX_X, ALU.max, apply_absolute_value=True)
            ins.then_inc(S["wmax_ready"], 1)
            unit = 0
            for h in range(2):
                for b in range(2 * HALF):
                    for n, hd0 in ((3, 0), (3, 3), (2, 6)):
                        dve.wait_ge(S["s_done"], unit + 1)
                        nc.vector.tensor_reduce(mneg[:, h, 8 * b + hd0:8 * b + hd0 + n],
                                                bank[unit % 2][:, 0:n * TOK].rearrange("p (a n) -> p a n", a=n),
                                                AX_X, ALU.max, negate=True).then_inc(S["max_ready"], 1)
                        unit += 1
                dve.wait_ge(S["sl_done"], h + 1)
                nc.vector.tensor_reduce(mlneg[:, h:h + 1], bank[6][:, 0:TOK], AX_X, ALU.max,
                                        negate=True).then_inc(S["mlneg_ready"], 1)
                dve.wait_ge(S["mt_done"], h + 1)
                nc.vector.tensor_copy(mT[:, h, :], bank[7][0:64, 0:TOK]).then_inc(S["mT_ready"], 1)
                dve.wait_ge(S["mT_ready"], h + 1)
                link(nc.vector.tensor_copy(m3[:, h, 0, :], mT[:, h, :]))
                link(nc.vector.tensor_tensor(mres[:, h, 0, :], mT[:, h, :], m3[:, h, 0, :], ALU.subtract))
                link(nc.vector.tensor_copy(m3[:, h, 1, :], mres[:, h, 0, :]))
                nc.vector.tensor_tensor(m3[:, h, 2, :], mres[:, h, 0, :], m3[:, h, 1, :],
                                        ALU.subtract).then_inc(S["m3_ready"], 1)
            dve.wait_ge(S["wred_ready"], 1)
            top = [wmax[:, 1, n:n + 1] for n in range(5)]
            den, pw = scale[:, 0, :], scale[:, 1, :]
            link(nc.vector.tensor_scalar(wmax[:, 1, :], wmax[:, 1, :], 1e-6, None, ALU.max))
            link(nc.vector.scalar_tensor_tensor(den[:, 0:1], top[0], float(D), top[1], ALU.mult, ALU.add))
            link(nc.vector.tensor_scalar(den[:, 0:1], den[:, 0:1], 2.0 ** -15, None, ALU.mult))
            link(nc.vector.tensor_scalar(den[:, 1:2], top[1], 16.0, 2.0 ** -17, ALU.add, ALU.mult))
            link(nc.vector.scalar_tensor_tensor(den[:, 1:2], top[0], 2.0 ** -10, den[:, 1:2], ALU.mult, ALU.max))
            link(nc.vector.tensor_scalar(den[:, 2:3], top[3], 2.0 ** -10, None, ALU.mult))
            link(nc.vector.reciprocal(pw[:, 0:3], den[:, 0:3]))
            link(nc.vector.tensor_scalar(pw[:, 0:3].bitcast(I32), pw[:, 0:3].bitcast(I32), EXPONENT, None, ALU.bitwise_and))
            link(nc.vector.tensor_tensor(den[:, 3:4], top[4], s_hid, ALU.mult))
            link(nc.vector.tensor_scalar(den[:, 3:4], den[:, 3:4], CHOICE ** -2, None, ALU.mult))
            link(nc.vector.scalar_tensor_tensor(den[:, 3:4], top[2], 2.0 ** -14, den[:, 3:4], ALU.mult, ALU.max))
            link(nc.vector.reciprocal(pw[:, 3:4], den[:, 3:4]))
            link(nc.vector.tensor_scalar(pw[:, 3:4].bitcast(I32), pw[:, 3:4].bitcast(I32), EXPONENT, None, ALU.bitwise_and))
            link(nc.vector.tensor_scalar(both[:, 0:1], s_up, SX, None, ALU.mult))
            link(nc.vector.tensor_tensor(both[:, 1:2], s_hid, s_down, ALU.mult))
            link(nc.vector.tensor_scalar(both[:, 2:3], both[:, 1:2], 1.0 / CHOICE, None, ALU.mult))
            link(nc.vector.tensor_scalar(both[:, 3:4], s_gate, SX, None, ALU.mult))
            nc.vector.reciprocal(scale[:, 3, 0:2], both[:, 0:2])
            nc.vector.tensor_scalar(up_a[:, :, :], up, s_up, None, ALU.mult)
            nc.vector.tensor_scalar(down2[:, :, 0, :], down, s_down, None, ALU.mult)
            nc.vector.tensor_scalar(gate2[:, 0, :], col["gate"], s_gate, None, ALU.mult)
            nc.vector.tensor_scalar(bg2[:, :], col["bg_row"], both[:, 3:4], None, ALU.mult)
            nc.vector.tensor_copy(up_b[64:128, :, :], col["mask_rows"][64:128, :].unsqueeze(2).to_broadcast([64, E_N, HID]))
            link(nc.vector.tensor_scalar(b2s[:, 0, :], col["b2rows"], both[:, 2:3], None, ALU.mult))
            nc.vector.scalar_tensor_tensor(up_b[0:64, :, :], up[0:64, :, :], s_up[0:64, :], up_a[0:64, :, :],
                                           ALU.mult, ALU.subtract)
            nc.vector.scalar_tensor_tensor(down2[:, :, 1, :], down, s_down, down2[:, :, 0, :], ALU.mult, ALU.subtract)
            nc.vector.scalar_tensor_tensor(gate2[:, 1, :], col["gate"], s_gate, gate2[:, 0, :], ALU.mult, ALU.subtract)
            for k in range(PARTS):
                link(nc.vector.tensor_copy(b2p[:, k, :], b2s[:, k, :]))
                if k < PARTS - 1:
                    link(nc.vector.tensor_tensor(b2s[:, k + 1, :], b2s[:, k, :], b2p[:, k, :], ALU.subtract))
            link(nc.vector.tensor_scalar(b2s[:, 0, :], b2p[:, 0, :], col["b2part"][:, 0:1], None, ALU.mult))
            link(nc.vector.scalar_tensor_tensor(b2s[:, 1, :], b2p[:, 1, :], col["b2part"][:, 1:2], b2s[:, 0, :],
                                                ALU.mult, ALU.add))
            nc.vector.scalar_tensor_tensor(b2r[:, :], b2p[:, 2, :], col["b2part"][:, 2:3], b2s[:, 1, :],
                                           ALU.mult, ALU.add).then_inc(S["wsplit_ready"], 1)
            for b in range(B):
                j, s = b // 2, b % 2
                mine, other = slice(64 * s, 64 * s + 64), slice(64 * (1 - s), 64 * (1 - s) + 64)
                dve.wait_ge(S["pv_done"], b + 1)
                link(nc.vector.reciprocal(rden[mine, b % 2, :], bank[6 + b % 2][other, 0:TOK]))
                nc.vector.tensor_tensor(OT[mine, j, :], bank[6 + b % 2][mine, 0:TOK], rden[mine, b % 2, :],
                                        ALU.mult).then_inc(S["ot_ready"], 1)

            def two_of(ap, c):
                return ap[:, 2 * c:2 * c + 2, :].rearrange("p j n -> p (j n)")

            def layer_norm_dve(k, ctr, gname, bname):
                for c in range(QUADS):
                    dve.wait_ge(S[f"sdev_ready{k}"], c + 1)
                    link(nc.vector.reciprocal(two_of(rstd, c), two_of(sdev, c)))
                    link(nc.vector.tensor_tensor(two_of(lnn, c), bank[ctr + c][:, 0:2 * TOK], two_of(rstd, c), ALU.mult))
                    nc.vector.tensor_scalar(two_of(enc[k], c), two_of(lnn, c), col[gname], col[bname],
                                            ALU.mult, ALU.add).then_inc(S[f"enc_ready{k}"], 1)

            dve.wait_ge(S["ld_enc"], 16)
            for c in range(QUADS):
                dve.wait_ge(S["wo_done"], c + 1)
                nc.vector.scalar_tensor_tensor(two_of(z[0], c), bank[c][:, 0:2 * TOK], col["bo"], two_of(src, c),
                                               ALU.add, ALU.add).then_inc(S["z_ready0"], 1)
            layer_norm_dve(0, 4, "g1", "b1")
            dve.wait_ge(S["enc_ready0"], QUADS)
            for c in range(QUADS):
                dve.wait_ge(S["ff2_done"], c + 1)
                nc.vector.scalar_tensor_tensor(two_of(z[1], c), bank[4 + c][:, 0:2 * TOK], col["ffb2"],
                                               two_of(enc[0], c), ALU.add, ALU.add).then_inc(S["z_ready1"], 1)
            layer_norm_dve(1, 0, "g2", "b2")

            dve.wait_ge(S["tau_q"], 1)
            link(nc.vector.tensor_scalar(tv["q"][:, :], bank[4][:, 0:PAIRS], col["bq2"], None, ALU.add))
            head32 = col["head32"].unsqueeze(1).to_broadcast([P, PAIRS, 32])
            nc.vector.tensor_tensor(q2m[:, :, :], tv["q"][:, :].unsqueeze(2).to_broadcast([P, PAIRS, 32]), head32,
                                    ALU.mult).then_inc(S["tau_q_ready"], 1)
            dve.wait_ge(S["tau_u"], 1)
            nc.vector.tensor_copy(u2[:, :, :], bank[5][:, 0:256].rearrange("p (j r) -> p j r", r=32)).then_inc(S["tau_u_ready"], 1)
            dve.wait_ge(S["tau_s"], 1)
            link(nc.vector.tensor_reduce(mx2[:, 0, :], bank[6][:, 0:2 * TOK].rearrange("p (j n) -> p j n", j=2), AX_X,
                                         ALU.max, negate=True))
            nc.vector.tensor_scalar(mx2[:, 1, :], mx2[:, 0, :], scale_h, None, ALU.mult).then_inc(S["tau_m"], 1)
            dve.wait_ge(S["tau_e"], 1)
            link(nc.vector.reciprocal(mx2[:, 2, :], psm[:, :]))
            for jj in range(2):
                ins = nc.vector.tensor_scalar(prob[:, jj, :], prob[:, jj, :], mx2[:, 2, jj:jj + 1], None, ALU.mult)
            ins.then_inc(S["tau_p_ready"], 1)
            dve.wait_ge(S["pT_done"], 1)
            nc.vector.tensor_copy(PT[:, :, :], bank[7][:, 0:2 * P].rearrange("p (j n) -> p j n", j=2))
            nc.vector.tensor_copy(PTl[:, :, :],
                                  bank[4][0:LEFT, 0:2 * P].rearrange("p (j n) -> p j n", j=2)).then_inc(S["pT_ready"], 1)
            dve.wait_ge(S["tau_c"], 1)
            nc.vector.tensor_copy(c2[:, :, :], bank[5][:, 0:256].rearrange("p (j r) -> p j r", r=32)).then_inc(S["tau_c_ready"], 1)
            dve.wait_ge(S["tau_v"], 1)
            link(nc.vector.tensor_tensor(o2t[:, :, :], bank[6][:, 0:256].rearrange("p (j r) -> p j r", r=32), head32, ALU.mult))
            link(nc.vector.tensor_reduce(tv["o"][:, :], o2t[:, :, :], AX_X, ALU.add))
            nc.vector.tensor_scalar(tv["ob"][:, :], tv["o"][:, :], col["bv2"], None, ALU.add).then_inc(S["tau_o_ready"], 1)
            dve.wait_ge(S["tau_out"], 1)
            link(nc.vector.tensor_scalar(tv["t0"][:, :], bank[7][:, 0:PAIRS], col["bo2"], None, ALU.add))
            nc.vector.scalar_tensor_tensor(tv["abs"][:, :], tv["t0"][:, :], -1.0, tv["t0"][:, :], ALU.mult, ALU.max).then_inc(S["tau_abs"], 1)
            dve.wait_ge(S["tau_ln"], 1)
            link(nc.vector.scalar_tensor_tensor(tv["sp"][:, :], tv["t0"][:, :], 0.0, tv["ln"][:, :], ALU.max, ALU.add))
            link(nc.vector.tensor_scalar(tv["clip"][:, :], tv["sp"][:, :], 0.1, 0.01, ALU.mult, ALU.max))
            link(nc.vector.tensor_scalar(tv["tau"][:, :], tv["clip"][:, :], 1.0, None, ALU.min))
            was = "tau"
            for n in ("p2", "p4", "p8", "p16", "p32"):
                link(nc.vector.tensor_tensor(tv[n][:, :], tv[was][:, :], tv[was][:, :], ALU.mult))
                was = n
            link(nc.vector.tensor_scalar(tv["s1"][:, :], tv["tau"][:, :], 1.0, None, ALU.add))
            was = "s1"
            for n, p in (("s2", "p2"), ("s3", "p4"), ("s4", "p8"), ("s5", "p16")):
                link(nc.vector.scalar_tensor_tensor(tv[n][:, :], tv[p][:, :], 1.0, tv[was][:, :], ALU.add, ALU.mult))
                was = n
            nc.vector.reciprocal(tv["inv"][:, :], tv["s5"][:, :]).then_inc(S["inv_ready"], 1)
            link(nc.vector.tensor_scalar(tv["neg32"][:, :], tv["p32"][:, :], -1.0, None, ALU.mult))
            link(nc.vector.memset(y[:, :, 0:1], 0.0))
            for j in range(PAIRS):
                link(nc.vector.tensor_tensor_scan(y[:, j, 1:L + 1], tv["tau"][:, j:j + 1].to_broadcast([P, L]), xT[:, j, :],
                                                  0.0, ALU.mult, ALU.add))
                nc.vector.scalar_tensor_tensor(hraw[:, j, :], y[:, j, 0:LOUT], tv["neg32"][:, j:j + 1],
                                               y[:, j, WIN:WIN + LOUT], ALU.mult, ALU.add).then_inc(S["hraw_ready"], 1)

            def grouped(ap):
                return ap.rearrange("p (g d) -> p g d", d=D)

            def variance(k):
                for c in range(QUADS):
                    dve.wait_ge(S["asq_ready"], QUADS * k + c + 1)
                    ins = nc.vector.tensor_reduce(st[f"ss{k}"][:, 8 * c:8 * c + 8], grouped(asq[:, c, :]), AX_X, ALU.add)
                ins.then_inc(S["var_ready"], 1)
                dve.wait_ge(S["sd_ready"], k + 1)
                nc.vector.reciprocal(st[f"rs{k}"][:, :], st[f"var{k}"][:, :]).then_inc(S["rs_ready"], 1)

            def xn_of(c):
                return xn[:, c, :, :, :, :].rearrange("p a b s d -> p (a b s) d")

            def per_group(name, c):
                return st[name][:, 8 * c:8 * c + 8].unsqueeze(2).to_broadcast([CH, 8, D])

            variance(0)
            dve.wait_ge(S["rs_ready"], 1)
            for c in range(QUADS):
                nc.vector.tensor_tensor(xn_of(c), grouped(bank[c][0:CH, :]), per_group("rs0", c),
                                        ALU.mult).then_inc(S["xn_ready"], 1)
            nc.vector.tensor_copy(identh[:, :], ident).then_inc(S["identh_ready"], 1)

            def key_max(n):
                dve.wait_ge(S["kp_done"], n + 1)
                nc.vector.tensor_reduce(km[:, n, :], bank[n % 4][:, 0:2 * LOUT].rearrange("p (j n) -> p j n", j=2), AX_X,
                                        ALU.max, negate=True).then_inc(S["km_ready"], 1)

            def key_transposed(n):
                dve.wait_ge(S["et_done"], n + 1)
                nc.vector.tensor_copy(ETt[:, n, :, :, :].rearrange("p a b n -> p (a b n)"),
                                      bank[4 + n % 4][0:CH, :]).then_inc(S["ett_ready"], 1)

            for n in range(8):
                key_max(n)
                if n >= 3:
                    key_transposed(n - 3)
            for n in range(5, 8):
                key_transposed(n)
            dve.wait_ge(S["ld_att"], 16)
            link(nc.vector.reciprocal(rks[:, :, :], ksum[:, :, :]))
            for c in range(QUADS):
                dve.wait_ge(S["ctx_done"], c + 1)
                for jj in range(2):
                    for s in range(2):
                        a = 256 * jj + P * s
                        ins = nc.vector.scalar_tensor_tensor(cx[:, 2 * c + jj, s, :], bank[4 + c][:, a:a + P],
                                                             rks[:, 2 * c + s, jj:jj + 1], col["ctx_mask"],
                                                             ALU.mult, ALU.mult)
                ins.then_inc(S["ctx_ready"], 1)
            dve.wait_ge(S["mx_done"], 1)
            nc.vector.tensor_tensor(Mb[:, :, :, :],
                                    bank[0].rearrange("p (j o) -> p j o", o=D).unsqueeze(2).to_broadcast([P, PAIRS, 2, D]),
                                    col["mix_mask"].rearrange("p (s o) -> p s o", s=2).unsqueeze(1).to_broadcast([P, PAIRS, 2, D]),
                                    ALU.mult).then_inc(S["mix_ready"], 1)

            def h2_of(c):
                return h2[:, c, :, :, :, :].rearrange("p a b s d -> p (a b s) d")

            for c in range(QUADS):
                dve.wait_ge(S["h2_done"], c + 1)
                nc.vector.tensor_tensor(h2[:, c, :, :, :, :].rearrange("p a b s d -> p (a b) (s d)"),
                                        bank[4 + c][0:CH, :].rearrange("p (a n) -> p a n", n=P),
                                        col["bout_row"][0:CH, :].unsqueeze(1).to_broadcast([CH, 4, P]),
                                        ALU.add).then_inc(S["h2_ready"], 1)
            for c in range(QUADS):
                dve.wait_ge(S["h2_ready"], c + 1)
                ins = nc.vector.tensor_reduce(st["sum1"][:, 8 * c:8 * c + 8], h2_of(c), AX_X, ALU.add)
            link(ins)
            link(nc.vector.tensor_scalar(st["mean1"][:, :], st["sum1"][:, :], 1.0 / D, None, ALU.mult))
            for c in range(QUADS):
                nc.vector.tensor_tensor(xn_of(c), h2_of(c), per_group("mean1", c), ALU.subtract).then_inc(S["xc_ready"], 1)
            variance(1)
            dve.wait_ge(S["rs_ready"], 2)
            for c in range(QUADS):
                nc.vector.tensor_tensor(xn_of(c), xn_of(c), per_group("rs1", c), ALU.mult).then_inc(S["x2_ready"], 1)
            for c in range(QUADS):
                dve.wait_ge(S["xhi_ready"], c + 1)
                nc.vector.tensor_tensor(xparts[:, c, :, :, :, 1, :].rearrange("p a b s d -> p (a b s) d"), xn_of(c),
                                        xparts[:, c, :, :, :, 0, :].rearrange("p a b s d -> p (a b s) d"),
                                        ALU.subtract).then_inc(S["xlo_ready"], 1)
            for t in range(PAIRS):
                dve.wait_ge(S["xa_ready"], t + 1)
                nc.vector.tensor_copy(xb[0:64, 2 * t:2 * t + 2, :], xa[0:64, 2 * t:2 * t + 2, :]).then_inc(S["xb_ready"], 1)

            rank = col["rank"][0:CH, :].rearrange("p (u e) -> p u e", e=E_N)

            def per_unit(ap):
                return ap[:, :].unsqueeze(2).to_broadcast([CH, 32, E_N])

            dve.wait_ge(S["gate_done"], 1)
            scores = bank[0][0:CH, :].rearrange("p (u k e) -> p u k e", k=2, e=E_N)
            link(nc.vector.tensor_tensor(tp["g"][:, :, :], scores[:, :, 1, :],
                                         bg2[0:CH, :].unsqueeze(1).to_broadcast([CH, 32, E_N]), ALU.add))
            link(nc.vector.tensor_tensor(tp["g"][:, :, :], scores[:, :, 0, :], tp["g"][:, :, :], ALU.add))
            for k, g in ((1, "g"), (2, "g2")):
                m, p, eq, rk, sel = tm[f"m{k}"], tm[f"p{k}"], tp[f"eq{k}"], tp[f"rk{k}"], tp[f"sel{k}"]
                link(nc.vector.tensor_reduce(m[:, :], tp[g][:, :, :], AX_X, ALU.max))
                link(nc.vector.tensor_tensor(eq[:, :, :], tp[g][:, :, :], per_unit(m), ALU.is_equal))
                link(nc.vector.tensor_tensor(rk[:, :, :], eq[:, :, :], rank, ALU.mult))
                link(nc.vector.tensor_reduce(p[:, :], rk[:, :, :], AX_X, ALU.max))
                link(nc.vector.tensor_tensor(sel[:, :, :], rk[:, :, :], per_unit(p), ALU.is_equal))
                if k == 1:
                    link(nc.vector.scalar_tensor_tensor(tp["g2"][:, :, :], sel[:, :, :], -3.0e38, tp["g"][:, :, :],
                                                        ALU.mult, ALU.add))
            link(nc.vector.tensor_tensor(tp["eq1"][:, :, :], tp["sel1"][:, :, :], tp["sel2"][:, :, :], ALU.add))
            nc.vector.tensor_scalar(nm[:, :, E_N:].rearrange("p u (k e) -> p u k e", e=E_N),
                                    tp["eq1"][:, :, :].unsqueeze(2).to_broadcast([CH, 32, PARTS, E_N]), CHOICE, None, ALU.mult)
            nc.vector.tensor_scalar(nm[:, :, 0:E_N], tp["eq1"][:, :, :], -MASK, MASK, ALU.mult,
                                    ALU.add).then_inc(S["nm_ready"], 1)
            for t in range(PAIRS):
                dve.wait_ge(S["mk_done"], t + 1)
                nc.vector.tensor_copy(xb[64:96, 2 * t:2 * t + 2, :],
                                      bank[4 + t % 2][64:96, 0:2 * LOUT].rearrange("p (j n) -> p j n", j=2)).then_inc(S["mk_ready"], 1)

            def output_tile(t):
                dve.wait_ge(S["down_done"], t + 1)
                if t >= 2:
                    dve.wait_ge(S[f"out_stored{t % 2}"], 32 * (t // 2))
                y4 = bank[6 + t % 2][0:CH, :].rearrange("p (s c k d) -> p s c k d", s=2, c=2, k=2)
                for bb in range(2):
                    ins = nc.vector.scalar_tensor_tensor(ob[:, t % 2, bb, :, :], y4[:, bb, :, 1, :], inv_down[0:CH, :],
                                                         h2[:, t // 2, t % 2, :, bb, :], ALU.mult, ALU.add)
                link(ins)
                nc.vector.scalar_tensor_tensor(osb[:, t % 2, :, :, :], y4[:, :, :, 0, :], inv_down[0:CH, :],
                                               ob[:, t % 2, :, :, :], ALU.mult, ALU.add).then_inc(S["o_ready"], 1)

            def second_part(t, g, firsts):
                if firsts:
                    dve.wait_ge(S["hi_dve"], firsts)
                two = slice(2 * g, 2 * g + 2)
                nc.vector.scalar_tensor_tensor(hparts[:, t % 2, 1, two, :], hid[:, t % 2, two, :], s_hid,
                                               hparts[:, t % 2, 0, two, :], ALU.mult,
                                               ALU.subtract).then_inc(S["lo_ready"], 1)

            firsts = 0
            for t in range(PAIRS):
                if t >= 2:
                    dve.wait_ge(S["down_done"], t - 1)
                for g in range(HPAIRS - 1):
                    dve.wait_ge(S["gelu_done"], E_N * t + 2 * g + 2)
                    two = slice(2 * g, 2 * g + 2)
                    nc.vector.tensor_scalar(hparts[:, t % 2, 0, two, :], hid[:, t % 2, two, :], s_hid, None,
                                            ALU.mult).then_inc(S["hi_dve"], 1)
                    firsts += 1
                    if g:
                        second_part(t, g - 1, firsts - 1)
                second_part(t, HPAIRS - 2, firsts)
                dve.wait_ge(S["hi_act"], t + 1)
                second_part(t, HPAIRS - 1, 0)
                if t:
                    output_tile(t - 1)
            output_tile(PAIRS - 1)

        @block.tensor
        def _(pe):
            mm, tr = nc.tensor.matmul, nc.tensor.transpose
            pe.wait_ge(S["ld_dft"], 16)
            for c in range(QUADS):
                if c % 2 == 0:
                    pe.wait_ge(S[f"ld_x{c // 2}"], 32)
                for jj in range(2):
                    j = 2 * c + jj
                    for t in range(2):
                        last = mm(bank[c][:, L * jj:L * jj + L], xl[:, t, P * j:P * j + P], dft[:, t, :],
                                  start=t == 0, stop=t == 1)
                last.then_inc(S["fft_done"], 1)
                for jj in range(2):
                    j = 2 * c + jj
                    for t in range(2):
                        last = tr(bank[4 + c][:, L * jj + P * t:L * jj + P * t + P], xl[:, t, P * j:P * j + P], ident)
                last.then_inc(S["xt_done"], 1)
            pe.wait_ge(S["ld_qkv"], 16)
            pe.wait_ge(S["sq_done"], QUADS)
            pe.wait_ge(S["xT_ready"], QUADS)
            for c in range(QUADS):
                pe.wait_ge(S["src_ready"], c + 1)
                pair2 = src[:, 2 * c:2 * c + 2, :]
                if c >= 2:
                    pe.wait_ge(S["qT_ready"], c - 1)
                mm(bank[c % 2][:, 0:2 * TOK], col["wq"], pair2, start=True, stop=True).then_inc(S["q_done"], 1)
                if c >= 2:
                    pe.wait_ge(S["kT_ready"], c - 1)
                mm(bank[2 + c % 2][:, 0:2 * TOK], col["wk"], pair2, start=True, stop=True).then_inc(S["k_done"], 1)
                if c >= 2:
                    pe.wait_ge(S["v_ready"], c - 1)
                for jj in range(2):
                    last = mm(bank[4 + c % 2][:, P * jj:P * jj + P], src[:, 2 * c + jj, 0:P], col["wv"],
                              start=True, stop=True)
                last.then_inc(S["v_done"], 1)
            pe.wait_ge(S["vleft_in_ready"], 1)
            for h in range(2):
                for q in range(HALF):
                    last = mm(bank[6 + h][32 * q:32 * q + 32, 0:D],
                              vleft_in[:, HALF * h + q, :, :].rearrange("p a t -> p (a t)"), col["wv_stack"],
                              start=True, stop=True)
                last.then_inc(S["vl_done"], 1)
            pe.wait_ge(S["qT_ready"], QUADS)
            pe.wait_ge(S["vl_ready"], 2)
            unit = 0
            for h in range(2):
                pe.wait_ge(S[f"strips{h}"], 16 * 4 * TERMS)
                for b in range(2 * HALF):
                    j, s = b // 2, b % 2
                    for n, hd0 in ((3, 0), (3, 3), (2, 6)):
                        if unit >= 2:
                            pe.wait_ge(S["max_ready"], unit - 1)
                        for a in range(n):
                            g, u = (hd0 + a) // 2, (hd0 + a) % 2
                            last = mm(bank[unit % 2][:, TOK * a:TOK * a + TOK], QS[h][:, u, s, g, TOK * j:TOK * j + P],
                                      KS[h][:, s, g, TOK * j:TOK * j + TOK], start=True, stop=True)
                        last.then_inc(S["s_done"], 1)
                        unit += 1
                pe.wait_ge(S["left_ready"], h + 1)
                for q in range(HALF):
                    last = mm(bank[6][32 * q:32 * q + 32, 0:TOK],
                              qleft[:, HALF * h + q, :, :].rearrange("p a t -> p (a t)"), KT[:, HALF * h + q, :],
                              start=True, stop=True)
                last.then_inc(S["sl_done"], 1)
                pe.wait_ge(S["max_ready"], unit)
                if h:
                    pe.wait_ge(S["mT_ready"], h)
                tr(bank[7][0:64, 0:P], mneg[:, h, :], ident)
                pe.wait_ge(S["mlneg_ready"], h + 1)
                for t in range(LEFT):
                    last = mm(bank[7][0:64, P + t:P + t + 1], sel_left[:, t, :], mlneg[:, h:h + 1], start=True, stop=True)
                last.then_inc(S["mt_done"], 1)
            pe.wait_ge(S["mT_ready"], 2)
            unit = 0

            def weighted_values(b):
                j, s, h = b // 2, b % 2, b // (2 * HALF)
                pe.wait_ge(S["exp_done"], 2 * b + 2)
                pe.wait_ge(S["vx_ready"], b + 1)
                pe.wait_ge(S["el_ready"], h + 1)
                if b >= 2:
                    pe.wait_ge(S["ot_ready"], b - 1)
                for hd in range(HEADS):
                    mm(bank[6 + b % 2][:, 0:TOK], Vx[:, b % 4, hd, :], ET[:, (2 * b + hd // 4) % 4, hd % 4, :],
                       start=hd == 0, stop=False)
                q = j % HALF
                mm(bank[6 + b % 2][:, 0:TOK], VL[32 * q:32 * q + 32, h, s, :], EL[32 * q:32 * q + 32, h, :],
                   start=False, stop=True).then_inc(S["pv_done"], 1)

            for h in range(2):
                if h:
                    weighted_values(2 * HALF - 1)
                    pe.wait_ge(S["ot_ready"], 2 * HALF - 1)
                for q in range(HALF):
                    mm(bank[6][32 * q:32 * q + 32, 0:TOK], kleft[:, HALF * h + q, :, :].rearrange("p a t -> p (a t)"),
                       QT[:, HALF * h + q, :], start=True, stop=False)
                    last = mm(bank[6][32 * q:32 * q + 32, 0:TOK], sel_pair[0:64, q, :], mT[:, h, :], start=False, stop=True)
                last.then_inc(S["kl_done"], 1)
                pe.wait_ge(S[f"shift{h}"], 16 * 12)
                for b in range(2 * HALF):
                    j, s = b // 2, b % 2
                    for pr in range(2):
                        if unit >= 2:
                            pe.wait_ge(S["exp_done"], unit - 1)
                        for a in range(4):
                            g, u = 2 * pr + a // 2, a % 2
                            last = mm(bank[2 + 2 * (unit % 2) + a // 2][:, TOK * u:TOK * u + TOK],
                                      KS[h][:, s, g, TOK * j:TOK * j + P],
                                      QS[h][:, u, s, g, TOK * j:TOK * j + TOK], start=True, stop=True)
                        last.then_inc(S["st_done"], 1)
                        unit += 1
                    if b >= 1:
                        weighted_values(2 * HALF * h + b - 1)
            weighted_values(B - 1)
            pe.wait_ge(S["exp_done"], 2 * B)
            pe.wait_ge(S["ld_enc"], 16)
            pe.wait_ge(S["ot_ready"], B)
            for c in range(QUADS):
                mm(bank[c][:, 0:2 * TOK], col["wo"], OT[:, 2 * c:2 * c + 2, :], start=True, stop=True).then_inc(S["wo_done"], 1)

            def layer_norm_pe(k, ctr, var):
                for c in range(QUADS):
                    pe.wait_ge(S[f"z_ready{k}"], c + 1)
                    mm(bank[ctr + c][:, 0:2 * TOK], col["center"], z[k][:, 2 * c:2 * c + 2, :],
                       start=True, stop=True).then_inc(S[f"ctr_done{k}"], 1)
                for c in range(QUADS):
                    pe.wait_ge(S[f"lsq_ready{k}"], c + 1)
                    mm(bank[var + c][:, 0:2 * TOK], col["mean"], lnsq[:, 2 * c:2 * c + 2, :],
                       start=True, stop=True).then_inc(S[f"var_done{k}"], 1)

            layer_norm_pe(0, 4, 0)
            pe.wait_ge(S["sdev_ready0"], QUADS)
            for c in range(QUADS):
                pe.wait_ge(S["enc_ready0"], c + 1)
                for q in range(4):
                    if c >= 1:
                        pe.wait_ge(S["relu_ready"], 4 * (c - 1) + q + 1)
                    mm(bank[q][:, 0:2 * TOK], ff1[:, q, :], enc[0][:, 2 * c:2 * c + 2, :],
                       start=True, stop=True).then_inc(S["ff1_done"], 1)
                for q in range(4):
                    pe.wait_ge(S["relu_ready"], 4 * c + q + 1)
                    last = mm(bank[4 + c][:, 0:2 * TOK], ff2[:, q, :], relu[:, c % 2, q, :], start=q == 0, stop=q == 3)
                last.then_inc(S["ff2_done"], 1)
            layer_norm_pe(1, 0, 4)

            pe.wait_ge(S["enc_ready1"], QUADS)
            for n in range(2):
                for jj in range(4):
                    tr(bank[n][:, P * jj:P * jj + P], enc[1][:, 4 * n + jj, 0:P], ident)
                    last = tr(bank[2 + n][0:LEFT, P * jj:P * jj + P], enc[1][:, 4 * n + jj, P:TOK], ident)
                last.then_inc(S["s2t_done"], 1)
            mm(bank[4][:, 0:PAIRS], col["wq2"], enc[1][:, :, P], start=True, stop=True).then_inc(S["tau_q"], 1)
            pe.wait_ge(S["tau_q_ready"], 1)
            mm(bank[5][:, 0:256], col["wk2"], q2m[:, :, :].rearrange("p j r -> p (j r)"),
               start=True, stop=True).then_inc(S["tau_u"], 1)
            pe.wait_ge(S["tau_u_ready"], 1)
            for j in range(PAIRS):
                a = TOK * (j // 4)
                last = mm(bank[6][32 * (j % 4):32 * (j % 4) + 32, a:a + TOK], u2[:, j, :], enc[1][:, j, :],
                          start=True, stop=True)
            last.then_inc(S["tau_s"], 1)
            pe.wait_ge(S["tau_p_ready"], 1)
            for jj in range(2):
                tr(bank[7][:, P * jj:P * jj + P], prob[:, jj, 0:P], ident)
                last = tr(bank[4][0:LEFT, P * jj:P * jj + P], prob[:, jj, P:TOK], ident)
            last.then_inc(S["pT_done"], 1)
            pe.wait_ge(S["pT_ready"], 1)
            pe.wait_ge(S["s2t_ready"], 2)
            for j in range(PAIRS):
                r = 32 * (j % 4)
                o = bank[5][:, 32 * j:32 * j + 32]
                mm(o, s2t[:, j, :], PT[:, j // 4, r:r + 32], start=True, stop=False)
                last = mm(o, s2l[:, j, :], PTl[:, j // 4, r:r + 32], start=False, stop=True)
            last.then_inc(S["tau_c"], 1)
            pe.wait_ge(S["tau_c_ready"], 1)
            mm(bank[6][:, 0:256], col["wv2"], c2[:, :, :].rearrange("p j r -> p (j r)"),
               start=True, stop=True).then_inc(S["tau_v"], 1)
            pe.wait_ge(S["tau_o_ready"], 1)
            mm(bank[7][:, 0:PAIRS], col["wo2"], tv["ob"][:, :], start=True, stop=True).then_inc(S["tau_out"], 1)

            for c in range(QUADS):
                pe.wait_ge(S["h_ready"], 2 * c + 2)
                for jj in range(2):
                    for t in range(2):
                        a = 256 * jj + P * t
                        last = mm(bank[c][0:CH, a:a + P], hT[:, 2 * c + jj, STEP * t:STEP * t + CH], col["center"],
                                  start=True, stop=True)
                last.then_inc(S["a1_done"], 1)

            def to_feature_major(bank0, ready, done):
                for c in range(QUADS):
                    pe.wait_ge(ready, c + 1)
                    for jj in range(2):
                        for t in range(2):
                            a = LOUT * jj + STEP * t
                            last = tr(bank[bank0 + c][:, a:a + CH], xn[:, c, jj, t, :, :].rearrange("p s d -> p (s d)"),
                                      ident[0:CH, 0:CH])
                    last.then_inc(done, 1)

            to_feature_major(4, S["xn_ready"], S["a2_done"])
            pe.wait_ge(S["ld_att"], 16)

            def exp_transposed(n):
                pe.wait_ge(S["ke_ready"], n + 1)
                if n >= 4:
                    pe.wait_ge(S["ett_ready"], n - 3)
                for jj in range(2):
                    for t in range(2):
                        a = 256 * jj + P * t
                        last = tr(bank[4 + n % 4][0:CH, a:a + P], E[:, n, jj, STEP * t:STEP * t + CH], ident)
                last.then_inc(S["et_done"], 1)

            for n in range(8):
                c, s = n // 2, n % 2
                pe.wait_ge(S["xnT_ready"], QUADS if n >= 1 else 1)
                if n >= 4:
                    pe.wait_ge(S["ke_ready"], n - 3)
                mm(bank[n % 4][:, 0:2 * LOUT], wk_att[:, s, :], xnT[:, 2 * c:2 * c + 2, :], start=True,
                   stop=True).then_inc(S["kp_done"], 1)
                if n >= 3:
                    exp_transposed(n - 3)
            for n in range(5, 8):
                exp_transposed(n)
            pe.wait_ge(S["ett_ready"], 8)
            for j in range(PAIRS):
                c, jj = j // 2, j % 2
                for s in range(2):
                    o = bank[j // 4][64 * s:64 * s + 64, P * (j % 4):P * (j % 4) + P]
                    mm(o, xn[0:STEP, c, jj, 0, s, :], ETt[0:STEP, 2 * c + s, jj, 0, :], start=True, stop=False)
                    last = mm(o, xn[:, c, jj, 1, s, :], ETt[:, 2 * c + s, jj, 1, :], start=False, stop=True)
                if j % 4 == 3:
                    last.then_inc(S["gt_done"], 1)
            for j in range(PAIRS):
                pe.wait_ge(S["gt_ready"], j // 4 + 1)
                last = mm(bank[4 + j // 2][:, 256 * (j % 2):256 * (j % 2) + 256], GT[:, j, :], col["wv_att"],
                          start=True, stop=True)
                if j % 2:
                    last.then_inc(S["ctx_done"], 1)
            for j in range(PAIRS):
                pe.wait_ge(S["ctx_ready"], j // 2 + 1)
                for s in range(2):
                    a = P * (j % 4) + D * s
                    last = mm(bank[2 + j // 4][:, a:a + D], cx[:, j, s, :], col["wqT"], start=True, stop=True)
                if j % 4 == 3:
                    last.then_inc(S["zz_done"], 1)
            for j in range(PAIRS):
                pe.wait_ge(S["zz_ready"], j // 4 + 1)
                last = mm(bank[0][:, D * j:D * j + D], Zs[:, j, :], col["wout"], start=True, stop=True)
            last.then_inc(S["mx_done"], 1)
            pe.wait_ge(S["mix_ready"], 1)
            for c in range(QUADS):
                for jj in range(2):
                    for t in range(2):
                        j, a = 2 * c + jj, 256 * jj + P * t
                        mm(bank[4 + c][0:CH, a:a + P], xnT[:, j, STEP * t:STEP * t + CH],
                           Mb[:, j, :, :].rearrange("p s o -> p (s o)"), start=True, stop=False)
                        last = mm(bank[4 + c][0:CH, a:a + P], hT[:, j, STEP * t:STEP * t + CH], ident,
                                  start=False, stop=True)
                last.then_inc(S["h2_done"], 1)
            pe.wait_ge(S["h2_ready"], QUADS)
            pe.wait_ge(S["identh_ready"], 1)
            for t in range(PAIRS):
                pe.wait_ge(S["xlo_ready"], t // 2 + 1)
                for bb in range(2):
                    for ch in range(2):
                        a = LOUT * bb + STEP * ch
                        last = mm(bank[t][:, a:a + CH],
                                  xparts[:, t // 2, t % 2, ch, bb, :, :].rearrange("p k d -> p (k d)"),
                                  identh[0:CH, 0:CH], start=True, stop=True)
                last.then_inc(S["a11_done"], 1)
            pe.wait_ge(S["wsplit_ready"], 1)
            for u in range(32):
                b, t = u // 2, u % 2
                pe.wait_ge(S["xa_ready"], b // 2 + 1)
                last = mm(bank[0][0:CH, 16 * u:16 * u + 16], xa[:, b, STEP * t:STEP * t + CH],
                          gate2[:, :, :].rearrange("p k e -> p (k e)"), start=True, stop=True)
            last.then_inc(S["gate_done"], 1)
            pe.wait_ge(S["nm_ready"], 1)
            for t in range(PAIRS):
                if t >= 2:
                    pe.wait_ge(S["mk_ready"], t - 1)
                for bb in range(2):
                    for ch in range(2):
                        a = LOUT * bb + STEP * ch
                        last = mm(bank[4 + t % 2][64:96, a:a + CH], nm[:, 4 * t + 2 * bb + ch, :], identh[0:CH, 0:CH],
                                  start=True, stop=True)
                last.then_inc(S["mk_done"], 1)
            pe.wait_ge(S["xb_preset"], 1)
            pe.wait_ge(S["xb_ready"], PAIRS)

            def down_tile(t):
                pe.wait_ge(S["lo_ready"], HPAIRS * (t + 1))
                if t >= 2:
                    pe.wait_ge(S["o_ready"], t - 1)
                for bb in range(2):
                    for ch in range(2):
                        n = 2 * D * (2 * bb + ch)
                        o = bank[6 + t % 2][0:CH, n:n + 2 * D]
                        a = LOUT * bb + STEP * ch
                        for e in range(E_N):
                            mm(o, hparts[:, t % 2, 0, e, a:a + CH], down2[:, e, :, :].rearrange("p k d -> p (k d)"),
                               start=e == 0, stop=False)
                        for e in range(E_N):
                            mm(o[:, 0:D], hparts[:, t % 2, 1, e, a:a + CH], down2[:, e, 0, :], start=False, stop=False)
                        last = mm(o[:, 0:D], xb[:, 2 * t + bb, STEP * ch:STEP * ch + CH], b2r[:, :], start=False, stop=True)
                last.then_inc(S["down_done"], 1)

            unit = 0
            for t in range(PAIRS):
                pe.wait_ge(S["mk_ready"], t + 1)
                for e in range(E_N):
                    if unit >= 4:
                        pe.wait_ge(S["gelu_done"], unit - 3)
                    mm(bank[e % 4][:, 0:2 * LOUT], up_a[:, e, :], xa[:, 2 * t:2 * t + 2, :], start=True, stop=False)
                    mm(bank[e % 4][:, 0:2 * LOUT], up_b[:, e, :], xb[:, 2 * t:2 * t + 2, :], start=False,
                       stop=True).then_inc(S["up_done"], 1)
                    unit += 1
                if t >= 1:
                    down_tile(t - 1)
            down_tile(PAIRS - 1)


def host_packs(w):
    f = np.float32

    def pair(m):
        o = np.zeros((P, 2 * m.shape[1]), f)
        o[:D, :m.shape[1]] = m
        o[D:, m.shape[1]:] = m
        return o

    def twice(v):
        return np.concatenate([v, v]).reshape(P, 1)

    def rows(v):
        return np.broadcast_to(v, (P, v.shape[0]))

    c = {}
    l = np.arange(L)[:, None].astype(np.float64)
    k = np.arange(NFREQ)[None, :]
    table = np.concatenate([np.cos(2 * np.pi * (l * k % L) / L), np.sin(2 * np.pi * (l * k % L) / L)], 1)
    table[:, NFREQ] = 1 - 2 * (l[:, 0] % 2)
    c["dft"] = table.astype(f).reshape(2, P, L).transpose(1, 0, 2).reshape(P, 2 * L)
    c["ident"] = np.eye(P, dtype=f)
    pos = np.arange(TOK)[:, None].astype(np.float64)
    div = np.exp(np.arange(0, D, 2) * (-np.log(10000.0) / D))
    pe = np.zeros((TOK, D), f)
    pe[:, 0::2] = np.sin(pos * div)
    pe[:, 1::2] = np.cos(pos * div)
    pe = np.concatenate([pe[1:], pe[:1]]).T
    c["posenc"] = np.concatenate([pe, pe])
    wi, bi = w["L0_tok_l_in_w"], w["L0_tok_l_in_b"]
    for n, name in enumerate("qkv"):
        c[f"w{name}"] = pair(wi[D * n:D * n + D].T)
    c["wv_stack"] = np.concatenate([wi[2 * D:].T] * 2)
    c["bq"], c["bk"] = twice(bi[:D]), twice(bi[D:2 * D])
    c["bv_row"] = rows(np.concatenate([bi[2 * D:]] * 2))
    p = np.arange(P)
    c["head16"] = (p[:, None] // DH == np.arange(16)[None]).astype(f)
    c["batch16"] = (p[:, None] // D == np.arange(16)[None] // HEADS).astype(f)
    ps, ph, pt, pj = p // 16 % 2, p // 2 % HEADS, p % 2, p // 32
    vm = np.zeros((P, 2, D), f)
    vc = np.zeros((P, 2, P), f)
    for s in range(2):
        own = (ps[:, None] == s) & (ph[:, None] == np.arange(D)[None] // DH)
        vm[:, s] = own
        vc[:, s, D * (1 - s):D * (1 - s) + D] = own
    c["vl_mask"], c["vl_const"] = vm.reshape(P, -1), vc.reshape(P, -1)
    m = np.arange(D)
    c["sel_left"] = np.stack([((p // 2)[:, None] == m[None]) & (pt[:, None] == t) for t in range(2)], 1).astype(f).reshape(P, -1)
    sp = np.zeros((P, HALF, 32), f)
    for j in range(HALF):
        sp[:D, j] = (m[:, None] // 16 == j) & (m[:, None] % 16 == np.arange(32)[None] // 2)
    c["sel_pair"] = sp.reshape(P, -1)

    c["wo"] = pair(w["L0_tok_l_out_w"].T)
    c["center"] = pair((np.eye(D) - 1.0 / D).astype(f))
    c["mean"] = pair(np.full((D, D), 1.0 / D, f))
    for n, name in (("bo", "l_out_b"), ("g1", "ln1_g"), ("b1", "ln1_b"), ("g2", "ln2_g"), ("b2", "ln2_b"), ("ffb2", "ff_b2"),
                    ("bo2", "m_out_b")):
        c[n] = twice(w["L0_tok_" + name])
    c["eps"] = np.full((P, 1), EPS, f)
    f1, f2 = np.zeros((P, 4, P), f), np.zeros((P, 4, P), f)
    for s in range(2):
        for k in range(2):
            f1[D * s:D * s + D, 2 * s + k] = w["L0_tok_ff_w1"][P * k:P * k + P].T
            f2[:, 2 * s + k, D * s:D * s + D] = w["L0_tok_ff_w2"][:, P * k:P * k + P].T
    c["ff1"], c["ff2"] = f1.reshape(P, -1), f2.reshape(P, -1)
    c["ffb1"] = w["L0_tok_ff_b1"].reshape(2, P).T
    wi, bi = w["L0_tok_m_in_w"], w["L0_tok_m_in_b"]
    c["wq2"], c["wk2"], c["wv2"] = pair(wi[:D].T), pair(wi[D:2 * D]), pair(wi[2 * D:].T)
    c["bq2"], c["bv2"] = twice(bi[:D]), twice(bi[2 * D:])
    c["head32"] = (p[:, None] // DH == np.arange(32)[None]).astype(f)
    c["wo2"] = pair(w["L0_tok_m_out_w"].T)

    wqkv, wout = w["L0_attn_W_qkv"], w["L0_attn_W_out"]
    c["wk_att"], c["wv_att"] = pair(wqkv[:, P:2 * P]), pair(wqkv[:, 2 * P:])
    c["ctx_mask"] = (p[:, None] // AD == p[None] // AD).astype(f)
    c["wqT"], c["wout"] = wqkv[:, :P].T, wout
    c["mix_mask"] = ((p[:, None] // D == p[None] // D) * AD ** -0.5).astype(f)
    c["bout_row"] = rows(np.concatenate([w["L0_attn_b_out"]] * 2))
    c["rank"] = rows((E_N - np.arange(2 * P) % E_N).astype(f))
    c["gate"] = np.concatenate([w["L0_ffn_Wg"]] * 2)
    c["bg_row"] = rows(w["L0_ffn_bg"])
    c["eb1"] = w["L0_ffn_b1"].T
    c["eps_sx"] = np.full((P, 1), EPS / (SX * SX), f)
    c["b2rows"], c["b2part"], c["mask_rows"] = np.zeros((P, D), f), np.zeros((P, PARTS), f), np.zeros((P, E_N), f)
    for k in range(PARTS):
        c["b2rows"][M_ROW + E_N * k:M_ROW + E_N * k + E_N] = w["L0_ffn_b2"]
        c["b2part"][M_ROW + E_N * k:M_ROW + E_N * k + E_N, k] = 1
    for e in range(E_N):
        c["mask_rows"][N_ROW + e, e] = -MASK
    c["up"] = np.concatenate([w["L0_ffn_W1"].transpose(1, 0, 2).reshape(D, -1)] * 2)
    c["down"] = w["L0_ffn_W2"].transpose(1, 0, 2).reshape(P, -1)
    return {k: np.ascontiguousarray(np.concatenate([c[n] for n, _ in v], 1), dtype=f) for k, v in PACKS.items()}


def kernel(**inputs):
    import concourse.bacc as bacc
    from concourse.bass_utils import run_bass_kernel_spmd

    w = {k: np.asarray(v) for k, v in inputs.items()}
    arrays = {"x_dram": np.ascontiguousarray(w["x"])}
    arrays.update({f"pack_{k}_dram": v for k, v in host_packs(w).items()})
    nc = bacc.Bacc("TRN2", target_bir_lowering=False, num_devices=1)
    aps = {k: nc.dram_tensor(k, v.shape, F32, kind="ExternalInput").ap() for k, v in arrays.items()}
    out = nc.dram_tensor("out_dram", (B, LOUT, D), F32, kind="ExternalOutput").ap()
    audio_tower(nc, aps["x_dram"], {k: aps[f"pack_{k}_dram"] for k in PACKS}, out)
    r = run_bass_kernel_spmd(nc, [arrays], core_ids=[0])
    return r.results[0]["out_dram"]
```

```python
from contextlib import ExitStack

import numpy as np
import concourse.bass as bass
from concourse import mybir

ACT = mybir.ActivationFunctionType
ALU = mybir.AluOpType
F32 = mybir.dt.float32
F16 = mybir.dt.float16
BF16 = mybir.dt.bfloat16
I32 = mybir.dt.int32
AX_X = mybir.AxisListType.X
RMAX = bass.bass_isa.ReduceOp.max

B, L, D = 16, 256, 64
P = 128
PAIRS = B // 2
HALF = PAIRS // 2
QUADS = PAIRS // 2
NFREQ = L // 2
TOK = NFREQ + 2
HEADS, DH = 8, 8
LEFT = TOK - P
WIN = 32
LOUT = L - WIN + 1
CH = 113
STEP = LOUT - CH
FF = 4 * D
AH, AD = 4, 32
E_N, HID = 8, 128
EPS = 1e-5
SX = 4096.0
QK_BANK = {"q": (0, 1, 2, 3), "k": (4, 5, 6, 7)}
SL_BANK, MT_BANK, KL_BANK = (6, 0), (7, 1), (6, 0)
AHEAD = 4
ENC_BANKS = ((0, 1), (2, 3))
FF1_BANKS, FF2_BANKS = ((0, 0), (2, 0)), ((1, 1), (3, 1))
MASK = 2.0 ** 15
CHOICE = 2.0 ** 14
PARTS = 3
EXPONENT = 0x7F800000
TERMS = 6
GROUPS = 4
ARENA = 27440
Q_TERM = (0, 0, 0, 1, 1, 2)
K_TERM = (0, 1, 2, 0, 1, 0)
TERM_RUNS = ((0, 3), (3, 2), (5, 1))
SHIFT_ROW = TERMS * DH
N_ROW, M_ROW = D, D + E_N

PACKS = {
    "dft": [("dft", 2 * L), ("ident", P)],
    "qkv": [("posenc", TOK), ("wq", P), ("wk", P), ("wv", P), ("wv_stack", D), ("bq", 1), ("bk", 1),
            ("bv_row", P), ("head16", 16), ("batch16", 16), ("vl_mask", 2 * D), ("vl_const", 2 * P),
            ("sel_left", 2 * D), ("sel_pair", P)],
    "enc": [("wo", P), ("center", P), ("mean2", 32), ("bo", 1), ("g1_rows", P), ("b1", 1), ("g2_rows", P), ("b2", 1),
            ("eps", 1), ("ff1", 4 * P), ("ffb1", 2), ("ff2", 4 * P), ("ffb2", 1),
            ("wq2", P), ("bq2", 1), ("wk2", P), ("head32", 32), ("wv2", P), ("bv2", 1), ("wo2", P), ("bo2", 1)],
    "att": [("wk_att", 2 * P), ("wv_att", 2 * P), ("ctx_mask", P), ("wqT", D), ("wout", D), ("mix_mask", P),
            ("bout_row", P), ("rank", P), ("gate", E_N), ("bg_row", E_N), ("b2rows", D), ("b2part", PARTS),
            ("eb1", E_N), ("mask_rows", E_N), ("eps_sx", 1)],
    "ffn": [("up", E_N * HID), ("down", E_N * D)],
}
WIDTH = {k: sum(w for _, w in v) for k, v in PACKS.items()}


def audio_tower(nc, x, packs, out):
    def up_bank(t, e):
        return (0, 1, 2, 4)[e % 4] if t >= HALF else (E_N * t + e) % 3

    def down_bank(t):
        return 5 if t > HALF and t % 2 else 3

    scr_qk = nc.dram_tensor("scr_qk", (2, 2, 2, 3, D, HALF * TOK), BF16, kind="Internal").ap()
    scr_m = nc.dram_tensor("scr_m", (2, 3, HALF * 16, TOK), BF16, kind="Internal").ap()

    with ExitStack() as ctx:
        def sb(name, shape, dt=F32):
            return ctx.enter_context(nc.sbuf_tensor(name, shape, dt))

        def sem(name):
            return ctx.enter_context(nc.semaphore(name))

        psum = ctx.enter_context(nc.psum_tensor("psum", [P, 8, 512], F32))
        bank = [psum[:, i, :] for i in range(8)]

        pk = {k: sb(f"pk_{k}", [P, w]) for k, w in WIDTH.items()}
        col = {}
        for k, cols in PACKS.items():
            at = 0
            for name, w in cols:
                col[name] = pk[k][:, at:at + w]
                at += w
        dft = col["dft"].rearrange("p (c n) -> p c n", c=2)
        ident = col["ident"]
        vl_mask = col["vl_mask"].rearrange("p (s d) -> p s d", s=2)
        sel_left = col["sel_left"].rearrange("p (t m) -> p t m", t=2)
        sel_pair = col["sel_pair"].rearrange("p (j m) -> p j m", j=HALF)
        ff1 = col["ff1"].rearrange("p (q n) -> p q n", q=4)
        ff2 = col["ff2"].rearrange("p (q n) -> p q n", q=4)
        wk_att = col["wk_att"].rearrange("p (s n) -> p s n", s=2)
        up = col["up"].rearrange("p (e n) -> p e n", e=E_N)
        down = col["down"].rearrange("p (e n) -> p e n", e=E_N)

        arena = sb("arena", [P, ARENA])
        used = {"encoder": 0, "layers": 0}

        def shared(time, shape, dt=F32):
            n = int(np.prod(shape[1:])) * (1 if dt == F32 else 2) // (1 if dt == F32 else 4)
            a = used[time]
            used[time] += n
            assert used[time] <= ARENA
            v = arena[0:shape[0], a:a + n]
            v = v if dt == F32 else v.bitcast(dt)
            dims = " ".join(f"d{i}" for i in range(1, len(shape)))
            return v.rearrange(f"p ({dims}) -> p {dims}", **{f"d{i}": shape[i] for i in range(1, len(shape))})

        early = sb("early", [P, 2 * PAIRS * L + 4 * PAIRS * TOK])
        taken = [0]

        def early_part(n):
            taken[0] += PAIRS * n
            return early[:, taken[0] - PAIRS * n:taken[0]].rearrange("p (j n) -> p j n", j=PAIRS)

        sq, xT = early_part(L), early_part(L)
        src, OT, enc = early_part(TOK), early_part(TOK), (early_part(TOK), early_part(TOK))
        amp2 = sb("amp2", [P, PAIRS, NFREQ + 1])
        amp = amp2
        vl_tmp = sb("vl_tmp", [P, 2, D])
        VL = sb("VL", [P, 2, 2, P])
        V = shared("encoder", [P, PAIRS, P])
        vleft_in = shared("encoder", [P, PAIRS, 16, LEFT])
        QS1 = shared("encoder", [P, 8 * HALF * TOK])
        KS1 = shared("encoder", [P, 2, 4, HALF * TOK], BF16)
        ET = shared("encoder", [P, 4, 4, TOK])
        Vx = shared("encoder", [P, 4, HEADS, P])
        used["middle"] = used["encoder"]
        QT = shared("encoder", [P, PAIRS, TOK])
        KT = shared("encoder", [P, PAIRS, TOK])
        resid = shared("encoder", [P, 2, HALF * TOK])
        qk3 = [shared("encoder", [P, 6, HALF * TOK], BF16) for h in range(2)]
        QS0 = shared("encoder", [P, 8 * HALF * TOK])
        KS0 = shared("encoder", [P, 2, 4, HALF * TOK], BF16)
        qleft = shared("encoder", [P, PAIRS, 16, LEFT])
        kleft = shared("encoder", [P, PAIRS, 16, LEFT])
        QS32, KS = (QS0, QS1), (KS0, KS1)
        QS = [q[:, :].bitcast(BF16).rearrange("p (u s g n) -> p u s g n", u=2, s=2, g=4) for q in QS32]
        mneg = sb("mneg", [P, 2, HALF * 16])
        mlneg = sb("mlneg", [P, 2])
        mT = sb("mT", [HALF * 16, 2, TOK])
        mres = sb("mres", [HALF * 16, 2, 2, TOK])
        m3 = sb("m3", [HALF * 16, 2, 3, TOK], BF16)
        EL = sb("EL", [P, 2, TOK])
        xl = ET.rearrange("p a b n -> p (a b n)")[:, 0:2 * B * D].rearrange("p (c n) -> p c n", c=2)
        rden = sb("rden", [P, 2, TOK])
        z = [shared("middle", [P, PAIRS, TOK]) for k in range(2)]
        lnsq = shared("middle", [P, PAIRS, TOK])
        sdev = shared("middle", [P, 2, 2 * TOK])
        rstd = shared("middle", [P, 2, 2 * TOK])
        zc = shared("middle", [P, PAIRS, TOK])
        lnn = shared("middle", [P, PAIRS, TOK])
        relu = shared("middle", [P, 2, 4, 2 * TOK])
        y = shared("middle", [P, PAIRS, L + 1])
        hraw = sq[:, :, 0:LOUT]
        hT = sb("hT", [P, PAIRS, LOUT])

        s2t = shared("middle", [P, PAIRS, P])
        s2l = sb("s2l", [LEFT, PAIRS, P])
        tv = {n: sb(f"tau_{n}", [P, PAIRS]) for n in ("q", "o", "ob", "t0", "abs", "exp", "ln", "sp", "clip", "tau", "p2",
                                                      "p4", "p8", "p16", "p32", "neg32", "s1", "s2", "s3", "s4", "s5",
                                                      "inv")}
        q2m = sb("q2m", [P, PAIRS, 32])
        u2 = sb("u2", [P, PAIRS, 32])
        c2 = sb("c2", [P, PAIRS, 32])
        o2t = sb("o2t", [P, PAIRS, 32])
        mx2 = sb("mx2", [P, 3, 2])
        psm = sb("psm", [P, 2])
        prob = sb("prob", [P, 2, TOK])
        PT = sb("PT", [P, 2, P])
        PTl = sb("PTl", [LEFT, 2, P])
        asq = shared("layers", [CH, QUADS, 512])
        xn = shared("layers", [CH, QUADS, 2, 2, 2, D])
        st = {n: sb(f"st_{n}", [CH, 32]) for n in ("ss0", "var0", "rs0", "sum1", "mean1", "ss1", "var1", "rs1")}
        km = sb("km", [P, 8, 2])
        ksum = sb("ksum", [P, 8, 2])
        rks = sb("rks", [P, 8, 2])
        xnT, E, ETt, GT, cx, Zs, Mb = [], [], [], [], [], [], []
        attention0 = used["layers"]
        for h in range(2):
            xnT.append(shared("layers", [P, HALF, LOUT]))
            E.append(shared("layers", [P, 4, 2, LOUT]))
            ETt.append(shared("layers", [CH, 4, 2, 2, P]))
            GT.append(shared("layers", [P, HALF, P]))
            cx.append(shared("layers", [P, HALF, 2, P]))
            Zs.append(shared("layers", [P, HALF, P]))
            Mb.append(shared("layers", [P, HALF, 2, D]))
        n_hid = 2 * E_N * 2 * LOUT
        hid = early[:, 0:n_hid].rearrange("p (a e n) -> p a e n", a=2, e=E_N)
        hparts = arena[:, attention0:attention0 + n_hid].bitcast(F16).rearrange("p (a k e n) -> p a k e n", a=2, k=2, e=E_N)
        h2 = shared("layers", [CH, QUADS, 2, 2, 2, D])
        xparts = asq[:, :, :].rearrange("p c n -> p (c n)").bitcast(F16).rearrange(
            "p (c a b s k d) -> p c a b s k d", c=QUADS, a=2, b=2, s=2, k=2)
        xa = shared("layers", [P, B, LOUT], F16)
        xb = shared("layers", [P, B, LOUT], F16)
        tp = {n: shared("layers", [CH, 32, E_N]) for n in ("g", "eq1", "rk1", "sel1", "g2", "eq2", "rk2", "sel2")}
        tm = {n: sb(f"topm_{n}", [CH, 32]) for n in ("m1", "p1", "m2", "p2")}
        nm = sb("nm", [CH, 32, 4 * E_N], F16)
        identh = sb("identh", [P, P], F16)
        wmax = sb("wmax", [P, 2, 5])
        scale = sb("scale", [P, 4, 4])
        up_ab = amp2[:, :, :].rearrange("p j n -> p (j n)")[:, 0:E_N * HID].bitcast(F16).rearrange(
            "p (k e n) -> p k e n", k=2, e=E_N)
        up_a, up_b = up_ab[:, 0], up_ab[:, 1]
        down2 = col["dft"].bitcast(F16).rearrange("p (e k d) -> p e k d", e=E_N, k=2)
        gate2 = sb("gate2", [P, 2, E_N], F16)
        bg2 = sb("bg2", [P, E_N])
        b2s = pk["qkv"][:, 0:3 * D].rearrange("p (k d) -> p k d", k=3)
        b2p = sb("b2p", [P, PARTS, D], F16)
        b2r = sb("b2r", [P, D], F16)
        ob = shared("layers", [CH, 2, 2, 2, D])
        osb = shared("layers", [CH, 2, 2, 2, D])

        both = scale[:, 2, :]
        s_hid, s_up, s_gate, s_down = (scale[:, 1, n:n + 1] for n in range(4))
        inv_up, inv_down = scale[:, 3, 0:1], scale[:, 3, 1:2]
        step_sems = {e: sem(f"{e}_step") for e in ("dve", "pool")}
        names = ("ld_dft ld_x0 ld_x1 ld_qkv ld_enc ld_att ld_ffn qs_zero ks_one fft_done xt_done sq_done xT_ready "
                 "amp2_ready amp_ready src_ready q_done k_done v_done vl_done qT_ready kT_ready v_ready vl_ready "
                 "vleft_in_ready split_q split_k q_stored0 q_stored1 k_stored0 k_stored1 strips0 strips1 left_ready s_done max_ready sl_done "
                 "mlneg_ready mt_done mT_ready m3_ready m_stored shift0 shift1 kl_done el_ready st_done exp_done "
                 "vx_ready pv_done ot_ready wo_done z_ready0 z_ready1 ctr_done0 ctr_done1 lsq_ready0 lsq_ready1 "
                 "var_done0 var_done1 sdev_ready0 sdev_ready1 rstd_ready0 rstd_ready1 spread_done0 spread_done1 lnn_ready0 lnn_ready1 zc_ready0 zc_ready1 enc_ready0 enc_ready1 ff1_done relu_ready ff2_done "
                 "tau_q tau_q_ready tau_u tau_u_ready tau_s tau_m tau_e tau_p_ready s2t_done s2t_ready pT_done "
                 "pT_ready tau_c tau_c_ready tau_v tau_o_ready tau_out tau_abs tau_exp tau_ln inv_ready hraw_ready "
                 "scales_ready xsq_ready scan_done h_ready xb_preset identh_ready a1_done asq_ready var_ready0 var_ready1 rs_ready0 rs_ready1 xn_ready a2_done xnT_ready "
                 "kp_done km_ready ke_ready et_done ett_ready gt_done gt_ready ctx_done ctx_ready zz_done zz_ready "
                 "mx_done mix_ready h2_done h2_ready xc_ready x2_ready xhi_ready xlo_ready a11_done xa_ready xb_ready gate_done nm_ready "
                 "wmax_ready wred_ready wsplit_ready hi_dve hi_pool hi_act lo_ready sd_ready0 sd_ready1 "
                 "mk_done mk_ready up_done gelu_done down_done o_ready out_stored0 out_stored1").split()
        S = {n: sem(n) for n in names}

        block = ctx.enter_context(nc.Block())
        scale_h = 1.0 / float(np.sqrt(np.float32(DH)))

        @block.sync
        def _(sp):
            xs = x.rearrange("b (c l) d -> l c b d", c=2)
            xd = xl[:, :, :].rearrange("p c (b d) -> p c b d", b=B)
            for h in range(2):
                for c in range(2):
                    sp.dma_start(xd[:, c, 8 * h:8 * h + 8, :], xs[:, c, 8 * h:8 * h + 8, :]).then_inc(S[f"ld_x{h}"], 16)
            sp.dma_start(pk["qkv"][:, :], packs["qkv"]).then_inc(S["ld_qkv"], 16)
            for h in range(2):
                for w, name in enumerate("qk"):
                    sp.wait_ge(S[f"split_{name}"], h + 1)
                    for u in range(2):
                        sp.dma_start(scr_qk[h, w, u].rearrange("t p n -> p t n"),
                                     qk3[h][64 * u:64 * u + 64, 3 * w:3 * w + 3, :]).then_inc(S[f"{name}_stored{h}"], 16)
                sp.wait_ge(S["qs_zero"], h + 1)
                sp.wait_ge(S["ks_one"], h + 1)
                sp.wait_ge(S[f"q_stored{h}"], 32)
                for t, n in TERM_RUNS:
                    for u in range(2):
                        r = 64 * u + DH * t
                        rows = scr_qk[h, 0, u, Q_TERM[t]].rearrange("(i g) n -> i (g n)", i=DH)
                        sp.dma_start(QS[h][r:r + DH * n, u, :, :, :].rearrange("p s g n -> p (s g n)"),
                                     rows.unsqueeze(0).to_broadcast([n, DH, 8 * HALF * TOK])).then_inc(S[f"strips{h}"], 16)
                sp.wait_ge(S[f"k_stored{h}"], 32)
                for t, n in TERM_RUNS:
                    for u in range(2):
                        r = 64 * u + DH * t
                        rows = scr_qk[h, 1, u, 0:n].rearrange("t (i g) n -> (t i) (g n)", i=DH)
                        sp.dma_start(KS[h][r:r + DH * n, :, :, :].rearrange("p s g n -> p (s g n)"), rows).then_inc(S[f"strips{h}"], 16)
            for h in range(2):
                sp.wait_ge(S["m3_ready"], h + 1)
                sp.dma_start(scr_m[h].rearrange("k r n -> r k n"), m3[:, h, :, :]).then_inc(S["m_stored"], 16)
                if h == 0:
                    sp.dma_start(pk["enc"][:, :], packs["enc"]).then_inc(S["ld_enc"], 16)
                sp.wait_ge(S["m_stored"], 16 * (h + 1))
                for u in range(2):
                    r = 64 * u + SHIFT_ROW
                    sp.dma_start(QS[h][r:r + 3, u, :, :, :].rearrange("p s g n -> p (s g n)"),
                                 scr_m[h, :, 32 * u:32 * u + 32, :].rearrange("k r n -> k (r n)")).then_inc(S[f"shift{h}"], 16)
            for t in range(PAIRS):
                sp.wait_ge(S["o_ready"], t + 1)
                for c in range(2):
                    n = STEP + c
                    sp.dma_start(out[2 * t:2 * t + 2, STEP * c:STEP * c + n, :].rearrange("s l d -> l s d"),
                                 osb[0:n, t % 2, :, c, :]).then_inc(S[f"out_stored{t % 2}"], 16)
            for k in range(2):
                sp.wait_ge(S[f"out_stored{k}"], 16 * PAIRS)

        @block.gpsimd
        def _(pool):
            def strips_preset(h):
                nc.gpsimd.memset(QS32[h][:, :], 0.0).then_inc(S["qs_zero"], 1)
                nc.gpsimd.memset(KS[h][:, :, :, :], 1.0).then_inc(S["ks_one"], 1)

            steps = [0]

            def link(ins):
                steps[0] += 1
                ins.then_inc(step_sems["pool"], 1)
                pool.wait_ge(step_sems["pool"], steps[0])

            strips_preset(0)
            strips_preset(1)
            link(nc.gpsimd.memset(Vx[:, :, :, :], 0.0))
            for slot in range(4):
                for hd in range(HEADS):
                    c0 = 64 * (1 - slot % 2) + DH * hd
                    last = nc.gpsimd.memset(Vx[:, slot, hd, c0:c0 + DH], 1.0)
            link(last)
            for b in range(B):
                j, s = b // 2, b % 2
                pool.wait_ge(S["v_ready"], j // 2 + 1)
                if b >= 4:
                    pool.wait_ge(S["pv_done"], b - 3)
                for hd in range(HEADS):
                    c0 = 64 * s + DH * hd
                    last = nc.gpsimd.tensor_copy(Vx[:, b % 4, hd, c0:c0 + DH],
                                                 V[:, j, 64 * s + DH * hd:64 * s + DH * hd + DH])
                last.then_inc(S["vx_ready"], 1)
            pool.wait_ge(S["wmax_ready"], 1)
            nc.gpsimd.partition_all_reduce(wmax[:, 1, :], wmax[:, 0, :], P, RMAX).then_inc(S["wred_ready"], 1)
            pool.wait_ge(S["scales_ready"], 1)
            link(nc.gpsimd.tensor_scalar(up, up, s_up, None, ALU.mult))
            link(nc.gpsimd.tensor_scalar(down, down, s_down, None, ALU.mult))
            link(nc.gpsimd.tensor_scalar(col["gate"], col["gate"], s_gate, None, ALU.mult))
            link(nc.gpsimd.tensor_scalar(b2s[:, 0, :], col["b2rows"], both[:, 2:3], None, ALU.mult))
            link(nc.gpsimd.tensor_copy(up_a[:, :, :], up))
            link(nc.gpsimd.tensor_copy(down2[:, :, 0, :], down))
            link(nc.gpsimd.tensor_copy(gate2[:, 0, :], col["gate"]))
            link(nc.gpsimd.tensor_scalar(bg2[:, :], col["bg_row"], both[:, 3:4], None, ALU.mult))
            link(nc.gpsimd.tensor_copy(up_b[64:128, :, :], col["mask_rows"][64:128, :].unsqueeze(2).to_broadcast([64, E_N, HID])))
            link(nc.gpsimd.tensor_tensor(up_b[0:64, :, :], up[0:64, :, :], up_a[0:64, :, :], ALU.subtract))
            link(nc.gpsimd.tensor_tensor(down2[:, :, 1, :], down, down2[:, :, 0, :], ALU.subtract))
            link(nc.gpsimd.tensor_tensor(gate2[:, 1, :], col["gate"], gate2[:, 0, :], ALU.subtract))
            for k in range(PARTS):
                link(nc.gpsimd.tensor_copy(b2p[:, k, :], b2s[:, k, :]))
                if k < PARTS - 1:
                    link(nc.gpsimd.tensor_tensor(b2s[:, k + 1, :], b2s[:, k, :], b2p[:, k, :], ALU.subtract))
            for k in range(PARTS):
                link(nc.gpsimd.tensor_scalar(b2s[:, k, :], b2p[:, k, :], col["b2part"][:, k:k + 1], None, ALU.mult))
            link(nc.gpsimd.tensor_tensor(b2s[:, 0, :], b2s[:, 0, :], b2s[:, 1, :], ALU.add))
            nc.gpsimd.tensor_tensor(b2r[:, :], b2s[:, 0, :], b2s[:, 2, :], ALU.add).then_inc(S["wsplit_ready"], 1)
            pool.wait_ge(S["wsplit_ready"], 1)
            pool.wait_ge(S["xc_ready"], 2)
            nc.gpsimd.memset(xb[96:128, :, :], 0.0).then_inc(S["xb_preset"], 1)
            pool.wait_ge(S["xb_preset"], 1)
            for t in range(1, PAIRS - 1):
                pool.wait_ge(S["gelu_done"], E_N * t + 4)
                if t >= 2:
                    pool.wait_ge(S["down_done"], t - 1)
                nc.gpsimd.tensor_scalar(hparts[:, t % 2, 0, 2:4, :], hid[:, t % 2, 2:4, :], s_hid, None,
                                        ALU.mult).then_inc(S["hi_pool"], 1)
                pool.wait_ge(S["hi_pool"], t)

        @block.scalar
        def _(act):
            act.dma_start(pk["dft"][:, :], packs["dft"]).then_inc(S["ld_dft"], 16)

            def amplitudes(h):
                for c in range(2 * h, 2 * h + 2):
                    act.wait_ge(S["fft_done"], c + 1)
                    nc.scalar.activation(sq[:, 2 * c:2 * c + 2, :], bank[c][:, :].rearrange("p (j n) -> p j n", j=2),
                                         ACT.Square).then_inc(S["sq_done"], 1)
                for c in range(2 * h, 2 * h + 2):
                    act.wait_ge(S["amp2_ready"], c + 1)
                    nc.scalar.activation(amp[:, 2 * c:2 * c + 2, :], amp2[:, 2 * c:2 * c + 2, :],
                                         ACT.Sqrt).then_inc(S["amp_ready"], 1)

            def queries_keys(h):
                for c in range(2 * h, 2 * h + 2):
                    for (w, T, b) in (("q", QT, "bq"), ("k", KT, "bk")):
                        act.wait_ge(S[f"{w}_done"], c + 1)
                        ps = bank[QK_BANK[w][c]][:, 0:2 * TOK].rearrange("p (j n) -> p j n", j=2)
                        nc.scalar.activation(T[:, 2 * c:2 * c + 2, :], ps, ACT.Identity,
                                             bias=col[b]).then_inc(S[f"{w}T_ready"], 1)

            amplitudes(0)
            for k in ("att", "ffn"):
                act.dma_start(pk[k][:, :], packs[k]).then_inc(S[f"ld_{k}"], 16)
            act.wait_ge(S["ld_qkv"], 16)
            queries_keys(0)
            amplitudes(1)
            queries_keys(1)
            def left_exp(h):
                act.wait_ge(S["kl_done"], h + 1)
                nc.scalar.activation(EL[:, h, :], bank[KL_BANK[h]][:, 0:TOK], ACT.Exp, scale=scale_h).then_inc(S["el_ready"], 1)

            def weights(b):
                for unit in (2 * b, 2 * b + 1):
                    act.wait_ge(S["st_done"], unit + 1)
                    if unit >= 4:
                        act.wait_ge(S["pv_done"], unit // 2 - 1)
                    k0 = 2 + 2 * (unit % 2)
                    nc.scalar.activation(ET[:, unit % 4, :, :].rearrange("p (k u) n -> p k (u n)", k=2),
                                         psum[:, k0:k0 + 2, 0:2 * TOK], ACT.Exp,
                                         scale=scale_h).then_inc(S["exp_done"], 1)

            def centred(k, h):
                for cl in range(2):
                    c = 2 * h + cl
                    act.wait_ge(S[f"ctr_done{k}"], c + 1)
                    nc.scalar.activation(lnsq[:, 2 * c:2 * c + 2, :],
                                         bank[ENC_BANKS[h][cl]][:, 0:2 * TOK].rearrange("p (j n) -> p j n", j=2),
                                         ACT.Square).then_inc(S[f"lsq_ready{k}"], 1)

            def variance(k, h):
                act.wait_ge(S[f"var_done{k}"], 2 * h + 2)
                nc.scalar.activation(sdev[0:64, k, :], bank[ENC_BANKS[h][0]][0:64, 0:2 * TOK], ACT.Sqrt,
                                     bias=col["eps"][0:64, :]).then_inc(S[f"sdev_ready{k}"], 1)

            def normalised(k, h):
                for c in range(2 * h, 2 * h + 2):
                    act.wait_ge(S[f"lnn_ready{k}"], c + 1)
                    nc.scalar.activation(enc[k][:, 2 * c:2 * c + 2, :], lnn[:, 2 * c:2 * c + 2, :], ACT.Identity,
                                         bias=col[f"b{k + 1}"]).then_inc(S[f"enc_ready{k}"], 1)

            def relu_step(h, cl, q):
                c = 2 * h + cl
                act.wait_ge(S["ff1_done"], 4 * c + q + 1)
                if c >= 2:
                    act.wait_ge(S["ff2_done"], c - 1)
                nc.scalar.activation(relu[:, c % 2, q, :], bank[FF1_BANKS[h][q % 2]][:, 0:2 * TOK], ACT.Relu,
                                     bias=col["ffb1"][:, q % 2:q % 2 + 1]).then_inc(S["relu_ready"], 1)

            def tau_query(h):
                act.wait_ge(S["s2t_done"], h + 1)
                nc.scalar.copy(s2t[:, 4 * h:4 * h + 4, :], bank[5].rearrange("p (j n) -> p j n", j=4))
                nc.scalar.copy(s2l[:, 4 * h:4 * h + 4, :],
                               bank[6][0:LEFT, :].rearrange("p (j n) -> p j n", j=4)).then_inc(S["s2t_ready"], 1)

            def tau_scores(h):
                act.wait_ge(S["tau_m"], h + 1)
                nc.scalar.activation(prob[:, h, :], bank[4][:, 0:TOK], ACT.Exp, bias=mx2[:, 1, h:h + 1],
                                     scale=scale_h, accum_out=psm[:, h:h + 1]).then_inc(S["tau_e"], 1)

            def tau_out(h):
                own = slice(HALF * h, HALF * h + HALF)
                act.wait_ge(S["tau_abs"], h + 1)
                nc.scalar.activation(tv["exp"][:, own], tv["abs"][:, own], ACT.Exp, scale=-1.0).then_inc(S["tau_exp"], 1)
                act.wait_ge(S["tau_exp"], h + 1)
                nc.scalar.activation(tv["ln"][:, own], tv["exp"][:, own], ACT.Ln, bias=1.0).then_inc(S["tau_ln"], 1)

            def window(h):
                act.wait_ge(S["inv_ready"], h + 1)
                for j in range(HALF * h, HALF * h + HALF):
                    act.wait_ge(S["hraw_ready"], j + 1)
                    nc.scalar.activation(hT[:, j, :], hraw[:, j, :], ACT.Identity,
                                         scale=tv["inv"][:, j:j + 1]).then_inc(S["h_ready"], 1)

            def norm1_centred(h):
                for cl in range(2):
                    c = 2 * h + cl
                    act.wait_ge(S["a1_done"], c + 1)
                    nc.scalar.activation(asq[:, c, :], bank[4 * h + cl][0:CH, :], ACT.Square).then_inc(S["asq_ready"], 1)

            def deviation(k, h):
                own = slice(16 * h, 16 * h + 16)
                act.wait_ge(S[f"var_ready{k}"], h + 1)
                nc.scalar.activation(st[f"var{k}"][:, own], st[f"ss{k}"][:, own], ACT.Sqrt,
                                     bias=col["eps_sx" if k else "eps"][0:CH, :],
                                     scale=1.0 / (D * SX * SX) if k else 1.0 / D).then_inc(S[f"sd_ready{k}"], 1)

            def norm1_transposed(h):
                for cl in range(2):
                    c = 2 * h + cl
                    act.wait_ge(S["a2_done"], c + 1)
                    nc.scalar.copy(xnT[h][:, 2 * cl:2 * cl + 2, :],
                                   bank[4 * h + 2 + cl][:, 0:2 * LOUT].rearrange("p (j n) -> p j n", j=2)).then_inc(S["xnT_ready"], 1)

            def keys(h):
                for n in range(4 * h, 4 * h + 4):
                    act.wait_ge(S["km_ready"], n + 1)
                    for jj in range(2):
                        ins = nc.scalar.activation(E[h][:, n % 4, jj, :], bank[4 * h + n % 2][:, LOUT * jj:LOUT * jj + LOUT], ACT.Exp,
                                                   bias=km[:, n, jj:jj + 1], accum_out=ksum[:, n, jj:jj + 1])
                    ins.then_inc(S["ke_ready"], 1)

            def gram(h):
                act.wait_ge(S["gt_done"], h + 1)
                nc.scalar.copy(GT[h][:, :, :],
                               bank[4 * h].rearrange("p (j n) -> p j n", j=4)).then_inc(S["gt_ready"], 1)

            def queries_in(h):
                act.wait_ge(S["zz_done"], h + 1)
                nc.scalar.copy(Zs[h][:, :, :],
                               bank[4 * h + 1].rearrange("p (j n) -> p j n", j=4)).then_inc(S["zz_ready"], 1)

            def norm2_squares(h):
                for c in range(2 * h, 2 * h + 2):
                    act.wait_ge(S["xc_ready"], c + 1)
                    nc.scalar.activation(asq[:, c, :], xn[:, c, :, :, :, :].rearrange("p a b s d -> p (a b s d)"),
                                         ACT.Square).then_inc(S["xsq_ready"], 1)
                deviation(1, h)

            def norm2_parts(h):
                for c in range(2 * h, 2 * h + 2):
                    act.wait_ge(S["x2_ready"], c + 1)
                    nc.scalar.copy(xparts[:, c, :, :, :, 0, :].rearrange("p a b s d -> p (a b s) d"),
                                   xn[:, c, :, :, :, :].rearrange("p a b s d -> p (a b s) d")).then_inc(S["xhi_ready"], 1)

            def norm2_transposed(h):
                for t in range(HALF * h, HALF * h + HALF):
                    act.wait_ge(S["a11_done"], t + 1)
                    nc.scalar.copy(xa[:, 2 * t:2 * t + 2, :],
                                   bank[t][:, 0:2 * LOUT].rearrange("p (j n) -> p j n", j=2)).then_inc(S["xa_ready"], 1)

            def mask_rows(h):
                for t in range(HALF * h, HALF * h + HALF):
                    act.wait_ge(S["mk_done"], t + 1)
                    nc.scalar.copy(xb[64:96, 2 * t:2 * t + 2, :],
                                   bank[t][64:96, 0:2 * LOUT].rearrange("p (j n) -> p j n", j=2)).then_inc(S["mk_ready"], 1)

            def first_part(t, g):
                act.wait_ge(S["gelu_done"], E_N * t + 2 * g + 2)
                if t >= 2:
                    act.wait_ge(S["down_done"], t - 1)
                two = slice(2 * g, 2 * g + 2)
                nc.scalar.activation(hparts[:, t % 2, 0, two, :], hid[:, t % 2, two, :], ACT.Copy,
                                     scale=s_hid).then_inc(S["hi_act"], 1)

            def hidden(t):
                act.wait_ge(S["wsplit_ready"], 1)
                if t >= 2:
                    act.wait_ge(S["lo_ready"], GROUPS * (t - 1))
                for e in range(E_N):
                    act.wait_ge(S["up_done"], E_N * t + e + 1)
                    nc.scalar.activation(hid[:, t % 2, e, :], bank[up_bank(t, e)][:, 0:2 * LOUT], ACT.Gelu,
                                         bias=col["eb1"][:, e:e + 1], scale=inv_up).then_inc(S["gelu_done"], 1)
                    if e == 6:
                        first_part(t, 2)
                first_part(t, 3)

            left_exp(0)
            for b in range(2 * HALF):
                weights(b)
            left_exp(1)
            act.wait_ge(S["ld_enc"], 16)
            for b in range(2 * HALF, B):
                weights(b)
                if b == 10:
                    centred(0, 0)
                elif b == 11:
                    variance(0, 0)
                elif b == 12:
                    normalised(0, 0)
                elif b == 13:
                    relu_step(0, 0, 0)
                    relu_step(0, 0, 1)
                elif b == 14:
                    relu_step(0, 0, 2)
                    relu_step(0, 0, 3)
                elif b == 15:
                    relu_step(0, 1, 0)
                    relu_step(0, 1, 1)
            relu_step(0, 1, 2)
            relu_step(0, 1, 3)
            centred(1, 0)
            variance(1, 0)
            centred(0, 1)
            normalised(1, 0)
            variance(0, 1)
            tau_query(0)
            normalised(0, 1)
            for q in range(4):
                relu_step(1, 0, q)
            tau_scores(0)
            for q in range(4):
                relu_step(1, 1, q)
            centred(1, 1)
            variance(1, 1)
            tau_out(0)
            normalised(1, 1)
            window(0)
            tau_query(1)
            norm1_centred(0)
            deviation(0, 0)
            tau_scores(1)
            norm1_transposed(0)
            keys(0)
            tau_out(1)
            gram(0)
            window(1)
            queries_in(0)
            norm1_centred(1)
            deviation(0, 1)
            norm1_transposed(1)
            keys(1)
            norm2_squares(0)
            norm2_parts(0)
            gram(1)
            norm2_transposed(0)
            queries_in(1)
            mask_rows(0)
            norm2_squares(1)
            hidden(0)
            norm2_parts(1)
            hidden(1)
            norm2_transposed(1)
            for t in range(2, PAIRS):
                hidden(t)

        @block.vector
        def _(dve):
            chain = [0]

            def link(ins):
                chain[0] += 1
                ins.then_inc(step_sems["dve"], 1)
                dve.wait_ge(step_sems["dve"], chain[0])

            pe_row = col["posenc"].unsqueeze(1)

            def transposed(h):
                for c in range(2 * h, 2 * h + 2):
                    dve.wait_ge(S["xt_done"], c + 1)
                    nc.vector.tensor_copy(xT[:, 2 * c:2 * c + 2, :],
                                          bank[4 + c][:, :].rearrange("p (j n) -> p j n", j=2)).then_inc(S["xT_ready"], 1)

            def squares(h):
                for c in range(2 * h, 2 * h + 2):
                    dve.wait_ge(S["sq_done"], c + 1)
                    two = slice(2 * c, 2 * c + 2)
                    nc.vector.tensor_tensor(amp2[:, two, 1:NFREQ], sq[:, two, 1:NFREQ], sq[:, two, NFREQ + 1:L], ALU.add)
                    nc.vector.tensor_copy(amp2[:, two, 0:NFREQ + 1:NFREQ],
                                          sq[:, two, 0:NFREQ + 1:NFREQ]).then_inc(S["amp2_ready"], 1)

            def tokens(h):
                dve.wait_ge(S["ld_qkv"], 16)
                dve.wait_ge(S["xT_ready"], 2 * h + 2)
                for c in range(2 * h, 2 * h + 2):
                    dve.wait_ge(S["amp_ready"], c + 1)
                    two = slice(2 * c, 2 * c + 2)
                    nc.vector.tensor_tensor(src[:, two, 0:NFREQ + 1], amp[:, two, :],
                                            pe_row[:, :, 0:NFREQ + 1].to_broadcast([P, 2, NFREQ + 1]), ALU.add)
                    nc.vector.tensor_tensor(src[:, two, TOK - 1:TOK], xT[:, two, L - 1:L],
                                            pe_row[:, :, TOK - 1:TOK].to_broadcast([P, 2, 1]), ALU.add).then_inc(S["src_ready"], 1)

            head16 = col["head16"].unsqueeze(2).to_broadcast([P, 16, LEFT])
            batch16 = col["batch16"].unsqueeze(2).to_broadcast([P, 16, LEFT])

            def left_inputs(h):
                dve.wait_ge(S["src_ready"], 2 * h + 2)
                for j in range(HALF * h, HALF * h + HALF):
                    ins = nc.vector.tensor_tensor(vleft_in[:, j, :, :],
                                                  src[:, j, P:TOK].unsqueeze(1).to_broadcast([P, 16, LEFT]), batch16, ALU.mult)
                ins.then_inc(S["vleft_in_ready"], 1)

            def split(h, n, T, done):
                full = T[:, HALF * h:HALF * h + HALF, :].rearrange("p j n -> p (j n)")
                link(nc.vector.tensor_copy(qk3[h][:, 3 * n, :], full))
                link(nc.vector.tensor_tensor(resid[:, n, :], full, qk3[h][:, 3 * n, :], ALU.subtract))
                link(nc.vector.tensor_copy(qk3[h][:, 3 * n + 1, :], resid[:, n, :]))
                nc.vector.tensor_tensor(qk3[h][:, 3 * n + 2, :], resid[:, n, :], qk3[h][:, 3 * n + 1, :],
                                        ALU.subtract).then_inc(done, 1)

            def values(h):
                bv2 = col["bv_row"].unsqueeze(1).to_broadcast([P, 2, P])
                for c in range(2 * h, 2 * h + 2):
                    dve.wait_ge(S["v_done"], c + 1)
                    nc.vector.tensor_tensor(V[:, 2 * c:2 * c + 2, :],
                                            bank[QK_BANK["q"][c]][:, 0:2 * P].rearrange("p (j n) -> p j n", j=2),
                                            bv2, ALU.add).then_inc(S["v_ready"], 1)
                dve.wait_ge(S["vl_done"], h + 1)
                link(nc.vector.tensor_tensor(vl_tmp[:, h, :], bank[QK_BANK["k"][2 * h]][:, 0:D], col["bv_row"][:, 0:D], ALU.add))
                for s in range(2):
                    ins = nc.vector.tensor_tensor(VL[:, h, s, 64 * s:64 * s + 64], vl_tmp[:, h, :], vl_mask[:, s, :], ALU.mult)
                ins.then_inc(S["vl_ready"], 1)

            def left_queries_keys(h):
                for j in range(HALF * h, HALF * h + HALF):
                    nc.vector.tensor_tensor(qleft[:, j, :, :], QT[:, j, P:TOK].unsqueeze(1).to_broadcast([P, 16, LEFT]),
                                            head16, ALU.mult)
                    ins = nc.vector.tensor_tensor(kleft[:, j, :, :], KT[:, j, P:TOK].unsqueeze(1).to_broadcast([P, 16, LEFT]),
                                                  head16, ALU.mult)
                ins.then_inc(S["left_ready"], 1)

            transposed(0)
            squares(0)
            tokens(0)
            transposed(1)
            dve.wait_ge(S["qT_ready"], 2)
            split(0, 0, QT, S["split_q"])
            dve.wait_ge(S["kT_ready"], 2)
            dve.wait_ge(S["split_q"], 1)
            split(0, 1, KT, S["split_k"])
            squares(1)
            tokens(1)
            nc.vector.tensor_copy(VL[:, :, :, :].rearrange("p h s n -> p h (s n)"),
                                  col["vl_const"].unsqueeze(1).to_broadcast([P, 2, 2 * P]))
            left_inputs(0)
            left_inputs(1)
            values(0)
            dve.wait_ge(S["qT_ready"], 4)
            split(1, 0, QT, S["split_q"])
            dve.wait_ge(S["kT_ready"], 4)
            split(1, 1, KT, S["split_k"])
            values(1)
            left_queries_keys(0)
            units = [0]

            def score_max(b):
                h, j, s = b // (2 * HALF), b // 2 % HALF, b % 2
                at = 16 * s + j
                for cols in (slice(at, at + 9, 4), slice(32 + at, 32 + at + 9, 4), slice(12 + at, 64, 32)):
                    n = len(range(*cols.indices(64)))
                    dve.wait_ge(S["s_done"], units[0] + 1)
                    nc.vector.tensor_reduce(mneg[:, h, cols], bank[units[0] % 2][:, 0:n * TOK].rearrange("p (a n) -> p a n", a=n),
                                            AX_X, ALU.max, negate=True).then_inc(S["max_ready"], 1)
                    units[0] += 1

            def max_parts(h):
                dve.wait_ge(S["sl_done"], h + 1)
                nc.vector.tensor_reduce(mlneg[:, h:h + 1], bank[SL_BANK[h]][:, 0:TOK], AX_X, ALU.max,
                                        negate=True).then_inc(S["mlneg_ready"], 1)
                dve.wait_ge(S["mt_done"], h + 1)
                nc.vector.tensor_copy(mT[:, h, :], bank[MT_BANK[h]][0:64, 0:TOK]).then_inc(S["mT_ready"], 1)
                dve.wait_ge(S["mT_ready"], h + 1)
                link(nc.vector.tensor_copy(m3[:, h, 0, :], mT[:, h, :]))
                link(nc.vector.tensor_tensor(mres[:, h, 0, :], mT[:, h, :], m3[:, h, 0, :], ALU.subtract))
                link(nc.vector.tensor_copy(m3[:, h, 1, :], mres[:, h, 0, :]))
                nc.vector.tensor_tensor(m3[:, h, 2, :], mres[:, h, 0, :], m3[:, h, 1, :],
                                        ALU.subtract).then_inc(S["m3_ready"], 1)

            def divide(b):
                j, s = b // 2, b % 2
                mine, other = slice(64 * s, 64 * s + 64), slice(64 * (1 - s), 64 * (1 - s) + 64)
                dve.wait_ge(S["pv_done"], b + 1)
                link(nc.vector.reciprocal(rden[mine, b % 2, :], bank[6 + b % 2][other, 0:TOK]))
                nc.vector.tensor_tensor(OT[mine, j, :], bank[6 + b % 2][mine, 0:TOK], rden[mine, b % 2, :],
                                        ALU.mult).then_inc(S["ot_ready"], 1)

            def weight_max():
                dve.wait_ge(S["ld_att"], 16)
                dve.wait_ge(S["ld_ffn"], 16)
                for n, name in enumerate(("up", "eb1", "down", "gate", "b2rows")):
                    ins = nc.vector.tensor_reduce(wmax[:, 0, n:n + 1], col[name], AX_X, ALU.max, apply_absolute_value=True)
                ins.then_inc(S["wmax_ready"], 1)

            top = [wmax[:, 1, n:n + 1] for n in range(5)]
            den, pw = scale[:, 0, :], scale[:, 1, :]

            def weight_scales():
                dve.wait_ge(S["wred_ready"], 1)
                link(nc.vector.tensor_scalar(wmax[:, 1, :], wmax[:, 1, :], 1e-6, None, ALU.max))
                link(nc.vector.scalar_tensor_tensor(den[:, 0:1], top[0], float(D), top[1], ALU.mult, ALU.add))
                link(nc.vector.tensor_scalar(den[:, 0:1], den[:, 0:1], 2.0 ** -15, None, ALU.mult))
                link(nc.vector.tensor_scalar(den[:, 1:2], top[1], 16.0, 2.0 ** -17, ALU.add, ALU.mult))
                link(nc.vector.scalar_tensor_tensor(den[:, 1:2], top[0], 2.0 ** -10, den[:, 1:2], ALU.mult, ALU.max))
                link(nc.vector.tensor_scalar(den[:, 2:3], top[3], 2.0 ** -10, None, ALU.mult))
                link(nc.vector.reciprocal(pw[:, 0:3], den[:, 0:3]))
                link(nc.vector.tensor_scalar(pw[:, 0:3].bitcast(I32), pw[:, 0:3].bitcast(I32), EXPONENT, None, ALU.bitwise_and))
                link(nc.vector.tensor_tensor(den[:, 3:4], top[4], s_hid, ALU.mult))
                link(nc.vector.tensor_scalar(den[:, 3:4], den[:, 3:4], CHOICE ** -2, None, ALU.mult))
                link(nc.vector.scalar_tensor_tensor(den[:, 3:4], top[2], 2.0 ** -14, den[:, 3:4], ALU.mult, ALU.max))
                link(nc.vector.reciprocal(pw[:, 3:4], den[:, 3:4]))
                link(nc.vector.tensor_scalar(pw[:, 3:4].bitcast(I32), pw[:, 3:4].bitcast(I32), EXPONENT, None, ALU.bitwise_and))
                link(nc.vector.tensor_scalar(both[:, 0:1], s_up, SX, None, ALU.mult))
                link(nc.vector.tensor_tensor(both[:, 1:2], s_hid, s_down, ALU.mult))
                link(nc.vector.tensor_scalar(both[:, 2:3], both[:, 1:2], 1.0 / CHOICE, None, ALU.mult))
                link(nc.vector.tensor_scalar(both[:, 3:4], s_gate, SX, None, ALU.mult))
                nc.vector.reciprocal(scale[:, 3, 0:2], both[:, 0:2]).then_inc(S["scales_ready"], 1)

            def two_of(ap, c):
                return ap[:, 2 * c:2 * c + 2, :].rearrange("p j n -> p (j n)")

            def attention_out(h):
                for cl in range(2):
                    c = 2 * h + cl
                    dve.wait_ge(S["wo_done"], c + 1)
                    nc.vector.scalar_tensor_tensor(two_of(z[0], c), bank[ENC_BANKS[h][cl]][:, 0:2 * TOK], col["bo"], two_of(src, c),
                                                   ALU.add, ALU.add).then_inc(S["z_ready0"], 1)

            def centred(k, h):
                for cl in range(2):
                    c = 2 * h + cl
                    dve.wait_ge(S[f"lsq_ready{k}"], c + 1)
                    nc.vector.tensor_copy(two_of(zc, c), bank[ENC_BANKS[h][cl]][:, 0:2 * TOK]).then_inc(S[f"zc_ready{k}"], 1)

            def variance(k, h):
                dve.wait_ge(S[f"sdev_ready{k}"], h + 1)
                nc.vector.reciprocal(rstd[0:64, k, :], sdev[0:64, k, :]).then_inc(S[f"rstd_ready{k}"], 1)

            def normalised(k, h):
                for cl in range(2):
                    c = 2 * h + cl
                    dve.wait_ge(S[f"zc_ready{k}"], c + 1)
                    dve.wait_ge(S[f"spread_done{k}"], c + 1)
                    nc.vector.tensor_tensor(two_of(lnn, c), two_of(zc, c), bank[ENC_BANKS[h][cl]][:, 0:2 * TOK],
                                            ALU.mult).then_inc(S[f"lnn_ready{k}"], 1)

            def feed_forward(h, cl):
                c = 2 * h + cl
                dve.wait_ge(S["ff2_done"], c + 1)
                dve.wait_ge(S["enc_ready0"], c + 1)
                nc.vector.scalar_tensor_tensor(two_of(z[1], c), bank[FF2_BANKS[h][cl]][:, 0:2 * TOK], col["ffb2"],
                                               two_of(enc[0], c), ALU.add, ALU.add).then_inc(S["z_ready1"], 1)

            head32 = col["head32"].unsqueeze(1).to_broadcast([P, HALF, 32])

            def tau_query(h):
                own = slice(HALF * h, HALF * h + HALF)
                dve.wait_ge(S["tau_q"], h + 1)
                link(nc.vector.tensor_scalar(tv["q"][:, own], bank[4][:, 0:HALF], col["bq2"], None, ALU.add))
                nc.vector.tensor_tensor(q2m[:, own, :], tv["q"][:, own].unsqueeze(2).to_broadcast([P, HALF, 32]), head32,
                                        ALU.mult).then_inc(S["tau_q_ready"], 1)

            def tau_keys(h):
                own = slice(HALF * h, HALF * h + HALF)
                dve.wait_ge(S["tau_u"], h + 1)
                nc.vector.tensor_copy(u2[:, own, :],
                                      bank[7][:, 0:P].rearrange("p (j r) -> p j r", r=32)).then_inc(S["tau_u_ready"], 1)

            def tau_max(h):
                dve.wait_ge(S["tau_s"], h + 1)
                link(nc.vector.tensor_reduce(mx2[:, 0, h:h + 1], bank[4][:, 0:TOK], AX_X, ALU.max, negate=True))
                nc.vector.tensor_scalar(mx2[:, 1, h:h + 1], mx2[:, 0, h:h + 1], scale_h, None, ALU.mult).then_inc(S["tau_m"], 1)

            def tau_normalise(h):
                dve.wait_ge(S["tau_e"], h + 1)
                link(nc.vector.reciprocal(mx2[:, 2, h:h + 1], psm[:, h:h + 1]))
                nc.vector.tensor_scalar(prob[:, h, :], prob[:, h, :], mx2[:, 2, h:h + 1], None,
                                        ALU.mult).then_inc(S["tau_p_ready"], 1)

            def tau_probs(h):
                dve.wait_ge(S["pT_done"], h + 1)
                nc.vector.tensor_copy(PT[:, h, :], bank[7][:, 0:P])
                nc.vector.tensor_copy(PTl[:, h, :], bank[4][0:LEFT, 0:P]).then_inc(S["pT_ready"], 1)

            def tau_context(h):
                own = slice(HALF * h, HALF * h + HALF)
                dve.wait_ge(S["tau_c"], h + 1)
                nc.vector.tensor_copy(c2[:, own, :],
                                      bank[5][:, 0:P].rearrange("p (j r) -> p j r", r=32)).then_inc(S["tau_c_ready"], 1)

            def tau_values(h):
                own = slice(HALF * h, HALF * h + HALF)
                dve.wait_ge(S["tau_v"], h + 1)
                link(nc.vector.tensor_tensor(o2t[:, own, :], bank[6][:, 0:P].rearrange("p (j r) -> p j r", r=32), head32, ALU.mult))
                link(nc.vector.tensor_reduce(tv["o"][:, own], o2t[:, own, :], AX_X, ALU.add))
                nc.vector.tensor_scalar(tv["ob"][:, own], tv["o"][:, own], col["bv2"], None, ALU.add).then_inc(S["tau_o_ready"], 1)

            def tau_out(h):
                v = {n: a[:, HALF * h:HALF * h + HALF] for n, a in tv.items()}
                dve.wait_ge(S["tau_out"], h + 1)
                link(nc.vector.tensor_scalar(v["t0"], bank[7][:, 0:HALF], col["bo2"], None, ALU.add))
                nc.vector.scalar_tensor_tensor(v["abs"], v["t0"], -1.0, v["t0"], ALU.mult, ALU.max).then_inc(S["tau_abs"], 1)

            def window_weights(h):
                v = {n: a[:, HALF * h:HALF * h + HALF] for n, a in tv.items()}
                dve.wait_ge(S["tau_ln"], h + 1)
                link(nc.vector.scalar_tensor_tensor(v["sp"], v["t0"], 0.0, v["ln"], ALU.max, ALU.add))
                link(nc.vector.tensor_scalar(v["clip"], v["sp"], 0.1, 0.01, ALU.mult, ALU.max))
                link(nc.vector.tensor_scalar(v["tau"], v["clip"], 1.0, None, ALU.min))
                nc.vector.tensor_scalar(v["s1"], v["tau"], 1.0, None, ALU.add)
                link(nc.vector.tensor_tensor(v["p2"], v["tau"], v["tau"], ALU.mult))
                for n in range(2, 6):
                    p = f"p{2 ** (n - 1)}"
                    nc.vector.scalar_tensor_tensor(v[f"s{n}"], v[p], 1.0, v[f"s{n - 1}"], ALU.add, ALU.mult)
                    link(nc.vector.tensor_tensor(v[f"p{2 ** n}"], v[p], v[p], ALU.mult))
                nc.vector.reciprocal(v["inv"], v["s5"]).then_inc(S["inv_ready"], 1)
                nc.vector.tensor_scalar(v["neg32"], v["p32"], -1.0, None, ALU.mult)
                link(nc.vector.memset(y[:, HALF * h:HALF * h + HALF, 0:1], 0.0))

            def window(h):
                for j in range(HALF * h, HALF * h + HALF):
                    ins = nc.vector.tensor_tensor_scan(y[:, j, 1:L + 1], tv["tau"][:, j:j + 1].to_broadcast([P, L]), xT[:, j, :],
                                                       0.0, ALU.mult, ALU.add)
                    ins.then_inc(S["scan_done"], 1)
                    if j % HALF:
                        windowed(j - 1)
                windowed(HALF * h + HALF - 1)

            def windowed(j):
                dve.wait_ge(S["scan_done"], j + 1)
                nc.vector.scalar_tensor_tensor(hraw[:, j, :], y[:, j, 0:LOUT], tv["neg32"][:, j:j + 1],
                                               y[:, j, WIN:WIN + LOUT], ALU.mult, ALU.add).then_inc(S["hraw_ready"], 1)

            def grouped(ap):
                return ap.rearrange("p (g d) -> p g d", d=D)

            def squares_sum(k, h, ready):
                for c in range(2 * h, 2 * h + 2):
                    dve.wait_ge(ready, c + 1)
                    ins = nc.vector.tensor_reduce(st[f"ss{k}"][:, 8 * c:8 * c + 8], grouped(asq[:, c, :]), AX_X, ALU.add)
                ins.then_inc(S[f"var_ready{k}"], 1)

            def deviation(k, h):
                own = slice(16 * h, 16 * h + 16)
                dve.wait_ge(S[f"sd_ready{k}"], h + 1)
                nc.vector.reciprocal(st[f"rs{k}"][:, own], st[f"var{k}"][:, own]).then_inc(S[f"rs_ready{k}"], 1)
                dve.wait_ge(S[f"rs_ready{k}"], h + 1)

            def xn_of(c):
                return xn[:, c, :, :, :, :].rearrange("p a b s d -> p (a b s) d")

            def per_group(name, c):
                return st[name][:, 8 * c:8 * c + 8].unsqueeze(2).to_broadcast([CH, 8, D])

            def norm1(h):
                deviation(0, h)
                for cl in range(2):
                    c = 2 * h + cl
                    nc.vector.tensor_tensor(xn_of(c), grouped(bank[4 * h + cl][0:CH, :]), per_group("rs0", c),
                                            ALU.mult).then_inc(S["xn_ready"], 1)

            def key_max(n):
                dve.wait_ge(S["kp_done"], n + 1)
                nc.vector.tensor_reduce(km[:, n, :],
                                        bank[4 * (n // 4) + n % 2][:, 0:2 * LOUT].rearrange("p (j n) -> p j n", j=2), AX_X,
                                        ALU.max, negate=True).then_inc(S["km_ready"], 1)

            def key_transposed(n):
                dve.wait_ge(S["et_done"], n + 1)
                nc.vector.tensor_copy(ETt[n // 4][:, n % 4, :, :, :].rearrange("p a b n -> p (a b n)"),
                                      bank[4 * (n // 4) + 2 + n % 2][0:CH, :]).then_inc(S["ett_ready"], 1)

            def keys(h):
                key_max(4 * h)
                key_max(4 * h + 1)
                for n in range(4 * h, 4 * h + 4):
                    key_transposed(n)
                    if n + 2 < 4 * h + 4:
                        key_max(n + 2)

            def context(h):
                own = slice(4 * h, 4 * h + 4)
                link(nc.vector.reciprocal(rks[:, own, :], ksum[:, own, :]))
                for cl in range(2):
                    c = 2 * h + cl
                    dve.wait_ge(S["ctx_done"], c + 1)
                    for jj in range(2):
                        for s in range(2):
                            a = 256 * jj + P * s
                            ins = nc.vector.scalar_tensor_tensor(cx[h][:, 2 * cl + jj, s, :], bank[4 * h + 2 + cl][:, a:a + P],
                                                                 rks[:, 2 * c + s, jj:jj + 1], col["ctx_mask"],
                                                                 ALU.mult, ALU.mult)
                    ins.then_inc(S["ctx_ready"], 1)

            def mix(h):
                dve.wait_ge(S["mx_done"], h + 1)
                nc.vector.tensor_tensor(Mb[h][:, :, :, :],
                                        bank[4 * h][:, 0:4 * D].rearrange("p (j o) -> p j o", o=D).unsqueeze(2).to_broadcast([P, HALF, 2, D]),
                                        col["mix_mask"].rearrange("p (s o) -> p s o", s=2).unsqueeze(1).to_broadcast([P, HALF, 2, D]),
                                        ALU.mult).then_inc(S["mix_ready"], 1)

            def h2_of(c):
                return h2[:, c, :, :, :, :].rearrange("p a b s d -> p (a b s) d")

            def residual(h):
                for cl in range(2):
                    c = 2 * h + cl
                    dve.wait_ge(S["h2_done"], c + 1)
                    nc.vector.tensor_tensor(h2[:, c, :, :, :, :].rearrange("p a b s d -> p (a b) (s d)"),
                                            bank[4 * h + 2 + cl][0:CH, :].rearrange("p (a n) -> p a n", n=P),
                                            col["bout_row"][0:CH, :].unsqueeze(1).to_broadcast([CH, 4, P]),
                                            ALU.add).then_inc(S["h2_ready"], 1)

            def norm2_centred(h):
                own = slice(16 * h, 16 * h + 16)
                for c in range(2 * h, 2 * h + 2):
                    dve.wait_ge(S["h2_ready"], c + 1)
                    ins = nc.vector.tensor_reduce(st["sum1"][:, 8 * c:8 * c + 8], h2_of(c), AX_X, ALU.add)
                link(ins)
                link(nc.vector.tensor_scalar(st["mean1"][:, own], st["sum1"][:, own], 1.0 / D, None, ALU.mult))
                for c in range(2 * h, 2 * h + 2):
                    nc.vector.tensor_tensor(xn_of(c), h2_of(c), per_group("mean1", c), ALU.subtract).then_inc(S["xc_ready"], 1)

            def norm2(h):
                deviation(1, h)
                for c in range(2 * h, 2 * h + 2):
                    nc.vector.tensor_tensor(xn_of(c), xn_of(c), per_group("rs1", c), ALU.mult).then_inc(S["x2_ready"], 1)

            def norm2_rests(h):
                for c in range(2 * h, 2 * h + 2):
                    dve.wait_ge(S["xhi_ready"], c + 1)
                    nc.vector.tensor_tensor(xparts[:, c, :, :, :, 1, :].rearrange("p a b s d -> p (a b s) d"), xn_of(c),
                                            xparts[:, c, :, :, :, 0, :].rearrange("p a b s d -> p (a b s) d"),
                                            ALU.subtract).then_inc(S["xlo_ready"], 1)

            def norm2_transposed(h):
                for t in range(HALF * h, HALF * h + HALF):
                    dve.wait_ge(S["xa_ready"], t + 1)
                    nc.vector.tensor_copy(xb[0:64, 2 * t:2 * t + 2, :], xa[0:64, 2 * t:2 * t + 2, :]).then_inc(S["xb_ready"], 1)

            def choose(h):
                units = slice(16 * h, 16 * h + 16)
                rank = col["rank"][0:CH, :].rearrange("p (u e) -> p u e", e=E_N)
                q = {n: a[:, units, :] for n, a in tp.items()}

                def per_unit(ap):
                    return ap[:, units].unsqueeze(2).to_broadcast([CH, 16, E_N])

                dve.wait_ge(S["gate_done"], h + 1)
                got = bank[4 * h][0:CH, 0:256].rearrange("p (u k e) -> p u k e", k=2, e=E_N)
                link(nc.vector.tensor_tensor(q["g"], got[:, :, 1, :], bg2[0:CH, :].unsqueeze(1).to_broadcast([CH, 16, E_N]), ALU.add))
                link(nc.vector.tensor_tensor(q["g"], got[:, :, 0, :], q["g"], ALU.add))
                for k, g in ((1, "g"), (2, "g2")):
                    m, p = tm[f"m{k}"], tm[f"p{k}"]
                    link(nc.vector.tensor_reduce(m[:, units], q[g], AX_X, ALU.max))
                    link(nc.vector.tensor_tensor(q[f"eq{k}"], q[g], per_unit(m), ALU.is_equal))
                    link(nc.vector.tensor_tensor(q[f"rk{k}"], q[f"eq{k}"], rank, ALU.mult))
                    link(nc.vector.tensor_reduce(p[:, units], q[f"rk{k}"], AX_X, ALU.max))
                    link(nc.vector.tensor_tensor(q[f"sel{k}"], q[f"rk{k}"], per_unit(p), ALU.is_equal))
                    if k == 1:
                        link(nc.vector.scalar_tensor_tensor(q["g2"], q["sel1"], -3.0e38, q["g"], ALU.mult, ALU.add))
                link(nc.vector.tensor_tensor(q["eq1"], q["sel1"], q["sel2"], ALU.add))
                nc.vector.tensor_scalar(nm[:, units, E_N:].rearrange("p u (k e) -> p u k e", e=E_N),
                                        q["eq1"].unsqueeze(2).to_broadcast([CH, 16, PARTS, E_N]), CHOICE, None, ALU.mult)
                nc.vector.tensor_scalar(nm[:, units, 0:E_N], q["eq1"], -MASK, MASK, ALU.mult, ALU.add).then_inc(S["nm_ready"], 1)

            def mask_row(t):
                dve.wait_ge(S["mk_done"], t + 1)
                nc.vector.tensor_copy(xb[64:96, 2 * t:2 * t + 2, :],
                                      bank[t][64:96, 0:2 * LOUT].rearrange("p (j n) -> p j n", j=2)).then_inc(S["mk_ready"], 1)

            def output_tile(t):
                dve.wait_ge(S["down_done"], t + 1)
                if t >= 2:
                    dve.wait_ge(S[f"out_stored{t % 2}"], 32 * (t // 2))
                y4 = bank[down_bank(t)][0:CH, :].rearrange("p (s c k d) -> p s c k d", s=2, c=2, k=2)
                for bb in range(2):
                    ins = nc.vector.scalar_tensor_tensor(ob[:, t % 2, bb, :, :], y4[:, bb, :, 1, :], inv_down[0:CH, :],
                                                         h2[:, t // 2, t % 2, :, bb, :], ALU.mult, ALU.add)
                link(ins)
                nc.vector.scalar_tensor_tensor(osb[:, t % 2, :, :, :], y4[:, :, :, 0, :], inv_down[0:CH, :],
                                               ob[:, t % 2, :, :, :], ALU.mult, ALU.add).then_inc(S["o_ready"], 1)

            def first_part(t, g):
                two = slice(2 * g, 2 * g + 2)
                dve.wait_ge(S["gelu_done"], E_N * t + 2 * g + 2)
                nc.vector.tensor_scalar(hparts[:, t % 2, 0, two, :], hid[:, t % 2, two, :], s_hid, None,
                                        ALU.mult).then_inc(S["hi_dve"], 1)

            def second_part(t, g):
                two = slice(2 * g, 2 * g + 2)
                nc.vector.scalar_tensor_tensor(hparts[:, t % 2, 1, two, :], hid[:, t % 2, two, :], s_hid,
                                               hparts[:, t % 2, 0, two, :], ALU.mult,
                                               ALU.subtract).then_inc(S["lo_ready"], 1)

            def hidden(t):
                if t >= 2:
                    dve.wait_ge(S["down_done"], t - 1)
                alone = t in (0, PAIRS - 1)
                made_before = t + (t > 0)
                first_part(t, 0)
                dve.wait_ge(S["hi_dve"], made_before + 1)
                second_part(t, 0)
                if alone:
                    first_part(t, 1)
                    dve.wait_ge(S["hi_dve"], made_before + 2)
                else:
                    dve.wait_ge(S["hi_pool"], t)
                second_part(t, 1)
                for g in (2, 3):
                    dve.wait_ge(S["hi_act"], 2 * t + g - 1)
                    second_part(t, g)

            for b in range(2 * HALF):
                score_max(b)
            max_parts(0)
            left_queries_keys(1)
            for b in range(2 * HALF, 2 * HALF + AHEAD):
                score_max(b)
            for b in range(2 * HALF):
                if 2 * HALF + AHEAD + b < B:
                    score_max(2 * HALF + AHEAD + b)
                    if 2 * HALF + AHEAD + b == B - 1:
                        max_parts(1)
                if b:
                    divide(b - 1)
            weight_max()
            dve.wait_ge(S["ld_enc"], 16)
            for b in range(2 * HALF, B):
                if b == 15:
                    feed_forward(0, 0)
                divide(b - 1)
                if b == 9:
                    attention_out(0)
                elif b == 10:
                    centred(0, 0)
                elif b == 11:
                    variance(0, 0)
                elif b == 12:
                    normalised(0, 0)
            divide(B - 1)
            feed_forward(0, 1)
            centred(1, 0)
            attention_out(1)
            variance(1, 0)
            centred(0, 1)
            normalised(1, 0)
            variance(0, 1)
            tau_query(0)
            normalised(0, 1)
            tau_keys(0)
            tau_max(0)
            feed_forward(1, 0)
            tau_normalise(0)
            tau_probs(0)
            weight_scales()
            tau_context(0)
            feed_forward(1, 1)
            tau_values(0)
            centred(1, 1)
            tau_out(0)
            variance(1, 1)
            window_weights(0)
            normalised(1, 1)
            window(0)
            tau_query(1)
            nc.vector.tensor_copy(identh[:, :], ident).then_inc(S["identh_ready"], 1)
            tau_keys(1)
            squares_sum(0, 0, S["asq_ready"])
            tau_max(1)
            norm1(0)
            tau_normalise(1)
            tau_probs(1)
            key_max(0)
            key_max(1)
            tau_context(1)
            key_transposed(0)
            key_max(2)
            tau_values(1)
            key_transposed(1)
            key_max(3)
            tau_out(1)
            key_transposed(2)
            key_transposed(3)
            window_weights(1)
            window(1)
            context(0)
            mix(0)
            squares_sum(0, 1, S["asq_ready"])
            norm1(1)
            residual(0)
            key_max(4)
            key_max(5)
            norm2_centred(0)
            key_transposed(4)
            key_max(6)
            key_transposed(5)
            key_max(7)
            squares_sum(1, 0, S["xsq_ready"])
            key_transposed(6)
            key_transposed(7)
            norm2(0)
            norm2_rests(0)
            norm2_transposed(0)
            context(1)
            mix(1)
            choose(0)
            residual(1)
            norm2_centred(1)
            squares_sum(1, 1, S["xsq_ready"])
            norm2(1)
            hidden(0)
            norm2_rests(1)
            hidden(1)
            output_tile(0)
            norm2_transposed(1)
            choose(1)
            hidden(2)
            output_tile(1)
            for t in range(HALF, PAIRS):
                mask_row(t)
            for t in range(3, PAIRS):
                hidden(t)
                output_tile(t - 1)
            output_tile(PAIRS - 1)

        @block.tensor
        def _(pe):
            mm, tr = nc.tensor.matmul, nc.tensor.transpose
            pe.wait_ge(S["ld_dft"], 16)
            for c in range(QUADS):
                if c % 2 == 0:
                    pe.wait_ge(S[f"ld_x{c // 2}"], 32)
                for jj in range(2):
                    j = 2 * c + jj
                    for t in range(2):
                        last = mm(bank[c][:, L * jj:L * jj + L], xl[:, t, P * j:P * j + P], dft[:, t, :],
                                  start=t == 0, stop=t == 1)
                last.then_inc(S["fft_done"], 1)
                for jj in range(2):
                    j = 2 * c + jj
                    for t in range(2):
                        last = tr(bank[4 + c][:, L * jj + P * t:L * jj + P * t + P], xl[:, t, P * j:P * j + P], ident)
                last.then_inc(S["xt_done"], 1)
            pe.wait_ge(S["ld_qkv"], 16)

            def projections(h):
                pe.wait_ge(S["sq_done"], 2 * h + 2)
                pe.wait_ge(S["xT_ready"], 2 * h + 2)
                for c in range(2 * h, 2 * h + 2):
                    pe.wait_ge(S["src_ready"], c + 1)
                    for w in "qk":
                        mm(bank[QK_BANK[w][c]][:, 0:2 * TOK], col[f"w{w}"], src[:, 2 * c:2 * c + 2, :],
                           start=True, stop=True).then_inc(S[f"{w}_done"], 1)

            def values(h):
                for c in range(2 * h, 2 * h + 2):
                    pe.wait_ge(S["qT_ready"], c + 1)
                    for jj in range(2):
                        last = mm(bank[QK_BANK["q"][c]][:, P * jj:P * jj + P], src[:, 2 * c + jj, 0:P], col["wv"],
                                  start=True, stop=True)
                    last.then_inc(S["v_done"], 1)

            def left_values(h):
                pe.wait_ge(S["vleft_in_ready"], h + 1)
                pe.wait_ge(S["kT_ready"], 2 * h + 1)
                for q in range(HALF):
                    last = mm(bank[QK_BANK["k"][2 * h]][32 * q:32 * q + 32, 0:D],
                              vleft_in[:, HALF * h + q, :, :].rearrange("p a t -> p (a t)"), col["wv_stack"],
                              start=True, stop=True)
                last.then_inc(S["vl_done"], 1)

            projections(0)
            values(0)
            projections(1)
            left_values(0)
            values(1)
            left_values(1)
            pe.wait_ge(S["v_ready"], 2)
            units = [0]

            def scores(b):
                h, j, s = b // (2 * HALF), b // 2 % HALF, b % 2
                if b % (2 * HALF) == 0:
                    pe.wait_ge(S[f"strips{h}"], 16 * 4 * len(TERM_RUNS))
                for heads in (((0, 0), (1, 0), (2, 0)), ((0, 1), (1, 1), (2, 1)), ((3, 0), (3, 1))):
                    if units[0] >= 2:
                        pe.wait_ge(S["max_ready"], units[0] - 1)
                    for a, (g, u) in enumerate(heads):
                        last = mm(bank[units[0] % 2][:, TOK * a:TOK * a + TOK], QS[h][:, u, s, g, TOK * j:TOK * j + P],
                                  KS[h][:, s, g, TOK * j:TOK * j + TOK], start=True, stop=True)
                    last.then_inc(S["s_done"], 1)
                    units[0] += 1

            def transposed_max(h):
                pe.wait_ge(S["left_ready"], h + 1)
                pe.wait_ge(S["vl_ready"], 2)
                pe.wait_ge(S["max_ready"], units[0])
                sl, mt = bank[SL_BANK[h]], bank[MT_BANK[h]]
                for q in range(HALF):
                    last = mm(sl[32 * q:32 * q + 32, 0:TOK], qleft[:, HALF * h + q, :, :].rearrange("p a t -> p (a t)"),
                              KT[:, HALF * h + q, :], start=True, stop=True)
                last.then_inc(S["sl_done"], 1)
                tr(mt[0:64, 0:P], mneg[:, h, :], ident)
                pe.wait_ge(S["mlneg_ready"], h + 1)
                for t in range(LEFT):
                    last = mm(mt[0:64, P + t:P + t + 1], sel_left[:, t, :], mlneg[:, h:h + 1], start=True, stop=True)
                last.then_inc(S["mt_done"], 1)

            def left_keys(h):
                pe.wait_ge(S["mT_ready"], h + 1)
                kl = bank[KL_BANK[h]]
                for q in range(HALF):
                    mm(kl[32 * q:32 * q + 32, 0:TOK], kleft[:, HALF * h + q, :, :].rearrange("p a t -> p (a t)"),
                       QT[:, HALF * h + q, :], start=True, stop=False)
                    last = mm(kl[32 * q:32 * q + 32, 0:TOK], sel_pair[0:64, q, :], mT[:, h, :], start=False, stop=True)
                last.then_inc(S["kl_done"], 1)

            def shifted_scores(b):
                h, j, s = b // (2 * HALF), b // 2 % HALF, b % 2
                if b % (2 * HALF) == 0:
                    pe.wait_ge(S[f"shift{h}"], 16 * 2)
                    pe.wait_ge(S["v_ready"], QUADS)
                for pr in range(2):
                    unit = 2 * b + pr
                    if unit >= 2:
                        pe.wait_ge(S["exp_done"], unit - 1)
                    for a in range(4):
                        g, u = 2 * pr + a // 2, a % 2
                        last = mm(bank[2 + 2 * (unit % 2) + a // 2][:, TOK * u:TOK * u + TOK],
                                  KS[h][:, s, g, TOK * j:TOK * j + P], QS[h][:, u, s, g, TOK * j:TOK * j + TOK],
                                  start=True, stop=True)
                    last.then_inc(S["st_done"], 1)

            def weighted_values(b):
                j, s, h = b // 2, b % 2, b // (2 * HALF)
                pe.wait_ge(S["exp_done"], 2 * b + 2)
                pe.wait_ge(S["vx_ready"], b + 1)
                pe.wait_ge(S["el_ready"], h + 1)
                if b >= 2:
                    pe.wait_ge(S["ot_ready"], b - 1)
                for hd in range(HEADS):
                    mm(bank[6 + b % 2][:, 0:TOK], Vx[:, b % 4, hd, :], ET[:, (2 * b + hd // 4) % 4, hd % 4, :],
                       start=hd == 0, stop=False)
                q = j % HALF
                mm(bank[6 + b % 2][:, 0:TOK], VL[32 * q:32 * q + 32, h, s, :], EL[32 * q:32 * q + 32, h, :],
                   start=False, stop=True).then_inc(S["pv_done"], 1)

            def attention_out(h):
                if h:
                    pe.wait_ge(S["exp_done"], 2 * B)
                pe.wait_ge(S["ot_ready"], 8 * h + 8)
                for cl in range(2):
                    c = 2 * h + cl
                    mm(bank[ENC_BANKS[h][cl]][:, 0:2 * TOK], col["wo"], OT[:, 2 * c:2 * c + 2, :], start=True, stop=True).then_inc(S["wo_done"], 1)

            def centred(k, h):
                for cl in range(2):
                    c = 2 * h + cl
                    pe.wait_ge(S[f"z_ready{k}"], c + 1)
                    mm(bank[ENC_BANKS[h][cl]][:, 0:2 * TOK], col["center"], z[k][:, 2 * c:2 * c + 2, :],
                       start=True, stop=True).then_inc(S[f"ctr_done{k}"], 1)

            def variance(k, h):
                pe.wait_ge(S[f"zc_ready{k}"], 2 * h + 2)
                for cl in range(2):
                    c = 2 * h + cl
                    mm(bank[ENC_BANKS[h][0]][32 * cl:32 * cl + 32, 0:2 * TOK], col["mean2"], lnsq[:, 2 * c:2 * c + 2, :],
                       start=True, stop=True).then_inc(S[f"var_done{k}"], 1)

            def normalised(k, h):
                pe.wait_ge(S[f"rstd_ready{k}"], h + 1)
                for cl in range(2):
                    r = slice(32 * cl, 32 * cl + 32)
                    mm(bank[ENC_BANKS[h][cl]][:, 0:2 * TOK], col[f"g{k + 1}_rows"][r, :], rstd[r, k, :],
                       start=True, stop=True).then_inc(S[f"spread_done{k}"], 1)

            def feed_step(h, cl, q):
                c, i = 2 * h + cl, 8 * h + 4 * cl + q
                if q == 0:
                    pe.wait_ge(S["enc_ready0"], 2 * h + 2)
                    if h:
                        pe.wait_ge(S["lnn_ready1"], 2)
                    if cl:
                        pe.wait_ge(S["z_ready1"], c)
                if q < 4:
                    apart = 1 + h
                    if i - 8 * h >= apart:
                        pe.wait_ge(S["relu_ready"], i - apart + 1)
                    mm(bank[FF1_BANKS[h][q % 2]][:, 0:2 * TOK], ff1[:, q, :], enc[0][:, 2 * c:2 * c + 2, :],
                       start=True, stop=True).then_inc(S["ff1_done"], 1)
                if q:
                    pe.wait_ge(S["relu_ready"], i)
                    last = mm(bank[FF2_BANKS[h][cl]][:, 0:2 * TOK], ff2[:, q - 1, :], relu[:, c % 2, q - 1, :],
                              start=q == 1, stop=q == 4)
                    if q == 4:
                        last.then_inc(S["ff2_done"], 1)

            def tau_query(h):
                pe.wait_ge(S["enc_ready1"], 2 * h + 2)
                mm(bank[4][:, 0:HALF], col["wq2"], enc[1][:, HALF * h:HALF * h + HALF, P],
                   start=True, stop=True).then_inc(S["tau_q"], 1)
                for jj in range(HALF):
                    tr(bank[5][:, P * jj:P * jj + P], enc[1][:, HALF * h + jj, 0:P], ident)
                    last = tr(bank[6][0:LEFT, P * jj:P * jj + P], enc[1][:, HALF * h + jj, P:TOK], ident)
                last.then_inc(S["s2t_done"], 1)

            def tau_keys(h):
                pe.wait_ge(S["tau_q_ready"], h + 1)
                if h:
                    pe.wait_ge(S["tau_abs"], h)
                mm(bank[7][:, 0:P], col["wk2"], q2m[:, HALF * h:HALF * h + HALF, :].rearrange("p j r -> p (j r)"),
                   start=True, stop=True).then_inc(S["tau_u"], 1)

            def tau_scores(h):
                pe.wait_ge(S["tau_u_ready"], h + 1)
                for q in range(HALF):
                    last = mm(bank[4][32 * q:32 * q + 32, 0:TOK], u2[:, HALF * h + q, :], enc[1][:, HALF * h + q, :],
                              start=True, stop=True)
                last.then_inc(S["tau_s"], 1)

            def tau_probs(h):
                pe.wait_ge(S["tau_p_ready"], h + 1)
                tr(bank[7][:, 0:P], prob[:, h, 0:P], ident)
                tr(bank[4][0:LEFT, 0:P], prob[:, h, P:TOK], ident).then_inc(S["pT_done"], 1)

            def tau_context(h):
                pe.wait_ge(S["pT_ready"], h + 1)
                pe.wait_ge(S["s2t_ready"], h + 1)
                for q in range(HALF):
                    o = bank[5][:, 32 * q:32 * q + 32]
                    mm(o, s2t[:, HALF * h + q, :], PT[:, h, 32 * q:32 * q + 32], start=True, stop=False)
                    last = mm(o, s2l[:, HALF * h + q, :], PTl[:, h, 32 * q:32 * q + 32], start=False, stop=True)
                last.then_inc(S["tau_c"], 1)

            def tau_values(h):
                pe.wait_ge(S["tau_c_ready"], h + 1)
                mm(bank[6][:, 0:P], col["wv2"], c2[:, HALF * h:HALF * h + HALF, :].rearrange("p j r -> p (j r)"),
                   start=True, stop=True).then_inc(S["tau_v"], 1)

            def tau_out(h):
                pe.wait_ge(S["tau_o_ready"], h + 1)
                mm(bank[7][:, 0:HALF], col["wo2"], tv["ob"][:, HALF * h:HALF * h + HALF],
                   start=True, stop=True).then_inc(S["tau_out"], 1)

            def norm1_centred(h):
                if h:
                    pe.wait_ge(S["tau_abs"], 2)
                else:
                    pe.wait_ge(S["lnn_ready1"], QUADS)
                for cl in range(2):
                    c = 2 * h + cl
                    pe.wait_ge(S["h_ready"], 2 * c + 2)
                    for jj in range(2):
                        for t in range(2):
                            a = 256 * jj + P * t
                            last = mm(bank[4 * h + cl][0:CH, a:a + P], hT[:, 2 * c + jj, STEP * t:STEP * t + CH], col["center"],
                                      start=True, stop=True)
                    last.then_inc(S["a1_done"], 1)

            def norm1_transposed(h):
                for cl in range(2):
                    c = 2 * h + cl
                    pe.wait_ge(S["xn_ready"], c + 1)
                    for jj in range(2):
                        for t in range(2):
                            a = LOUT * jj + STEP * t
                            last = tr(bank[4 * h + 2 + cl][:, a:a + CH], xn[:, c, jj, t, :, :].rearrange("p s d -> p (s d)"),
                                      ident[0:CH, 0:CH])
                    last.then_inc(S["a2_done"], 1)

            def key_projection(n):
                h, c = n // 4, n // 2
                pe.wait_ge(S["xnT_ready"], 2 * h + 2)
                if n % 4 >= 2:
                    pe.wait_ge(S["ke_ready"], n - 1)
                mm(bank[4 * h + n % 2][:, 0:2 * LOUT], wk_att[:, n % 2, :], xnT[h][:, 2 * (c % 2):2 * (c % 2) + 2, :], start=True,
                   stop=True).then_inc(S["kp_done"], 1)

            def exp_transposed(n):
                pe.wait_ge(S["ke_ready"], n + 1)
                if n % 4 >= 2:
                    pe.wait_ge(S["ett_ready"], n - 1)
                for jj in range(2):
                    for t in range(2):
                        a = 256 * jj + P * t
                        last = tr(bank[4 * (n // 4) + 2 + n % 2][0:CH, a:a + P], E[n // 4][:, n % 4, jj, STEP * t:STEP * t + CH], ident)
                last.then_inc(S["et_done"], 1)

            def keys(h):
                key_projection(4 * h)
                key_projection(4 * h + 1)
                for n in range(4 * h, 4 * h + 4):
                    exp_transposed(n)
                    if n + 2 < 4 * h + 4:
                        key_projection(n + 2)

            def gram(h):
                pe.wait_ge(S["ett_ready"], 4 * h + 4)
                for j in range(HALF * h, HALF * h + HALF):
                    c, jj = j // 2, j % 2
                    for s in range(2):
                        o = bank[4 * h][64 * s:64 * s + 64, P * (j % 4):P * (j % 4) + P]
                        mm(o, xn[0:STEP, c, jj, 0, s, :], ETt[h][0:STEP, 2 * (c % 2) + s, jj, 0, :], start=True, stop=False)
                        last = mm(o, xn[:, c, jj, 1, s, :], ETt[h][:, 2 * (c % 2) + s, jj, 1, :], start=False, stop=True)
                last.then_inc(S["gt_done"], 1)

            def context(h):
                pe.wait_ge(S["gt_ready"], h + 1)
                for j in range(HALF * h, HALF * h + HALF):
                    last = mm(bank[2 * h + 2 + j // 2][:, 256 * (j % 2):256 * (j % 2) + 256], GT[h][:, j % 4, :], col["wv_att"],
                              start=True, stop=True)
                    if j % 2:
                        last.then_inc(S["ctx_done"], 1)

            def queries_in(h):
                for j in range(HALF * h, HALF * h + HALF):
                    pe.wait_ge(S["ctx_ready"], j // 2 + 1)
                    for s in range(2):
                        a = P * (j % 4) + D * s
                        last = mm(bank[4 * h + 1][:, a:a + D], cx[h][:, j % 4, s, :], col["wqT"], start=True, stop=True)
                last.then_inc(S["zz_done"], 1)

            def mix(h):
                pe.wait_ge(S["zz_ready"], h + 1)
                for j in range(HALF * h, HALF * h + HALF):
                    last = mm(bank[4 * h][:, D * (j % 4):D * (j % 4) + D], Zs[h][:, j % 4, :], col["wout"], start=True, stop=True)
                last.then_inc(S["mx_done"], 1)

            def residual(h):
                pe.wait_ge(S["mix_ready"], h + 1)
                for cl in range(2):
                    for jj in range(2):
                        for t in range(2):
                            j, a = 4 * h + 2 * cl + jj, 256 * jj + P * t
                            mm(bank[4 * h + 2 + cl][0:CH, a:a + P], xnT[h][:, j % 4, STEP * t:STEP * t + CH],
                               Mb[h][:, j % 4, :, :].rearrange("p s o -> p (s o)"), start=True, stop=False)
                            last = mm(bank[4 * h + 2 + cl][0:CH, a:a + P], hT[:, j, STEP * t:STEP * t + CH], ident,
                                      start=False, stop=True)
                    last.then_inc(S["h2_done"], 1)

            def norm2_transposed(h):
                pe.wait_ge(S["h2_ready"], 2 * h + 2)
                pe.wait_ge(S["identh_ready"], 1)
                for t in range(HALF * h, HALF * h + HALF):
                    pe.wait_ge(S["xlo_ready"], t // 2 + 1)
                    for bb in range(2):
                        for ch in range(2):
                            a = LOUT * bb + STEP * ch
                            last = mm(bank[t][:, a:a + CH],
                                      xparts[:, t // 2, t % 2, ch, bb, :, :].rearrange("p k d -> p (k d)"),
                                      identh[0:CH, 0:CH], start=True, stop=True)
                    last.then_inc(S["a11_done"], 1)

            def gates(h):
                pe.wait_ge(S["wsplit_ready"], 1)
                for u in range(16 * h, 16 * h + 16):
                    b, t = u // 2, u % 2
                    pe.wait_ge(S["xa_ready"], b // 2 + 1)
                    last = mm(bank[4 * h][0:CH, 16 * (u % 16):16 * (u % 16) + 16], xa[:, b, STEP * t:STEP * t + CH],
                              gate2[:, :, :].rearrange("p k e -> p (k e)"), start=True, stop=True)
                last.then_inc(S["gate_done"], 1)

            def mask_rows(h):
                pe.wait_ge(S["nm_ready"], h + 1)
                for t in range(HALF * h, HALF * h + HALF):
                    for bb in range(2):
                        for ch in range(2):
                            a = LOUT * bb + STEP * ch
                            last = mm(bank[t][64:96, a:a + CH], nm[:, 4 * t + 2 * bb + ch, :], identh[0:CH, 0:CH],
                                      start=True, stop=True)
                    last.then_inc(S["mk_done"], 1)

            def up_tile(t):
                pe.wait_ge(S["xb_preset"], 1)
                pe.wait_ge(S["xb_ready"], t + 1)
                pe.wait_ge(S["mk_ready"], HALF if t < HALF else PAIRS)
                for e in range(E_N):
                    unit = E_N * t + e
                    if t >= HALF:
                        pe.wait_ge(S["gelu_done"], max(unit - 3, E_N * HALF))
                    elif unit >= 3:
                        pe.wait_ge(S["gelu_done"], unit - 2)
                    ps = bank[up_bank(t, e)][:, 0:2 * LOUT]
                    mm(ps, up_a[:, e, :], xa[:, 2 * t:2 * t + 2, :], start=True, stop=False)
                    mm(ps, up_b[:, e, :], xb[:, 2 * t:2 * t + 2, :], start=False, stop=True).then_inc(S["up_done"], 1)

            def down_tile(t):
                if t:
                    pe.wait_ge(S["o_ready"], t if t <= HALF else t - 1)
                parts = [(bb, ch) for bb in range(2) for ch in range(2)]
                for e in range(E_N):
                    if e % 2 == 0:
                        pe.wait_ge(S["lo_ready"], GROUPS * t + e // 2 + 1)
                    for bb, ch in parts:
                        o = bank[down_bank(t)][0:CH, 2 * D * (2 * bb + ch):2 * D * (2 * bb + ch) + 2 * D]
                        a = LOUT * bb + STEP * ch
                        mm(o, hparts[:, t % 2, 0, e, a:a + CH], down2[:, e, :, :].rearrange("p k d -> p (k d)"),
                           start=e == 0 and (bb, ch) == (0, 0), stop=False)
                        mm(o[:, 0:D], hparts[:, t % 2, 1, e, a:a + CH], down2[:, e, 0, :], start=False, stop=False)
                for bb, ch in parts:
                    n = 2 * D * (2 * bb + ch)
                    last = mm(bank[down_bank(t)][0:CH, n:n + D], xb[:, 2 * t + bb, STEP * ch:STEP * ch + CH], b2r[:, :],
                              start=False, stop=(bb, ch) == (1, 1))
                last.then_inc(S["down_done"], 1)

            for b in range(2 * HALF):
                scores(b)
            transposed_max(0)
            for b in range(2 * HALF, 2 * HALF + AHEAD):
                scores(b)
            left_keys(0)
            for b in range(2 * HALF):
                shifted_scores(b)
                if 2 * HALF + AHEAD + b < B:
                    scores(2 * HALF + AHEAD + b)
                    if 2 * HALF + AHEAD + b == B - 1:
                        transposed_max(1)
                if b:
                    weighted_values(b - 1)
            left_keys(1)
            pe.wait_ge(S["el_ready"], 2)
            pe.wait_ge(S["ld_enc"], 16)
            for b in range(2 * HALF, B):
                shifted_scores(b)
                if b == 13:
                    feed_step(0, 0, 0)
                elif b == 14:
                    feed_step(0, 0, 2)
                elif b == 15:
                    feed_step(0, 0, 4)
                    feed_step(0, 1, 0)
                weighted_values(b - 1)
                if b == 9:
                    attention_out(0)
                elif b == 10:
                    centred(0, 0)
                elif b == 11:
                    variance(0, 0)
                elif b == 12:
                    normalised(0, 0)
                elif b == 13:
                    feed_step(0, 0, 1)
                elif b == 14:
                    feed_step(0, 0, 3)
                elif b == 15:
                    feed_step(0, 1, 1)
            weighted_values(B - 1)
            for q in range(2, 5):
                feed_step(0, 1, q)
            centred(1, 0)
            attention_out(1)
            variance(1, 0)
            centred(0, 1)
            normalised(1, 0)
            variance(0, 1)
            tau_query(0)
            normalised(0, 1)
            tau_keys(0)
            tau_scores(0)
            for q in range(5):
                feed_step(1, 0, q)
            tau_probs(0)
            for q in range(2):
                feed_step(1, 1, q)
            tau_context(0)
            for q in range(2, 5):
                feed_step(1, 1, q)
            tau_values(0)
            centred(1, 1)
            tau_out(0)
            variance(1, 1)
            normalised(1, 1)
            tau_query(1)
            tau_keys(1)
            norm1_centred(0)
            tau_scores(1)
            norm1_transposed(0)
            tau_probs(1)
            key_projection(0)
            key_projection(1)
            tau_context(1)
            exp_transposed(0)
            key_projection(2)
            tau_values(1)
            exp_transposed(1)
            key_projection(3)
            tau_out(1)
            exp_transposed(2)
            exp_transposed(3)
            gram(0)
            context(0)
            queries_in(0)
            mix(0)
            norm1_centred(1)
            residual(0)
            norm1_transposed(1)
            keys(1)
            gram(1)
            norm2_transposed(0)
            gates(0)
            context(1)
            queries_in(1)
            mix(1)
            residual(1)
            mask_rows(0)
            up_tile(0)
            up_tile(1)
            norm2_transposed(1)
            down_tile(0)
            gates(1)
            up_tile(2)
            down_tile(1)
            mask_rows(1)
            up_tile(3)
            down_tile(2)
            for t in range(HALF, PAIRS):
                up_tile(t)
                down_tile(t - 1)
            down_tile(PAIRS - 1)


def host_packs(w):
    f = np.float32

    def pair(m):
        o = np.zeros((P, 2 * m.shape[1]), f)
        o[:D, :m.shape[1]] = m
        o[D:, m.shape[1]:] = m
        return o

    def twice(v):
        return np.concatenate([v, v]).reshape(P, 1)

    def rows(v):
        return np.broadcast_to(v, (P, v.shape[0]))

    c = {}
    l = np.arange(L)[:, None].astype(np.float64)
    k = np.arange(NFREQ)[None, :]
    table = np.concatenate([np.cos(2 * np.pi * (l * k % L) / L), np.sin(2 * np.pi * (l * k % L) / L)], 1)
    table[:, NFREQ] = 1 - 2 * (l[:, 0] % 2)
    c["dft"] = table.astype(f).reshape(2, P, L).transpose(1, 0, 2).reshape(P, 2 * L)
    c["ident"] = np.eye(P, dtype=f)
    pos = np.arange(TOK)[:, None].astype(np.float64)
    div = np.exp(np.arange(0, D, 2) * (-np.log(10000.0) / D))
    pe = np.zeros((TOK, D), f)
    pe[:, 0::2] = np.sin(pos * div)
    pe[:, 1::2] = np.cos(pos * div)
    pe = np.concatenate([pe[1:], pe[:1]]).T
    c["posenc"] = np.concatenate([pe, pe])
    wi, bi = w["L0_tok_l_in_w"], w["L0_tok_l_in_b"]
    p = np.arange(P)
    batch, head = p // 4 % 2, p // 64 + 2 * (p % 4)
    order = D * batch + DH * head + p // 8 % DH
    for n, name in enumerate("qkv"):
        c[f"w{name}"] = pair(wi[D * n:D * n + D].T)
        if name != "v":
            c[f"w{name}"] = c[f"w{name}"][:, order]
    c["wv_stack"] = np.concatenate([wi[2 * D:].T] * 2)
    c["bq"], c["bk"] = twice(bi[:D])[order], twice(bi[D:2 * D])[order]
    c["bv_row"] = rows(np.concatenate([bi[2 * D:]] * 2))
    c["head16"] = ((HEADS * batch + head)[:, None] == np.arange(16)[None]).astype(f)
    c["batch16"] = (p[:, None] // D == np.arange(16)[None] // HEADS).astype(f)
    ps, ph, pt, pj = p // 16 % 2, p // 2 % HEADS, p % 2, p // 32
    vm = np.zeros((P, 2, D), f)
    vc = np.zeros((P, 2, P), f)
    for s in range(2):
        own = (ps[:, None] == s) & (ph[:, None] == np.arange(D)[None] // DH)
        vm[:, s] = own
        vc[:, s, D * (1 - s):D * (1 - s) + D] = own
    c["vl_mask"], c["vl_const"] = vm.reshape(P, -1), vc.reshape(P, -1)
    row = 32 * (ph % 2) + 16 * ps + 4 * (ph // 2) + pj
    m = np.arange(D)
    c["sel_left"] = np.stack([(row[:, None] == m[None]) & (pt[:, None] == t) for t in range(2)], 1).astype(f).reshape(P, -1)
    sp = np.zeros((P, HALF, 32), f)
    sp[row, pj, p % 32] = 1
    c["sel_pair"] = sp.reshape(P, -1)

    c["wo"] = pair(w["L0_tok_l_out_w"].T)
    c["center"] = pair((np.eye(D) - 1.0 / D).astype(f))
    c["mean2"] = np.zeros((P, 32), f)
    c["mean2"][:D, 0] = c["mean2"][D:, 1] = 1.0 / D
    for n, name in (("g1_rows", "ln1_g"), ("g2_rows", "ln2_g")):
        c[n] = np.zeros((P, P), f)
        for r in range(0, P, 32):
            c[n][r, :D] = c[n][r + 1, D:] = w["L0_tok_" + name]
    for n, name in (("bo", "l_out_b"), ("b1", "ln1_b"), ("b2", "ln2_b"), ("ffb2", "ff_b2"),
                    ("bo2", "m_out_b")):
        c[n] = twice(w["L0_tok_" + name])
    c["eps"] = np.full((P, 1), EPS, f)
    f1, f2 = np.zeros((P, 4, P), f), np.zeros((P, 4, P), f)
    for s in range(2):
        for k in range(2):
            f1[D * s:D * s + D, 2 * s + k] = w["L0_tok_ff_w1"][P * k:P * k + P].T
            f2[:, 2 * s + k, D * s:D * s + D] = w["L0_tok_ff_w2"][:, P * k:P * k + P].T
    c["ff1"], c["ff2"] = f1.reshape(P, -1), f2.reshape(P, -1)
    c["ffb1"] = w["L0_tok_ff_b1"].reshape(2, P).T
    wi, bi = w["L0_tok_m_in_w"], w["L0_tok_m_in_b"]
    c["wq2"], c["wk2"], c["wv2"] = pair(wi[:D].T), pair(wi[D:2 * D]), pair(wi[2 * D:].T)
    c["bq2"], c["bv2"] = twice(bi[:D]), twice(bi[2 * D:])
    c["head32"] = (p[:, None] // DH == np.arange(32)[None]).astype(f)
    c["wo2"] = pair(w["L0_tok_m_out_w"].T)

    wqkv, wout = w["L0_attn_W_qkv"], w["L0_attn_W_out"]
    c["wk_att"], c["wv_att"] = pair(wqkv[:, P:2 * P]), pair(wqkv[:, 2 * P:])
    c["ctx_mask"] = (p[:, None] // AD == p[None] // AD).astype(f)
    c["wqT"], c["wout"] = wqkv[:, :P].T, wout
    c["mix_mask"] = ((p[:, None] // D == p[None] // D) * AD ** -0.5).astype(f)
    c["bout_row"] = rows(np.concatenate([w["L0_attn_b_out"]] * 2))
    c["rank"] = rows((E_N - np.arange(P) % E_N).astype(f))
    c["gate"] = np.concatenate([w["L0_ffn_Wg"]] * 2)
    c["bg_row"] = rows(w["L0_ffn_bg"])
    c["eb1"] = w["L0_ffn_b1"].T
    c["eps_sx"] = np.full((P, 1), EPS / (SX * SX), f)
    c["b2rows"], c["b2part"], c["mask_rows"] = np.zeros((P, D), f), np.zeros((P, PARTS), f), np.zeros((P, E_N), f)
    for k in range(PARTS):
        c["b2rows"][M_ROW + E_N * k:M_ROW + E_N * k + E_N] = w["L0_ffn_b2"]
        c["b2part"][M_ROW + E_N * k:M_ROW + E_N * k + E_N, k] = 1
    for e in range(E_N):
        c["mask_rows"][N_ROW + e, e] = -MASK
    c["up"] = np.concatenate([w["L0_ffn_W1"].transpose(1, 0, 2).reshape(D, -1)] * 2)
    c["down"] = w["L0_ffn_W2"].transpose(1, 0, 2).reshape(P, -1)
    return {k: np.ascontiguousarray(np.concatenate([c[n] for n, _ in v], 1), dtype=f) for k, v in PACKS.items()}


def kernel(**inputs):
    import concourse.bacc as bacc
    from concourse.bass_utils import run_bass_kernel_spmd

    w = {k: np.asarray(v) for k, v in inputs.items()}
    arrays = {"x_dram": np.ascontiguousarray(w["x"])}
    arrays.update({f"pack_{k}_dram": v for k, v in host_packs(w).items()})
    nc = bacc.Bacc("TRN2", target_bir_lowering=False, num_devices=1)
    aps = {k: nc.dram_tensor(k, v.shape, F32, kind="ExternalInput").ap() for k, v in arrays.items()}
    out = nc.dram_tensor("out_dram", (B, LOUT, D), F32, kind="ExternalOutput").ap()
    audio_tower(nc, aps["x_dram"], {k: aps[f"pack_{k}_dram"] for k in PACKS}, out)
    r = run_bass_kernel_spmd(nc, [arrays], core_ids=[0])
    return r.results[0]["out_dram"]
```
